# Optimizing a Trainium2 kernel written in Bass

```python
import numpy as np
import jax
import jax.numpy as jnp

def _softmax(x, axis=-1):
    return jax.nn.softmax(x, axis=axis)

def _gelu(x):
    return jax.nn.gelu(x, approximate=True)

def _silu(x):
    return jax.nn.silu(x)

def _sigmoid(x):
    return jax.nn.sigmoid(x)

def _layernorm(x, axis=-1, eps=1e-05):
    m = jnp.mean(x, axis=axis, keepdims=True)
    v = jnp.var(x, axis=axis, keepdims=True)
    return (x - m) / jnp.sqrt(v + eps)

def _scatter_add(tgt, idx, src, axis=0):
    return tgt.at[idx].add(src)

def _segment_sum(src, seg, n):
    return jax.ops.segment_sum(src, seg, n)
kernel_name = 'mk_decoder_preln_d4_seqx_r4_cb8943'

def setup_inputs(seed: int=0):
    np.random.seed(seed)
    _w = jnp.asarray

    def _rec_inputs():
        import jax
        import jax.numpy as jnp
        _rk = jax.random.key(seed)
        x = -0.0002928 + 1 * jax.random.normal(jax.random.fold_in(_rk, 1), (8, 256, 256), jnp.float32)
        _lenS = 256 - jax.random.randint(jax.random.fold_in(_rk, 7), (8,), 0, max(1, 256 // 4) + 1, jnp.int32)
        _lenS2 = 77 - jax.random.randint(jax.random.fold_in(_rk, 8), (8,), 0, max(1, 77 // 4) + 1, jnp.int32)
        _ctx_1024P = jax.random.normal(jax.random.fold_in(_rk, 11), (8, 16, 256), jnp.float32)
        _ctx_1024c = jax.random.dirichlet(jax.random.fold_in(_rk, 511), 0.3 * jnp.ones((16,), jnp.float32), (8, 77))
        _ctx_1024t = jnp.einsum('bsk,bkd->bsd', _ctx_1024c, _ctx_1024P)
        _ctx_1024t = _ctx_1024t * jax.lax.rsqrt(jnp.mean(jnp.square(_ctx_1024t)) + 1e-12) * 0.953939
        ctx_1024 = -1.39393e-06 + 0.999914 * (_ctx_1024t + 0.3 * jax.random.normal(jax.random.fold_in(_rk, 611), (8, 77, 256), jnp.float32))
        return (x, ctx_1024)
    x, ctx_1024 = _rec_inputs()

    def _L0_attn_setup():
        import jax, jax.numpy as jnp
        import numpy as np
        DIM = 256
        HID = 1024
        NUM_HEADS = 4
        WINDOW = 128
        NUM_PM = 64
        NEG = -1e+30

        def _swa(x_in, wq, wk, wv, wo):
            B, S, D = x_in.shape
            h, dh = (NUM_HEADS, D // NUM_HEADS)
            q = (x_in @ wq.T).reshape(B, S, h, dh).transpose(0, 2, 1, 3)
            k = (x_in @ wk.T).reshape(B, S, h, dh).transpose(0, 2, 1, 3)
            v = (x_in @ wv.T).reshape(B, S, h, dh).transpose(0, 2, 1, 3)
            i = jnp.arange(S)[:, None]
            j = jnp.arange(S)[None, :]
            mask = (j <= i) & (j > i - WINDOW)
            logits = jnp.einsum('bhqd,bhkd->bhqk', q, k) / np.sqrt(dh).astype(np.float32)
            logits = jnp.where(mask, logits, NEG)
            attn = jax.nn.softmax(logits, axis=-1)
            out = jnp.einsum('bhqk,bhkd->bhqd', attn, v)
            out = out.transpose(0, 2, 1, 3).reshape(B, S, D)
            return out @ wo.T

        def _mlp(w1, b1, w2, b2, x):
            return jax.nn.silu(x @ w1.T + b1) @ w2.T + b2
        key = jax.random.key(seed)
        ks = jax.random.split(key, 12)
        B, S = (2, 512)
        sc = 0.02
        n = lambda k, shape, s=sc: jax.random.normal(k, shape, jnp.float32) * s
        return {'x': n(ks[0], (B, S, DIM), 1.0), 'mem': n(ks[1], (NUM_PM, DIM), 1.0), 'wq': n(ks[2], (DIM, DIM)), 'wk': n(ks[3], (DIM, DIM)), 'wv': n(ks[4], (DIM, DIM)), 'wo': n(ks[5], (DIM, DIM)), 'w1': n(ks[6], (HID, DIM)), 'b1': jnp.zeros((HID,), jnp.float32), 'w2': n(ks[7], (DIM, HID)), 'b2': jnp.zeros((DIM,), jnp.float32), 'lin1': n(ks[8], (DIM, DIM)), 'lin2': n(ks[9], (DIM, DIM)), 'alpha': jnp.float32(0.0001), 'theta': jnp.float32(0.0001)}
    _L0_attn_all = _L0_attn_setup()
    _L0_attn_in = {k: v for k, v in _L0_attn_all.items() if k in ('mem', 'wq', 'wk', 'wv', 'wo', 'w1', 'b1', 'w2', 'b2', 'lin1', 'lin2', 'alpha', 'theta')}
    del _L0_attn_all

    def _L0_xattn_setup():
        import jax, jax.numpy as jnp
        import numpy as np
        import math
        D_MODEL = 256
        N_HEADS = 16
        HEAD_DIM = D_MODEL // N_HEADS
        TOP_K = 32
        SCALE = math.sqrt(HEAD_DIM)

        def _split_heads(t, n):
            B, L, _ = t.shape
            return t.reshape(B, L, N_HEADS, HEAD_DIM).transpose(0, 2, 1, 3)
        key = jax.random.key(seed)
        ks = jax.random.split(key, 12)
        B, S, N = (2, 512, 512)
        std = 1.0 / math.sqrt(D_MODEL)
        inp = {'x': jax.random.normal(ks[0], (B, S, D_MODEL), dtype=jnp.float32), 'knowledge_embeddings': jax.random.normal(ks[1], (B, N, D_MODEL), dtype=jnp.float32), 'Wq': jax.random.normal(ks[2], (D_MODEL, D_MODEL), dtype=jnp.float32) * std, 'bq': jnp.zeros((D_MODEL,), dtype=jnp.float32), 'Wk': jax.random.normal(ks[3], (D_MODEL, D_MODEL), dtype=jnp.float32) * std, 'bk': jnp.zeros((D_MODEL,), dtype=jnp.float32), 'Wv': jax.random.normal(ks[4], (D_MODEL, D_MODEL), dtype=jnp.float32) * std, 'bv': jnp.zeros((D_MODEL,), dtype=jnp.float32), 'Wo': jax.random.normal(ks[5], (D_MODEL, D_MODEL), dtype=jnp.float32) * std, 'bo': jnp.zeros((D_MODEL,), dtype=jnp.float32)}
        return inp
    _L0_xattn_all = _L0_xattn_setup()
    _L0_xattn_in = {k: v for k, v in _L0_xattn_all.items() if k in ('Wq', 'bq', 'Wk', 'bk', 'Wv', 'bv', 'Wo', 'bo')}
    del _L0_xattn_all

    def _L0_ffn_setup():
        import jax, jax.numpy as jnp
        import numpy as np
        BEST_K = 2

        def _expert(xf, w1, w3, w2):
            return jax.nn.silu(xf @ w1) * (xf @ w3) @ w2
        key = jax.random.key(seed)
        ks = jax.random.split(key, 9)
        E, S_sh, D, H = (8, 2, 256, 128)
        B, S = (2, 512)
        w = lambda k, shape: jax.random.normal(k, shape, dtype=jnp.float32) * 0.02
        return {'x': jax.random.normal(ks[0], (B, S, D), dtype=jnp.float32), 'router_w': w(ks[1], (D, E)), 'router_b': jnp.zeros((E,), dtype=jnp.float32), 'routed_w1': w(ks[2], (E, D, H)), 'routed_w3': w(ks[3], (E, D, H)), 'routed_w2': w(ks[4], (E, H, D)), 'shared_w1': w(ks[5], (S_sh, D, H)), 'shared_w3': w(ks[6], (S_sh, D, H)), 'shared_w2': w(ks[7], (S_sh, H, D))}
    _L0_ffn_all = _L0_ffn_setup()
    _L0_ffn_in = {k: v for k, v in _L0_ffn_all.items() if k in ('router_w', 'router_b', 'routed_w1', 'routed_w3', 'routed_w2', 'shared_w1', 'shared_w3', 'shared_w2')}
    del _L0_ffn_all

    def _L1_attn_setup():
        import jax, jax.numpy as jnp
        import numpy as np
        D_MODEL = 256
        N_HEADS = 16
        HEAD_DIM = D_MODEL // N_HEADS
        WINDOW = 128
        FF_HID = 512
        LN_EPS = 1e-05

        def _layernorm(x, g, b):
            mu = jnp.mean(x, axis=-1, keepdims=True)
            var = jnp.mean(jnp.square(x - mu), axis=-1, keepdims=True)
            return (x - mu) * jax.lax.rsqrt(var + LN_EPS) * g + b

        def _local_attn(q, k, v, window):
            BH, S, d = q.shape
            nw = S // window
            scale = d ** (-0.5)
            qw = (q * scale).reshape(BH, nw, window, d)
            kw = k.reshape(BH, nw, window, d)
            vw = v.reshape(BH, nw, window, d)
            kprev = jnp.pad(kw, ((0, 0), (1, 0), (0, 0), (0, 0)))[:, :-1]
            vprev = jnp.pad(vw, ((0, 0), (1, 0), (0, 0), (0, 0)))[:, :-1]
            bk = jnp.concatenate([kprev, kw], axis=2)
            bv = jnp.concatenate([vprev, vw], axis=2)
            tq = jnp.arange(S).reshape(nw, window)
            tprev = jnp.pad(tq, ((1, 0), (0, 0)), constant_values=-1)[:-1]
            tk = jnp.concatenate([tprev, tq], axis=1)
            mask = (tq[:, :, None] >= tk[:, None, :]) & (tk[:, None, :] >= 0)
            sim = jnp.einsum('bnwd,bnkd->bnwk', qw, bk)
            sim = jnp.where(mask[None], sim, -1000000000.0)
            attn = jax.nn.softmax(sim, axis=-1)
            out = jnp.einsum('bnwk,bnkd->bnwd', attn, bv)
            return out.reshape(BH, S, d)
        key = jax.random.key(seed)
        ks = jax.random.split(key, 16)
        B, S = (4, 1024)

        def xavier(k, shape):
            fan_in, fan_out = (shape[-2], shape[-1])
            lim = (6.0 / (fan_in + fan_out)) ** 0.5
            return jax.random.uniform(k, shape, jnp.float32, -lim, lim)
        return {'x': jax.random.normal(ks[0], (B, S, D_MODEL), jnp.float32), 'q_proj': xavier(ks[1], (N_HEADS, D_MODEL, HEAD_DIM)), 'k_proj': xavier(ks[2], (N_HEADS, D_MODEL, HEAD_DIM)), 'v_proj': xavier(ks[3], (N_HEADS, D_MODEL, HEAD_DIM)), 'q_bias': jax.random.uniform(ks[4], (N_HEADS, 1, HEAD_DIM), jnp.float32, -0.1, 0.1), 'k_bias': jax.random.uniform(ks[5], (N_HEADS, 1, HEAD_DIM), jnp.float32, -0.1, 0.1), 'v_bias': jax.random.uniform(ks[6], (N_HEADS, 1, HEAD_DIM), jnp.float32, -0.1, 0.1), 'ln1_g': jnp.ones((D_MODEL,), jnp.float32), 'ln1_b': jnp.zeros((D_MODEL,), jnp.float32), 'ln2_g': jnp.ones((D_MODEL,), jnp.float32), 'ln2_b': jnp.zeros((D_MODEL,), jnp.float32), 'ff1_w': xavier(ks[7], (D_MODEL, FF_HID)), 'ff1_b': jnp.zeros((FF_HID,), jnp.float32), 'ff2_w': xavier(ks[8], (FF_HID, D_MODEL)), 'ff2_b': jnp.zeros((D_MODEL,), jnp.float32)}
    _L1_attn_all = _L1_attn_setup()
    _L1_attn_in = {k: v for k, v in _L1_attn_all.items() if k in ('q_proj', 'k_proj', 'v_proj', 'q_bias', 'k_bias', 'v_bias', 'ln1_g', 'ln1_b', 'ln2_g', 'ln2_b', 'ff1_w', 'ff1_b', 'ff2_w', 'ff2_b')}
    del _L1_attn_all

    def _L1_xattn_setup():
        import jax, jax.numpy as jnp
        import numpy as np
        B, SD, SE, D, H = (4, 512, 512, 256, 16)
        HD = D // H

        def _mha(xq, xk, xv, Wq, bq, Wk, bk, Wv, bv, Wo, bo, causal):
            q = jnp.einsum('bsd,hde->bhse', xq, Wq) + bq[None, :, None, :]
            k = jnp.einsum('bsd,hde->bhse', xk, Wk) + bk[None, :, None, :]
            v = jnp.einsum('bsd,hde->bhse', xv, Wv) + bv[None, :, None, :]
            scale = 1.0 / jnp.sqrt(jnp.asarray(HD, q.dtype))
            scores = jnp.einsum('bhqe,bhke->bhqk', q, k) * scale
            if causal:
                mask = jnp.tril(jnp.ones((q.shape[2], k.shape[2]), bool))
                scores = jnp.where(mask, scores, jnp.finfo(scores.dtype).min)
            w = jax.nn.softmax(scores, axis=-1)
            out = jnp.einsum('bhqk,bhke->bhqe', w, v)
            out = out.transpose(0, 2, 1, 3).reshape(out.shape[0], out.shape[2], D)
            return out @ Wo + bo
        key = jax.random.key(seed)
        ks = jax.random.split(key, 19)
        sd = 1.0 / np.sqrt(D)
        n = lambda k, shape, s: jax.random.normal(k, shape, jnp.float32) * s
        inp = {'x': n(ks[0], (B, SD, D), 1.0), 'encoder_k': n(ks[1], (B, SE, D), 1.0), 'encoder_v': n(ks[2], (B, SE, D), 1.0), 'Wq1': n(ks[3], (H, D, HD), sd), 'bq1': jnp.zeros((H, HD), jnp.float32), 'Wk1': n(ks[4], (H, D, HD), sd), 'bk1': jnp.zeros((H, HD), jnp.float32), 'Wv1': n(ks[5], (H, D, HD), sd), 'bv1': jnp.zeros((H, HD), jnp.float32), 'Wo1': n(ks[6], (D, D), sd), 'bo1': jnp.zeros((D,), jnp.float32), 'Wq2': n(ks[7], (H, D, HD), sd), 'bq2': jnp.zeros((H, HD), jnp.float32), 'Wk2': n(ks[8], (H, D, HD), sd), 'bk2': jnp.zeros((H, HD), jnp.float32), 'Wv2': n(ks[9], (H, D, HD), sd), 'bv2': jnp.zeros((H, HD), jnp.float32), 'Wo2': n(ks[10], (D, D), sd), 'bo2': jnp.zeros((D,), jnp.float32)}
        return inp
    _L1_xattn_all = _L1_xattn_setup()
    _L1_xattn_in = {k: v for k, v in _L1_xattn_all.items() if k in ('Wq1', 'bq1', 'Wk1', 'bk1', 'Wv1', 'bv1', 'Wo1', 'bo1', 'Wq2', 'bq2', 'Wk2', 'bk2', 'Wv2', 'bv2', 'Wo2', 'bo2')}
    del _L1_xattn_all

    def _L1_ffn_setup():
        import jax, jax.numpy as jnp
        import numpy as np
        FEATURES = 256
        D_IN = 256

        def fp8_gemm_optimized(x, input_scale, kernel, kernel_scale):
            s_in = input_scale[0]
            s_k = kernel_scale[0]
            x_q = (x.astype(jnp.float32) / s_in).astype(jnp.float8_e4m3fn)
            k_q = (kernel.astype(jnp.float32) / s_k).astype(jnp.float8_e4m3fn)
            y = jnp.dot(x_q.astype(jnp.float32), k_q.astype(jnp.float32), preferred_element_type=jnp.float32)
            return y * (s_in * s_k)
        key = jax.random.key(seed)
        kx, kk, kb = jax.random.split(key, 3)
        x = jax.random.normal(kx, (4, 2048, D_IN), dtype=jnp.float32)
        limit = np.sqrt(6.0 / (D_IN + FEATURES)).astype(np.float32)
        kernel = jax.random.uniform(kk, (D_IN, FEATURES), dtype=jnp.float32, minval=-limit, maxval=limit).astype(jnp.bfloat16)
        input_scale = jnp.ones((1,), dtype=jnp.float32)
        kernel_scale = jnp.ones((1,), dtype=jnp.float32)
        bias = jnp.zeros((FEATURES,), dtype=jnp.bfloat16)
        return {'x': x, 'kernel': kernel, 'input_scale': input_scale, 'kernel_scale': kernel_scale, 'bias': bias}
    _L1_ffn_all = _L1_ffn_setup()
    _L1_ffn_in = {k: v for k, v in _L1_ffn_all.items() if k in ('kernel', 'input_scale', 'kernel_scale', 'bias')}
    del _L1_ffn_all

    def _L2_attn_setup():
        import jax, jax.numpy as jnp
        import numpy as np
        DIM = 256
        DIM_HEADS = 64
        key = jax.random.key(seed)
        k1, k2, k3 = jax.random.split(key, 3)
        x = jax.random.normal(k1, (1, 512, DIM), dtype=jnp.float32)
        w_qkv = jax.random.normal(k2, (DIM_HEADS * 3, DIM), dtype=jnp.float32) * 0.02
        w_out = jax.random.normal(k3, (DIM, DIM_HEADS), dtype=jnp.float32) * 0.02
        return {'x': x, 'w_qkv': w_qkv, 'w_out': w_out}
    _L2_attn_all = _L2_attn_setup()
    _L2_attn_in = {k: v for k, v in _L2_attn_all.items() if k in ('w_qkv', 'w_out')}
    del _L2_attn_all

    def _L2_xattn_setup():
        import jax, jax.numpy as jnp
        import numpy as np
        D_MODEL = 256
        N_HEADS = 16
        HEAD_DIM = D_MODEL // N_HEADS
        B, S = (2, 512)

        def _split_heads(x):
            b, s, _ = x.shape
            return x.reshape(b, s, N_HEADS, HEAD_DIM).transpose(0, 2, 1, 3)
        key = jax.random.key(seed)
        ks = jax.random.split(key, 11)
        scale = 1.0 / np.sqrt(D_MODEL)
        return {'query': jax.random.normal(ks[0], (B, S, D_MODEL), jnp.float32), 'key': jax.random.normal(ks[1], (B, S, D_MODEL), jnp.float32), 'value': jax.random.normal(ks[2], (B, S, D_MODEL), jnp.float32), 'Wq': jax.random.normal(ks[3], (D_MODEL, D_MODEL), jnp.float32) * scale, 'bq': jnp.zeros((D_MODEL,), jnp.float32), 'Wk': jax.random.normal(ks[4], (D_MODEL, D_MODEL), jnp.float32) * scale, 'bk': jnp.zeros((D_MODEL,), jnp.float32), 'Wv': jax.random.normal(ks[5], (D_MODEL, D_MODEL), jnp.float32) * scale, 'bv': jnp.zeros((D_MODEL,), jnp.float32), 'Wo': jax.random.normal(ks[6], (D_MODEL, D_MODEL), jnp.float32) * scale, 'bo': jnp.zeros((D_MODEL,), jnp.float32)}
    _L2_xattn_all = _L2_xattn_setup()
    _L2_xattn_in = {k: v for k, v in _L2_xattn_all.items() if k in ('Wq', 'bq', 'Wk', 'bk', 'Wv', 'bv', 'Wo', 'bo')}
    del _L2_xattn_all

    def _L2_ffn_setup():
        import jax, jax.numpy as jnp
        import numpy as np
        EPS = 1e-12

        def rms_norm(t, gamma):
            n = jnp.maximum(jnp.linalg.norm(t, axis=-1, keepdims=True), EPS)
            scale = jnp.sqrt(jnp.asarray(t.shape[-1], t.dtype))
            return t / n * scale * gamma
        key = jax.random.key(seed)
        ks = jax.random.split(key, 4)
        b, s, d = (4, 1024, 256)
        e, t = (8, 128)
        hidden = 4 * d
        return {'x': jax.random.normal(ks[0], (b, s, d), dtype=jnp.float32), 'gamma_x': jnp.ones((d,), dtype=jnp.float32), 'gamma_slot': jnp.ones((d,), dtype=jnp.float32), 'slot_embeds': jax.random.normal(ks[1], (e, t, d), dtype=jnp.float32), 'w1': jax.random.normal(ks[2], (d, hidden), dtype=jnp.float32) * (1.0 / np.sqrt(d)), 'w2': jax.random.normal(ks[3], (hidden, d), dtype=jnp.float32) * (1.0 / np.sqrt(hidden))}
    _L2_ffn_all = _L2_ffn_setup()
    _L2_ffn_in = {k: v for k, v in _L2_ffn_all.items() if k in ('gamma_x', 'gamma_slot', 'slot_embeds', 'w1', 'w2')}
    del _L2_ffn_all

    def _L3_attn_setup():
        import jax, jax.numpy as jnp
        import numpy as np
        B, L, D = (4, 1024, 256)
        LN_EPS = 1e-05
        SCAN_EPS = 1e-08
        key = jax.random.key(seed)
        ks = jax.random.split(key, 5)
        s = 1.0 / np.sqrt(D)
        return {'X': jax.random.normal(ks[0], (B, L, D), dtype=jnp.float32), 'Wa': jax.random.normal(ks[1], (D, D), dtype=jnp.float32) * s, 'ba': jnp.zeros((D,), dtype=jnp.float32), 'Wb': jax.random.normal(ks[2], (D, D), dtype=jnp.float32) * s, 'bb': jnp.zeros((D,), dtype=jnp.float32), 'Wc': jax.random.normal(ks[3], (D, D), dtype=jnp.float32) * s, 'bc': jnp.zeros((D,), dtype=jnp.float32), 'gamma': jnp.ones((D,), dtype=jnp.float32), 'beta': jnp.zeros((D,), dtype=jnp.float32), 'h0': jax.random.normal(ks[4], (1, D), dtype=jnp.float32)}
    _L3_attn_all = _L3_attn_setup()
    _L3_attn_in = {k: v for k, v in _L3_attn_all.items() if k in ('Wa', 'ba', 'Wb', 'bb', 'Wc', 'bc', 'gamma', 'beta', 'h0')}
    del _L3_attn_all

    def _L3_xattn_setup():
        import jax, jax.numpy as jnp
        import numpy as np
        EMBED = 256
        HEADS = 16
        HEAD_DIM = EMBED // HEADS
        EXP_DIM = 2 * HEAD_DIM

        def _feature_map(x, fm_w, fm_b):
            z = jnp.einsum('nshd,ed->nshe', x, fm_w) + fm_b
            return jnp.concatenate([jnp.exp(z), jnp.exp(-z)], axis=-1)
        key = jax.random.key(seed)
        ks = jax.random.split(key, 7)
        N, S = (4, 512)
        values = jax.random.normal(ks[0], (N, S, EMBED), dtype=jnp.float32)
        keys_ = jax.random.normal(ks[1], (N, S, EMBED), dtype=jnp.float32)
        query = jax.random.normal(ks[2], (N, S, EMBED), dtype=jnp.float32)
        fm_w = jnp.eye(HEAD_DIM, dtype=jnp.float32) + 0.02 * jax.random.normal(ks[3], (HEAD_DIM, HEAD_DIM), dtype=jnp.float32)
        fm_b = 0.02 * jax.random.normal(ks[4], (HEAD_DIM,), dtype=jnp.float32)
        fc_w = jax.random.normal(ks[5], (EMBED, HEADS * EXP_DIM), dtype=jnp.float32) * (1.0 / np.sqrt(HEADS * EXP_DIM))
        fc_b = jnp.zeros((EMBED,), dtype=jnp.float32)
        return {'values': values, 'keys': keys_, 'query': query, 'fm_w': fm_w, 'fm_b': fm_b, 'fc_w': fc_w, 'fc_b': fc_b}
    _L3_xattn_all = _L3_xattn_setup()
    _L3_xattn_in = {k: v for k, v in _L3_xattn_all.items() if k in ('fm_w', 'fm_b', 'fc_w', 'fc_b')}
    del _L3_xattn_all

    def _L3_ffn_setup():
        import jax, jax.numpy as jnp
        import numpy as np
        B, S, DIM = (4, 1024, 256)
        BASE_COUPLING = 0.1
        NUM_CYCLES = 3

        def _gelu(x):
            return jax.nn.gelu(x, approximate=False)

        def _coupling_net(h, w1, b1, w2, b2, w3, b3, w4, b4):
            h = _gelu(h @ w1 + b1)
            h = _gelu(h @ w2 + b2)
            h = _gelu(h @ w3 + b3)
            return jax.nn.sigmoid(h @ w4 + b4)

        def _global_net(h, w1, b1, w2, b2, w3, b3):
            h = _gelu(h @ w1 + b1)
            h = _gelu(h @ w2 + b2)
            return jax.nn.sigmoid(h @ w3 + b3)

        def _twist(x):
            o_r, o_i, p_r, p_i = jnp.split(x, 4, axis=-1)
            return jnp.concatenate([p_r, -p_i, -o_r, o_i], axis=-1)
        key = jax.random.key(seed)
        ks = jax.random.split(key, 9)
        d = DIM

        def w(k, fan_in, fan_out):
            return jax.random.normal(k, (fan_in, fan_out), dtype=jnp.float32) / np.sqrt(fan_in).astype(np.float32)
        inp = {'x': jax.random.normal(ks[0], (B, S, d), dtype=jnp.float32)}
        cn_dims = [(d, d), (d, d // 2), (d // 2, d // 4), (d // 4, 1)]
        for i, (a, b) in enumerate(cn_dims):
            inp[f'cn_w{i + 1}'] = w(ks[1 + i], a, b)
            inp[f'cn_b{i + 1}'] = jnp.zeros((b,), dtype=jnp.float32)
        gc_dims = [(d, d // 2), (d // 2, d // 4), (d // 4, 1)]
        for i, (a, b) in enumerate(gc_dims):
            inp[f'gc_w{i + 1}'] = w(ks[5 + i], a, b)
            inp[f'gc_b{i + 1}'] = jnp.zeros((b,), dtype=jnp.float32)
        inp['adaptive_range'] = jnp.full((1,), 0.2, dtype=jnp.float32)
        return inp
    _L3_ffn_all = _L3_ffn_setup()
    _L3_ffn_in = {k: v for k, v in _L3_ffn_all.items() if k in ('cn_w1', 'cn_b1', 'cn_w2', 'cn_b2', 'cn_w3', 'cn_b3', 'cn_w4', 'cn_b4', 'gc_w1', 'gc_b1', 'gc_w2', 'gc_b2', 'gc_w3', 'gc_b3', 'adaptive_range')}
    del _L3_ffn_all
    return {'x': x, 'ctx_1024': ctx_1024, 'L0_attn_mem': _L0_attn_in['mem'], 'L0_attn_wq': _L0_attn_in['wq'], 'L0_attn_wk': _L0_attn_in['wk'], 'L0_attn_wv': _L0_attn_in['wv'], 'L0_attn_wo': _L0_attn_in['wo'], 'L0_attn_w1': _L0_attn_in['w1'], 'L0_attn_b1': _L0_attn_in['b1'], 'L0_attn_w2': _L0_attn_in['w2'], 'L0_attn_b2': _L0_attn_in['b2'], 'L0_attn_lin1': _L0_attn_in['lin1'], 'L0_attn_lin2': _L0_attn_in['lin2'], 'L0_attn_alpha': _L0_attn_in['alpha'], 'L0_attn_theta': _L0_attn_in['theta'], 'L0_xattn_Wq': _L0_xattn_in['Wq'], 'L0_xattn_bq': _L0_xattn_in['bq'], 'L0_xattn_Wk': _L0_xattn_in['Wk'], 'L0_xattn_bk': _L0_xattn_in['bk'], 'L0_xattn_Wv': _L0_xattn_in['Wv'], 'L0_xattn_bv': _L0_xattn_in['bv'], 'L0_xattn_Wo': _L0_xattn_in['Wo'], 'L0_xattn_bo': _L0_xattn_in['bo'], 'L0_ffn_router_w': _L0_ffn_in['router_w'], 'L0_ffn_router_b': _L0_ffn_in['router_b'], 'L0_ffn_routed_w1': _L0_ffn_in['routed_w1'], 'L0_ffn_routed_w3': _L0_ffn_in['routed_w3'], 'L0_ffn_routed_w2': _L0_ffn_in['routed_w2'], 'L0_ffn_shared_w1': _L0_ffn_in['shared_w1'], 'L0_ffn_shared_w3': _L0_ffn_in['shared_w3'], 'L0_ffn_shared_w2': _L0_ffn_in['shared_w2'], 'L1_attn_q_proj': _L1_attn_in['q_proj'], 'L1_attn_k_proj': _L1_attn_in['k_proj'], 'L1_attn_v_proj': _L1_attn_in['v_proj'], 'L1_attn_q_bias': _L1_attn_in['q_bias'], 'L1_attn_k_bias': _L1_attn_in['k_bias'], 'L1_attn_v_bias': _L1_attn_in['v_bias'], 'L1_attn_ln1_g': _L1_attn_in['ln1_g'], 'L1_attn_ln1_b': _L1_attn_in['ln1_b'], 'L1_attn_ln2_g': _L1_attn_in['ln2_g'], 'L1_attn_ln2_b': _L1_attn_in['ln2_b'], 'L1_attn_ff1_w': _L1_attn_in['ff1_w'], 'L1_attn_ff1_b': _L1_attn_in['ff1_b'], 'L1_attn_ff2_w': _L1_attn_in['ff2_w'], 'L1_attn_ff2_b': _L1_attn_in['ff2_b'], 'L1_xattn_Wq1': _L1_xattn_in['Wq1'], 'L1_xattn_bq1': _L1_xattn_in['bq1'], 'L1_xattn_Wk1': _L1_xattn_in['Wk1'], 'L1_xattn_bk1': _L1_xattn_in['bk1'], 'L1_xattn_Wv1': _L1_xattn_in['Wv1'], 'L1_xattn_bv1': _L1_xattn_in['bv1'], 'L1_xattn_Wo1': _L1_xattn_in['Wo1'], 'L1_xattn_bo1': _L1_xattn_in['bo1'], 'L1_xattn_Wq2': _L1_xattn_in['Wq2'], 'L1_xattn_bq2': _L1_xattn_in['bq2'], 'L1_xattn_Wk2': _L1_xattn_in['Wk2'], 'L1_xattn_bk2': _L1_xattn_in['bk2'], 'L1_xattn_Wv2': _L1_xattn_in['Wv2'], 'L1_xattn_bv2': _L1_xattn_in['bv2'], 'L1_xattn_Wo2': _L1_xattn_in['Wo2'], 'L1_xattn_bo2': _L1_xattn_in['bo2'], 'L1_ffn_kernel': _L1_ffn_in['kernel'], 'L1_ffn_input_scale': _L1_ffn_in['input_scale'], 'L1_ffn_kernel_scale': _L1_ffn_in['kernel_scale'], 'L1_ffn_bias': _L1_ffn_in['bias'], 'L2_attn_w_qkv': _L2_attn_in['w_qkv'], 'L2_attn_w_out': _L2_attn_in['w_out'], 'L2_xattn_Wq': _L2_xattn_in['Wq'], 'L2_xattn_bq': _L2_xattn_in['bq'], 'L2_xattn_Wk': _L2_xattn_in['Wk'], 'L2_xattn_bk': _L2_xattn_in['bk'], 'L2_xattn_Wv': _L2_xattn_in['Wv'], 'L2_xattn_bv': _L2_xattn_in['bv'], 'L2_xattn_Wo': _L2_xattn_in['Wo'], 'L2_xattn_bo': _L2_xattn_in['bo'], 'L2_ffn_gamma_x': _L2_ffn_in['gamma_x'], 'L2_ffn_gamma_slot': _L2_ffn_in['gamma_slot'], 'L2_ffn_slot_embeds': _L2_ffn_in['slot_embeds'], 'L2_ffn_w1': _L2_ffn_in['w1'], 'L2_ffn_w2': _L2_ffn_in['w2'], 'L3_attn_Wa': _L3_attn_in['Wa'], 'L3_attn_ba': _L3_attn_in['ba'], 'L3_attn_Wb': _L3_attn_in['Wb'], 'L3_attn_bb': _L3_attn_in['bb'], 'L3_attn_Wc': _L3_attn_in['Wc'], 'L3_attn_bc': _L3_attn_in['bc'], 'L3_attn_gamma': _L3_attn_in['gamma'], 'L3_attn_beta': _L3_attn_in['beta'], 'L3_attn_h0': _L3_attn_in['h0'], 'L3_xattn_fm_w': _L3_xattn_in['fm_w'], 'L3_xattn_fm_b': _L3_xattn_in['fm_b'], 'L3_xattn_fc_w': _L3_xattn_in['fc_w'], 'L3_xattn_fc_b': _L3_xattn_in['fc_b'], 'L3_ffn_cn_w1': _L3_ffn_in['cn_w1'], 'L3_ffn_cn_b1': _L3_ffn_in['cn_b1'], 'L3_ffn_cn_w2': _L3_ffn_in['cn_w2'], 'L3_ffn_cn_b2': _L3_ffn_in['cn_b2'], 'L3_ffn_cn_w3': _L3_ffn_in['cn_w3'], 'L3_ffn_cn_b3': _L3_ffn_in['cn_b3'], 'L3_ffn_cn_w4': _L3_ffn_in['cn_w4'], 'L3_ffn_cn_b4': _L3_ffn_in['cn_b4'], 'L3_ffn_gc_w1': _L3_ffn_in['gc_w1'], 'L3_ffn_gc_b1': _L3_ffn_in['gc_b1'], 'L3_ffn_gc_w2': _L3_ffn_in['gc_w2'], 'L3_ffn_gc_b2': _L3_ffn_in['gc_b2'], 'L3_ffn_gc_w3': _L3_ffn_in['gc_w3'], 'L3_ffn_gc_b3': _L3_ffn_in['gc_b3'], 'L3_ffn_adaptive_range': _L3_ffn_in['adaptive_range']}

def reference(x, ctx_1024, L0_attn_mem, L0_attn_wq, L0_attn_wk, L0_attn_wv, L0_attn_wo, L0_attn_w1, L0_attn_b1, L0_attn_w2, L0_attn_b2, L0_attn_lin1, L0_attn_lin2, L0_attn_alpha, L0_attn_theta, L0_xattn_Wq, L0_xattn_bq, L0_xattn_Wk, L0_xattn_bk, L0_xattn_Wv, L0_xattn_bv, L0_xattn_Wo, L0_xattn_bo, L0_ffn_router_w, L0_ffn_router_b, L0_ffn_routed_w1, L0_ffn_routed_w3, L0_ffn_routed_w2, L0_ffn_shared_w1, L0_ffn_shared_w3, L0_ffn_shared_w2, L1_attn_q_proj, L1_attn_k_proj, L1_attn_v_proj, L1_attn_q_bias, L1_attn_k_bias, L1_attn_v_bias, L1_attn_ln1_g, L1_attn_ln1_b, L1_attn_ln2_g, L1_attn_ln2_b, L1_attn_ff1_w, L1_attn_ff1_b, L1_attn_ff2_w, L1_attn_ff2_b, L1_xattn_Wq1, L1_xattn_bq1, L1_xattn_Wk1, L1_xattn_bk1, L1_xattn_Wv1, L1_xattn_bv1, L1_xattn_Wo1, L1_xattn_bo1, L1_xattn_Wq2, L1_xattn_bq2, L1_xattn_Wk2, L1_xattn_bk2, L1_xattn_Wv2, L1_xattn_bv2, L1_xattn_Wo2, L1_xattn_bo2, L1_ffn_kernel, L1_ffn_input_scale, L1_ffn_kernel_scale, L1_ffn_bias, L2_attn_w_qkv, L2_attn_w_out, L2_xattn_Wq, L2_xattn_bq, L2_xattn_Wk, L2_xattn_bk, L2_xattn_Wv, L2_xattn_bv, L2_xattn_Wo, L2_xattn_bo, L2_ffn_gamma_x, L2_ffn_gamma_slot, L2_ffn_slot_embeds, L2_ffn_w1, L2_ffn_w2, L3_attn_Wa, L3_attn_ba, L3_attn_Wb, L3_attn_bb, L3_attn_Wc, L3_attn_bc, L3_attn_gamma, L3_attn_beta, L3_attn_h0, L3_xattn_fm_w, L3_xattn_fm_b, L3_xattn_fc_w, L3_xattn_fc_b, L3_ffn_cn_w1, L3_ffn_cn_b1, L3_ffn_cn_w2, L3_ffn_cn_b2, L3_ffn_cn_w3, L3_ffn_cn_b3, L3_ffn_cn_w4, L3_ffn_cn_b4, L3_ffn_gc_w1, L3_ffn_gc_b1, L3_ffn_gc_w2, L3_ffn_gc_b2, L3_ffn_gc_w3, L3_ffn_gc_b3, L3_ffn_adaptive_range):
    import jax
    import jax.numpy as jnp

    def _L0_attn_ref(x, mem, wq, wk, wv, wo, w1, b1, w2, b2, lin1, lin2, alpha, theta):
        import jax, jax.numpy as jnp
        import numpy as np
        DIM = 256
        HID = 1024
        NUM_HEADS = 4
        WINDOW = 128
        NUM_PM = 64
        NEG = -1e+30

        def _swa(x_in, wq, wk, wv, wo):
            B, S, D = x_in.shape
            h, dh = (NUM_HEADS, D // NUM_HEADS)
            q = (x_in @ wq.T).reshape(B, S, h, dh).transpose(0, 2, 1, 3)
            k = (x_in @ wk.T).reshape(B, S, h, dh).transpose(0, 2, 1, 3)
            v = (x_in @ wv.T).reshape(B, S, h, dh).transpose(0, 2, 1, 3)
            i = jnp.arange(S)[:, None]
            j = jnp.arange(S)[None, :]
            mask = (j <= i) & (j > i - WINDOW)
            logits = jnp.einsum('bhqd,bhkd->bhqk', q, k) / np.sqrt(dh).astype(np.float32)
            logits = jnp.where(mask, logits, NEG)
            attn = jax.nn.softmax(logits, axis=-1)
            out = jnp.einsum('bhqk,bhkd->bhqd', attn, v)
            out = out.transpose(0, 2, 1, 3).reshape(B, S, D)
            return out @ wo.T

        def _mlp(w1, b1, w2, b2, x):
            return jax.nn.silu(x @ w1.T + b1) @ w2.T + b2
        B, S, D = x.shape
        pm = jnp.broadcast_to(mem[None], (B, NUM_PM, D))
        x_in = jnp.concatenate([pm, x], axis=1)
        out_swa = _swa(x_in, wq, wk, wv, wo)
        k_flat = x_in.reshape(-1, D)
        v_flat = out_swa.reshape(-1, D)

        def loss_fn(params):
            pred = _mlp(*params, k_flat)
            return 0.5 * jnp.sum((pred - v_flat) ** 2)
        grads = jax.grad(loss_fn)((w1, b1, w2, b2))
        upd = jax.tree_util.tree_map(lambda p, g: (1.0 - alpha) * p - theta * g, (w1, b1, w2, b2), grads)
        out_mem = _mlp(*upd, k_flat).reshape(x_in.shape)
        g1 = jax.nn.sigmoid(out_swa @ lin1.T)
        g2 = jax.nn.sigmoid(out_mem @ lin2.T)
        out_merged = g1 * out_swa + g2 * out_mem
        return out_merged[:, NUM_PM:, :]

    def _L0_xattn_ref(x, knowledge_embeddings, Wq, bq, Wk, bk, Wv, bv, Wo, bo):
        import jax, jax.numpy as jnp
        import numpy as np
        import math
        D_MODEL = 256
        N_HEADS = 16
        HEAD_DIM = D_MODEL // N_HEADS
        TOP_K = 32
        SCALE = math.sqrt(HEAD_DIM)

        def _split_heads(t, n):
            B, L, _ = t.shape
            return t.reshape(B, L, N_HEADS, HEAD_DIM).transpose(0, 2, 1, 3)
        B, S, _ = x.shape
        N = knowledge_embeddings.shape[1]
        Q = _split_heads(x @ Wq.T + bq, N_HEADS)
        K = _split_heads(knowledge_embeddings @ Wk.T + bk, N_HEADS)
        V = _split_heads(knowledge_embeddings @ Wv.T + bv, N_HEADS)
        scores = jnp.einsum('bhsd,bhnd->bhsn', Q, K) / SCALE
        k = min(TOP_K, N)
        topk_scores, topk_indices = jax.lax.top_k(scores, k)
        sparse_weights = jax.nn.softmax(topk_scores, axis=-1)
        sel_V = jnp.take_along_axis(V[:, :, None, :, :], topk_indices[..., None], axis=3)
        context = jnp.einsum('bhsk,bhskd->bhsd', sparse_weights, sel_V)
        context = context.transpose(0, 2, 1, 3).reshape(B, S, D_MODEL)
        return context @ Wo.T + bo

    def _L0_ffn_ref(x, router_w, router_b, routed_w1, routed_w3, routed_w2, shared_w1, shared_w3, shared_w2):
        import jax, jax.numpy as jnp
        import numpy as np
        BEST_K = 2

        def _expert(xf, w1, w3, w2):
            return jax.nn.silu(xf @ w1) * (xf @ w3) @ w2
        B, S, D = x.shape
        T = B * S
        xf = x.reshape(T, D)
        logits = xf @ router_w + router_b
        topk_vals, topk_idx = jax.lax.top_k(logits, BEST_K)
        sparse = jnp.full_like(logits, -jnp.inf)
        sparse = sparse.at[jnp.arange(T)[:, None], topk_idx].set(topk_vals)
        gates = jax.nn.softmax(sparse, axis=-1)
        routed = jax.vmap(_expert, in_axes=(None, 0, 0, 0))(xf, routed_w1, routed_w3, routed_w2)
        routed_out = jnp.einsum('etd,te->td', routed, gates)
        shared_out = jax.vmap(_expert, in_axes=(None, 0, 0, 0))(xf, shared_w1, shared_w3, shared_w2).sum(axis=0)
        return (routed_out + shared_out).reshape(B, S, D)

    def _L1_attn_ref(x, q_proj, k_proj, v_proj, q_bias, k_bias, v_bias, ln1_g, ln1_b, ln2_g, ln2_b, ff1_w, ff1_b, ff2_w, ff2_b):
        import jax, jax.numpy as jnp
        import numpy as np
        D_MODEL = 256
        N_HEADS = 16
        HEAD_DIM = D_MODEL // N_HEADS
        WINDOW = 128
        FF_HID = 512
        LN_EPS = 1e-05

        def _layernorm(x, g, b):
            mu = jnp.mean(x, axis=-1, keepdims=True)
            var = jnp.mean(jnp.square(x - mu), axis=-1, keepdims=True)
            return (x - mu) * jax.lax.rsqrt(var + LN_EPS) * g + b

        def _local_attn(q, k, v, window):
            BH, S, d = q.shape
            nw = S // window
            scale = d ** (-0.5)
            qw = (q * scale).reshape(BH, nw, window, d)
            kw = k.reshape(BH, nw, window, d)
            vw = v.reshape(BH, nw, window, d)
            kprev = jnp.pad(kw, ((0, 0), (1, 0), (0, 0), (0, 0)))[:, :-1]
            vprev = jnp.pad(vw, ((0, 0), (1, 0), (0, 0), (0, 0)))[:, :-1]
            bk = jnp.concatenate([kprev, kw], axis=2)
            bv = jnp.concatenate([vprev, vw], axis=2)
            tq = jnp.arange(S).reshape(nw, window)
            tprev = jnp.pad(tq, ((1, 0), (0, 0)), constant_values=-1)[:-1]
            tk = jnp.concatenate([tprev, tq], axis=1)
            mask = (tq[:, :, None] >= tk[:, None, :]) & (tk[:, None, :] >= 0)
            sim = jnp.einsum('bnwd,bnkd->bnwk', qw, bk)
            sim = jnp.where(mask[None], sim, -1000000000.0)
            attn = jax.nn.softmax(sim, axis=-1)
            out = jnp.einsum('bnwk,bnkd->bnwd', attn, bv)
            return out.reshape(BH, S, d)
        B, S, D = x.shape
        H, dh = (N_HEADS, HEAD_DIM)
        Q = (jnp.einsum('bsd,hde->bhse', x, q_proj) + q_bias[None]).reshape(B * H, S, dh)
        K = (jnp.einsum('bsd,hde->bhse', x, k_proj) + k_bias[None]).reshape(B * H, S, dh)
        V = (jnp.einsum('bsd,hde->bhse', x, v_proj) + v_bias[None]).reshape(B * H, S, dh)
        attn = _local_attn(Q, K, V, WINDOW)
        attn = attn.reshape(B, H, S, dh).transpose(0, 2, 1, 3).reshape(B, S, D)
        x = _layernorm(x + attn, ln1_g, ln1_b)
        ff = jnp.maximum(x @ ff1_w + ff1_b, 0.0) @ ff2_w + ff2_b
        x = _layernorm(x + ff, ln2_g, ln2_b)
        return x

    def _L1_xattn_ref(x, encoder_k, encoder_v, Wq1, bq1, Wk1, bk1, Wv1, bv1, Wo1, bo1, Wq2, bq2, Wk2, bk2, Wv2, bv2, Wo2, bo2):
        import jax, jax.numpy as jnp
        import numpy as np
        B, SD, SE, D, H = (4, 512, 512, 256, 16)
        HD = D // H

        def _mha(xq, xk, xv, Wq, bq, Wk, bk, Wv, bv, Wo, bo, causal):
            q = jnp.einsum('bsd,hde->bhse', xq, Wq) + bq[None, :, None, :]
            k = jnp.einsum('bsd,hde->bhse', xk, Wk) + bk[None, :, None, :]
            v = jnp.einsum('bsd,hde->bhse', xv, Wv) + bv[None, :, None, :]
            scale = 1.0 / jnp.sqrt(jnp.asarray(HD, q.dtype))
            scores = jnp.einsum('bhqe,bhke->bhqk', q, k) * scale
            if causal:
                mask = jnp.tril(jnp.ones((q.shape[2], k.shape[2]), bool))
                scores = jnp.where(mask, scores, jnp.finfo(scores.dtype).min)
            w = jax.nn.softmax(scores, axis=-1)
            out = jnp.einsum('bhqk,bhke->bhqe', w, v)
            out = out.transpose(0, 2, 1, 3).reshape(out.shape[0], out.shape[2], D)
            return out @ Wo + bo
        h = _mha(x, x, x, Wq1, bq1, Wk1, bk1, Wv1, bv1, Wo1, bo1, causal=True)
        out = _mha(h, encoder_k, encoder_v, Wq2, bq2, Wk2, bk2, Wv2, bv2, Wo2, bo2, causal=False)
        return out

    def _L1_ffn_ref(x, kernel, input_scale, kernel_scale, bias):
        import jax, jax.numpy as jnp
        import numpy as np
        FEATURES = 256
        D_IN = 256

        def fp8_gemm_optimized(x, input_scale, kernel, kernel_scale):
            s_in = input_scale[0]
            s_k = kernel_scale[0]
            x_q = (x.astype(jnp.float32) / s_in).astype(jnp.float8_e4m3fn)
            k_q = (kernel.astype(jnp.float32) / s_k).astype(jnp.float8_e4m3fn)
            y = jnp.dot(x_q.astype(jnp.float32), k_q.astype(jnp.float32), preferred_element_type=jnp.float32)
            return y * (s_in * s_k)
        dtype = jnp.bfloat16
        x = x.astype(dtype)
        orig_shape = x.shape
        x2 = x.reshape(-1, x.shape[-1])
        y = fp8_gemm_optimized(x2, input_scale, kernel, kernel_scale)
        y = y.astype(dtype) + bias
        return y.reshape(orig_shape[:-1] + (FEATURES,))

    def _L2_attn_ref(x, w_qkv, w_out):
        import jax, jax.numpy as jnp
        import numpy as np
        DIM = 256
        DIM_HEADS = 64
        b, n, _ = x.shape
        h = DIM_HEADS
        qkv = jnp.einsum('bnc,fc->bnf', x, w_qkv)
        q, k, v = jnp.split(qkv, 3, axis=-1)
        q = q.transpose(0, 2, 1)[..., None]
        k = k.transpose(0, 2, 1)[..., None]
        v = v.transpose(0, 2, 1)[..., None]
        scale = 1.0 / jnp.sqrt(jnp.float32(h))
        dots = jnp.einsum('bhid,bhjd->bhij', q, k) * scale
        causal = jnp.tril(jnp.ones((n, n), dtype=bool))
        dots = jnp.where(causal, dots, -jnp.inf)
        attn = jax.nn.softmax(dots, axis=-1)
        out = jnp.einsum('bhij,bhjd->bhid', attn, v)
        out = out[..., 0].transpose(0, 2, 1)
        return jnp.einsum('bnh,ch->bnc', out, w_out)

    def _L2_xattn_ref(query, key, value, Wq, bq, Wk, bk, Wv, bv, Wo, bo):
        import jax, jax.numpy as jnp
        import numpy as np
        D_MODEL = 256
        N_HEADS = 16
        HEAD_DIM = D_MODEL // N_HEADS
        B, S = (2, 512)

        def _split_heads(x):
            b, s, _ = x.shape
            return x.reshape(b, s, N_HEADS, HEAD_DIM).transpose(0, 2, 1, 3)
        q = _split_heads(query @ Wq.T + bq)
        k = _split_heads(key @ Wk.T + bk)
        v = _split_heads(value @ Wv.T + bv)
        energy = jnp.einsum('bhqd,bhkd->bhqk', q, k) / jnp.sqrt(jnp.asarray(HEAD_DIM, q.dtype))
        attn = jax.nn.softmax(energy, axis=-1)
        x = jnp.einsum('bhqk,bhkd->bhqd', attn, v)
        x = x.transpose(0, 2, 1, 3).reshape(query.shape[0], -1, D_MODEL)
        return x @ Wo.T + bo

    def _L2_ffn_ref(x, gamma_x, gamma_slot, slot_embeds, w1, w2):
        import jax, jax.numpy as jnp
        import numpy as np
        EPS = 1e-12

        def rms_norm(t, gamma):
            n = jnp.maximum(jnp.linalg.norm(t, axis=-1, keepdims=True), EPS)
            scale = jnp.sqrt(jnp.asarray(t.shape[-1], t.dtype))
            return t / n * scale * gamma
        b, s, d = x.shape
        e, t, _ = slot_embeds.shape
        xn = rms_norm(x, gamma_x)
        se = rms_norm(slot_embeds, gamma_slot)
        logits = jnp.einsum('bsd,etd->bset', xn, se)
        dispatch = jax.nn.softmax(logits, axis=1)
        slots = jnp.einsum('bsd,bset->betd', xn, dispatch)
        h = jax.nn.gelu(slots @ w1, approximate=False)
        processed = h @ w2
        combine = jax.nn.softmax(logits.reshape(b, s, e * t), axis=-1)
        out = jnp.einsum('bnd,bsn->bsd', processed.reshape(b, e * t, d), combine)
        return out

    def _L3_attn_ref(X, Wa, ba, Wb, bb, Wc, bc, gamma, beta, h0):
        import jax, jax.numpy as jnp
        import numpy as np
        B, L, D = (4, 1024, 256)
        LN_EPS = 1e-05
        SCAN_EPS = 1e-08
        mu = jnp.mean(X, axis=-1, keepdims=True)
        var = jnp.mean(jnp.square(X - mu), axis=-1, keepdims=True)
        Z = (X - mu) * jax.lax.rsqrt(var + LN_EPS) * gamma + beta
        A = jax.nn.sigmoid(jnp.einsum('bld,ed->ble', Z, Wa) + ba)
        P = jnp.cumprod(A, axis=1)
        Bx = jnp.einsum('bld,ed->ble', Z, Wb) + bb
        S = jnp.cumsum(Bx / (P + SCAN_EPS), axis=1)
        h = P * (h0[:, None, :] + S)
        C = jnp.einsum('bld,ed->ble', Z, Wc) + bc
        return C * h + X

    def _L3_xattn_ref(values, keys, query, fm_w, fm_b, fc_w, fc_b):
        import jax, jax.numpy as jnp
        import numpy as np
        EMBED = 256
        HEADS = 16
        HEAD_DIM = EMBED // HEADS
        EXP_DIM = 2 * HEAD_DIM

        def _feature_map(x, fm_w, fm_b):
            z = jnp.einsum('nshd,ed->nshe', x, fm_w) + fm_b
            return jnp.concatenate([jnp.exp(z), jnp.exp(-z)], axis=-1)
        N, S, _ = query.shape
        v = values.reshape(N, -1, HEADS, HEAD_DIM)
        k = keys.reshape(N, -1, HEADS, HEAD_DIM)
        q = query.reshape(N, -1, HEADS, HEAD_DIM)
        v, k, q = (_feature_map(x, fm_w, fm_b) for x in (v, k, q))
        scores = jnp.einsum('nqhd,nkhd->nhqk', q, k) / jnp.sqrt(jnp.float32(EMBED))
        attn = jax.nn.softmax(scores, axis=-1)
        out = jnp.einsum('nhql,nlhd->nqhd', attn, v)
        out = out.reshape(N, S, HEADS * EXP_DIM)
        return out @ fc_w.T + fc_b

    def _L3_ffn_ref(x, cn_w1, cn_b1, cn_w2, cn_b2, cn_w3, cn_b3, cn_w4, cn_b4, gc_w1, gc_b1, gc_w2, gc_b2, gc_w3, gc_b3, adaptive_range):
        import jax, jax.numpy as jnp
        import numpy as np
        B, S, DIM = (4, 1024, 256)
        BASE_COUPLING = 0.1
        NUM_CYCLES = 3

        def _gelu(x):
            return jax.nn.gelu(x, approximate=False)

        def _coupling_net(h, w1, b1, w2, b2, w3, b3, w4, b4):
            h = _gelu(h @ w1 + b1)
            h = _gelu(h @ w2 + b2)
            h = _gelu(h @ w3 + b3)
            return jax.nn.sigmoid(h @ w4 + b4)

        def _global_net(h, w1, b1, w2, b2, w3, b3):
            h = _gelu(h @ w1 + b1)
            h = _gelu(h @ w2 + b2)
            return jax.nn.sigmoid(h @ w3 + b3)

        def _twist(x):
            o_r, o_i, p_r, p_i = jnp.split(x, 4, axis=-1)
            return jnp.concatenate([p_r, -p_i, -o_r, o_i], axis=-1)
        global_context = x.mean(axis=1, keepdims=True)
        gf = _global_net(global_context, gc_w1, gc_b1, gc_w2, gc_b2, gc_w3, gc_b3)
        out = x
        for _ in range(NUM_CYCLES):
            tf = _coupling_net(out, cn_w1, cn_b1, cn_w2, cn_b2, cn_w3, cn_b3, cn_w4, cn_b4)
            combined = 0.7 * gf + 0.3 * tf
            coupling = BASE_COUPLING + adaptive_range * (combined - 0.5) * 2.0
            out = out + coupling * _twist(out)
        return out
    x = x + _L0_attn_ref(_layernorm(x, axis=-1), L0_attn_mem, L0_attn_wq, L0_attn_wk, L0_attn_wv, L0_attn_wo, L0_attn_w1, L0_attn_b1, L0_attn_w2, L0_attn_b2, L0_attn_lin1, L0_attn_lin2, L0_attn_alpha, L0_attn_theta)
    x = x + _L0_xattn_ref(_layernorm(x, axis=-1), ctx_1024, L0_xattn_Wq, L0_xattn_bq, L0_xattn_Wk, L0_xattn_bk, L0_xattn_Wv, L0_xattn_bv, L0_xattn_Wo, L0_xattn_bo)
    x = x + _L0_ffn_ref(_layernorm(x, axis=-1), L0_ffn_router_w, L0_ffn_router_b, L0_ffn_routed_w1, L0_ffn_routed_w3, L0_ffn_routed_w2, L0_ffn_shared_w1, L0_ffn_shared_w3, L0_ffn_shared_w2)
    x = x + _L1_attn_ref(_layernorm(x, axis=-1), L1_attn_q_proj, L1_attn_k_proj, L1_attn_v_proj, L1_attn_q_bias, L1_attn_k_bias, L1_attn_v_bias, L1_attn_ln1_g, L1_attn_ln1_b, L1_attn_ln2_g, L1_attn_ln2_b, L1_attn_ff1_w, L1_attn_ff1_b, L1_attn_ff2_w, L1_attn_ff2_b)
    x = x + _L1_xattn_ref(_layernorm(x, axis=-1), ctx_1024, ctx_1024, L1_xattn_Wq1, L1_xattn_bq1, L1_xattn_Wk1, L1_xattn_bk1, L1_xattn_Wv1, L1_xattn_bv1, L1_xattn_Wo1, L1_xattn_bo1, L1_xattn_Wq2, L1_xattn_bq2, L1_xattn_Wk2, L1_xattn_bk2, L1_xattn_Wv2, L1_xattn_bv2, L1_xattn_Wo2, L1_xattn_bo2)
    x = x + _L1_ffn_ref(_layernorm(x, axis=-1), L1_ffn_kernel, L1_ffn_input_scale, L1_ffn_kernel_scale, L1_ffn_bias)
    x = x + _L2_attn_ref(_layernorm(x, axis=-1), L2_attn_w_qkv, L2_attn_w_out)
    x = x + _L2_xattn_ref(_layernorm(x, axis=-1), ctx_1024, ctx_1024, L2_xattn_Wq, L2_xattn_bq, L2_xattn_Wk, L2_xattn_bk, L2_xattn_Wv, L2_xattn_bv, L2_xattn_Wo, L2_xattn_bo)
    x = x + _L2_ffn_ref(_layernorm(x, axis=-1), L2_ffn_gamma_x, L2_ffn_gamma_slot, L2_ffn_slot_embeds, L2_ffn_w1, L2_ffn_w2)
    x = x + _L3_attn_ref(_layernorm(x, axis=-1), L3_attn_Wa, L3_attn_ba, L3_attn_Wb, L3_attn_bb, L3_attn_Wc, L3_attn_bc, L3_attn_gamma, L3_attn_beta, L3_attn_h0)
    x = x + _L3_xattn_ref(ctx_1024, ctx_1024, _layernorm(x, axis=-1), L3_xattn_fm_w, L3_xattn_fm_b, L3_xattn_fc_w, L3_xattn_fc_b)
    x = x + _L3_ffn_ref(_layernorm(x, axis=-1), L3_ffn_cn_w1, L3_ffn_cn_b1, L3_ffn_cn_w2, L3_ffn_cn_b2, L3_ffn_cn_w3, L3_ffn_cn_b3, L3_ffn_cn_w4, L3_ffn_cn_b4, L3_ffn_gc_w1, L3_ffn_gc_b1, L3_ffn_gc_w2, L3_ffn_gc_b2, L3_ffn_gc_w3, L3_ffn_gc_b3, L3_ffn_adaptive_range)
    return x

_drawn_inputs = setup_inputs


def setup_inputs(seed=0):
    import zlib

    import numpy as np

    out = dict(_drawn_inputs(seed))
    spreads = {'L0_attn_b1': (0.0, 0.1),
     'L0_attn_b2': (0.0, 0.44),
     'L0_xattn_bq': (0.0, 0.1),
     'L0_xattn_bk': (0.0, 2.0),
     'L0_xattn_bv': (0.0, 0.1),
     'L0_xattn_bo': (0.0, 0.1),
     'L0_ffn_router_b': (0.0, 0.8),
     'L1_attn_ln1_g': (1.0, 0.2),
     'L1_attn_ln1_b': (0.0, 0.1),
     'L1_attn_ln2_g': (1.0, 0.2),
     'L1_attn_ln2_b': (0.0, 0.1),
     'L1_attn_ff1_b': (0.0, 0.299),
     'L1_attn_ff2_b': (0.0, 0.304),
     'L1_xattn_bq1': (0.0, 2.0),
     'L1_xattn_bk1': (0.0, 2.0),
     'L1_xattn_bv1': (0.0, 0.41),
     'L1_xattn_bo1': (0.0, 0.995),
     'L1_xattn_bq2': (0.0, 0.383),
     'L1_xattn_bk2': (0.0, 2.0),
     'L1_xattn_bv2': (0.0, 0.1),
     'L1_xattn_bo2': (0.0, 0.1),
     'L1_ffn_bias': (0.0, 0.315),
     'L2_xattn_bq': (0.0, 0.539),
     'L2_xattn_bk': (0.0, 2.0),
     'L2_xattn_bv': (0.0, 0.295),
     'L2_xattn_bo': (0.0, 0.273),
     'L2_ffn_gamma_x': (1.0, 0.2),
     'L2_ffn_gamma_slot': (1.0, 0.2),
     'L3_attn_ba': (0.0, 0.494),
     'L3_attn_bb': (0.0, 0.51),
     'L3_attn_bc': (0.0, 0.304),
     'L3_attn_gamma': (1.0, 0.2),
     'L3_attn_beta': (0.0, 0.275),
     'L3_xattn_fc_b': (0.0, 0.657),
     'L3_ffn_cn_b1': (0.0, 2.0),
     'L3_ffn_cn_b2': (0.0, 2.0),
     'L3_ffn_cn_b3': (0.0, 2.0),
     'L3_ffn_gc_b1': (0.0, 2.0),
     'L3_ffn_gc_b2': (0.0, 2.0)}
    factors = {'L0_attn_mem': 3.843,
     'L0_attn_wq': 8.0,
     'L0_attn_wk': 8.0,
     'L0_attn_wv': 3.672,
     'L0_attn_wo': 3.297,
     'L0_attn_lin1': 8.0,
     'L0_attn_lin2': 8.0,
     'L0_ffn_router_w': 4.552,
     'L0_ffn_routed_w1': 4.043,
     'L0_ffn_routed_w3': 3.886,
     'L0_ffn_routed_w2': 3.795,
     'L1_attn_q_bias': 3.945,
     'L1_attn_k_bias': 200.0,
     'L1_xattn_Wq1': 2.668,
     'L2_attn_w_qkv': 7.431,
     'L3_attn_h0': 5.248,
     'L3_ffn_cn_w1': 125.534,
     'L3_ffn_cn_w2': 199.521,
     'L3_ffn_cn_w3': 59.17,
     'L3_ffn_cn_w4': 152.046,
     'L3_ffn_gc_w1': 8.0,
     'L3_ffn_gc_w2': 8.0,
     'L3_ffn_gc_w3': 7.407,
     'L0_ffn_shared_w1': 4.096,
     'L0_ffn_shared_w3': 4.577,
     'L0_ffn_shared_w2': 4.877,
     'L1_attn_v_bias': 2.866}
    for name, (base, spread) in spreads.items():
        noise = np.random.default_rng([zlib.crc32(name.encode()), seed]).standard_normal(out[name].shape)
        drawn = base * np.exp(spread * noise) if base else spread * noise
        out[name] = jnp.asarray(drawn.astype(out[name].dtype))
    for name, factor in factors.items():
        out[name] = (out[name] * factor).astype(out[name].dtype)
    return out
```

```python
from contextlib import ExitStack

import concourse.bass as bass
from concourse import mybir

F32 = mybir.dt.float32
BF16 = mybir.dt.bfloat16
U32 = mybir.dt.uint32
I32 = mybir.dt.int32
ALU = mybir.AluOpType
ACT = mybir.ActivationFunctionType
AX = mybir.AxisListType.X

P = 128
B, SEQ, D = 8, 256, 256
TILES = B * SEQ // P
KC = D // P
CTX = 77
H, HD, PAD = 16, 16, 32
HC = H // 4
VW = HD + 1
MEM, SH, SD_ = 64, 4, 64
SVW = SD_ + 1
HID = 1024
E_ROUTED, E_ALL, EH = 8, 10, 128
FF = 512
SLOTS, E_SLOT_HID = 1024, 1024
TOPK = 32
NH1 = 64
LN_EPS = 1e-5
BIG = 3.0e38

PACKS = {
    "L0_attn": [("wq", KC * D), ("wk", KC * D), ("wv", KC * SH * SVW), ("wo", KC * D), ("lin1", KC * D),
                ("lin2", KC * D), ("w1T", KC * HID), ("w2T", HID // P * D), ("w2", KC * HID)],
    "L0_xattn": [("wq", KC * H * PAD), ("wk", KC * H * PAD), ("wv", KC * H * VW), ("wo", KC * D)],
    "L0_ffn": [("router", KC * E_ROUTED), ("w1", E_ALL * KC * EH), ("w3", E_ALL * KC * EH), ("w2", E_ALL * D)],
    "L1_attn": [("wq", KC * H * PAD), ("wk", KC * H * PAD), ("wv", KC * H * VW), ("ff1", KC * FF),
                ("ff2", FF // P * D)],
    "L1_xattn": [(w + n, c) for n in "12" for w, c in (("wq", KC * H * PAD), ("wk", KC * H * PAD),
                                                       ("wv", KC * H * VW), ("wo", KC * D))],
    "L1_ffn": [],
    "L2_attn": [("wqkv", KC * 3 * NH1), ("wout", D)],
    "L2_xattn": [("wq", KC * H * PAD), ("wk", KC * H * PAD), ("wv", KC * H * VW), ("wo", KC * D)],
    "L2_ffn": [("slots", SLOTS // P * D), ("w1", KC * E_SLOT_HID), ("w2", E_SLOT_HID // P * D)],
    "L3_attn": [("wa", KC * D), ("wb", KC * D), ("wc", KC * D)],
    "L3_xattn": [("wf", KC * H * PAD), ("wv", KC * D), ("fc", 4 * D)],
    "L3_ffn": [("cn1", KC * D), ("cn2", KC * 128), ("cn3", 64), ("cn4", 1), ("gc1", KC * 128), ("gc2", 64),
               ("gc3", 1)],
}
ROWS = {
    "L0_attn": [("v1", SH * SVW), ("b1", HID), ("b2", D)],
    "L0_xattn": [("bv", H * VW), ("bo", D)],
    "L0_ffn": [("rb", E_ROUTED)],
    "L1_attn": [("bv", H * VW), ("ff2b", D)],
    "L1_xattn": [("bv1", H * VW), ("bv2", H * VW), ("bo2", D)],
    "L1_ffn": [], "L2_attn": [],
    "L2_xattn": [("bv", H * VW), ("bo", D)],
    "L2_ffn": [], "L3_attn": [],
    "L3_xattn": [("bf", H * PAD), ("bv", D), ("fcb", D)],
    "L3_ffn": [],
}
SPREAD = {"L1_attn": ["ln1_g", "ln1_b", "ln2_g", "ln2_b"]}
STAGES = list(PACKS)
COLS = [("L0_attn_b1", 8), ("L0_xattn_bq", HC), ("L0_xattn_bk", HC), ("L1_attn_bq", HC), ("L1_attn_bk", HC),
        ("L1_attn_ff1b", 4), ("L1_xattn_bq1", HC), ("L1_xattn_bk1", HC), ("L1_xattn_bo1", KC),
        ("L1_xattn_bq2", HC), ("L1_xattn_bk2", HC), ("L2_xattn_bq", HC), ("L2_xattn_bk", HC),
        ("L2_ffn_gx", KC), ("L2_ffn_gs", KC), ("L3_attn_ba", KC), ("L3_attn_bb", KC), ("L3_attn_bc", KC),
        ("L3_attn_g", KC), ("L3_attn_be", KC), ("L3_attn_h0", KC), ("L3_ffn_cb1", KC), ("L3_ffn_cb2", 1),
        ("L3_ffn_cb3", 1), ("L3_ffn_gb1", 1), ("L3_ffn_gb2", 1), ("sign", 1), ("mean", 1), ("one", 1)]
SCALARS = ["alpha", "theta", "s_in", "s_k", "cn_b4", "gc_b3", "ar"]
MASKS = [("selfA", 512), ("selfB", 512), ("keyA", 512), ("keyC", 512), ("swa0", 2 * (MEM + P)), ("swa1", 512),
         ("swam", 2 * MEM)]


def Bag(**things):
    return type("Bag", (), things)


def places(fields):
    at, out = 0, {}
    for name, n in fields:
        out[name] = (at, n)
        at += n
    return out, at


COMMON = ("done", "dve_step", "z", "zT_ps", "zT", "qkv_ps", "q", "kv", "s_ps", "s_sb", "prob", "probT_ps", "probT_a",
          "probT_v", "o_ps", "o", "oT_ps", "oT", "out_ps", "ctx")


class SignalPool:

    def __init__(self, nc, ctx):
        self.nc, self.ctx, self.sems, self.raised, self.own = nc, ctx, {}, {}, {}

    def called(self, stage, name):
        if name in COMMON:
            return name
        own = self.own.setdefault(stage, {})
        return own.setdefault(name, f"of_stage_{len(own)}")

    def lanes(self, name, n):
        sems = self.sems.setdefault(name, [])
        while len(sems) < n:
            sems.append(self.ctx.enter_context(self.nc.semaphore(f"{name}_{len(sems)}")))
        self.raised.setdefault(name, [0, 0])
        return sems


class Signals:

    def __init__(self, pool, stage, trips, lanes, **per):
        self.stage, self.trips, self.lanes, self.per = stage, trips, lanes, per
        at = {n: pool.called(stage, n) for n in per}
        self.sems = {n: pool.lanes(at[n], lanes) for n in per}
        self.base = {n: list(pool.raised[at[n]]) for n in per}
        for n, k in per.items():
            for lane in range(lanes):
                pool.raised[at[n]][lane] += trips * k
        self.ends = [pool.raised["done"][lane] for lane in (0, 1)]

    def up(self, name, lane=0):
        return self.sems[name][lane], 1

    def at(self, name, lane, trip, n):
        k = self.per[name]
        assert n <= k, (self.stage, name, n, k)
        return self.sems[name][lane], trip * k + (self.base[name][lane] + n)


class Chain:

    def __init__(self, eng, sig, lane, trip):
        self.eng, self.sig, self.lane, self.trip, self.n = eng, sig, lane, trip, 0

    def link(self, ins):
        self.n += 1
        ins.then_inc(*self.sig.up("dve_step", self.lane))
        self.eng.wait_ge(*self.sig.at("dve_step", self.lane, self.trip, self.n))

    def close(self):
        assert self.n == self.sig.per["dve_step"], (self.sig.stage, self.n)


def cut(ap, **sizes):
    (name, n), = sizes.items()
    return ap.rearrange(f"p ({name} f) -> p {name} f", **{name: n})


class Carve:

    def __init__(self, tensor, size):
        self.tensor, self.size, self.at = tensor, size, 0

    def take(self, *shape, dt=None):
        n = 1
        for s in shape:
            n *= s
        words = n if dt is None else (n + 1) // 2
        ap = self.tensor[:, self.at:self.at + words]
        self.at += words
        assert self.at <= self.size, (self.at, self.size)
        if dt is not None:
            ap = ap.bitcast(dt)
        if len(shape) == 2:
            ap = ap.rearrange("p (a b) -> p a b", a=shape[0])
        if len(shape) == 3:
            ap = ap.rearrange("p (a b c) -> p a b c", a=shape[0], b=shape[1])
        return ap



def enter(k, eng, sig):
    for lane in (0, 1):
        if sig.base["done"][lane]:
            eng.wait_ge(sig.sems["done"][lane], sig.base["done"][lane])
    sem, value = k.loaded[sig.stage]
    if value:
        eng.wait_ge(sem, value)


def hold(k, eng, name):
    eng.sem_inc(k.held[name], 1)


def x_of(k, trip, lane, lanes=2):
    return k.x[:, bass.ts(trip * lanes + lane, 2), :]


def bank(k, lane, i):
    return k.ps[:, 4 * lane + i, :]


def banks(k, lane, i, n):
    return k.ps[:, 4 * lane + i:4 * lane + i + n, :]


def w_of(k, stage, name, rows=None):
    at, n = k.pack[stage][name]
    ap = k.slot[stage][:, at:at + n]
    return ap if rows is None else ap.rearrange("p (r n) -> p r n", r=rows)


def row_of(k, stage, name):
    at, n = k.rows[stage][name]
    return k.slot[stage][0:1, at:at + n]


def spread_of(k, stage, name):
    at, n = k.spread[stage][name]
    return k.slot[stage][:, at:at + n]


def col_of(k, name, c=0, parts=P):
    at, _ = k.colpos[name]
    return k.cols[0:parts, at + c:at + c + 1]


def scalar_of(k, name, parts=P):
    i = SCALARS.index(name)
    return k.scalars[0:parts, i:i + 1]


def mask_of(k, name):
    at, n = k.maskpos[name]
    return k.masks[:, at:at + n]


RSQRT_STEPS = 10
RSQRT_GUESS = float(0x5F3759DF)


def rsqrt(k, link, y, v, t):
    dve = k.nc.vector
    link(dve.tensor_scalar(y.bitcast(I32), v.bitcast(I32), -0.5, RSQRT_GUESS, ALU.mult, ALU.add))
    for _ in range(3):
        link(dve.scalar_tensor_tensor(t, y, -0.5, y, ALU.mult, ALU.mult))
        link(dve.tensor_tensor(t, t, v, ALU.mult))
        link(dve.scalar_tensor_tensor(y, t, 1.5, y, ALU.add, ALU.mult))


def layernorm(k, ch, src, dst, st):
    v = k.nc.vector
    for t in (0, 1):
        ins = v.bn_stats(st[:, 6 * t:6 * t + 6], src[:, t, :])
    ch.link(ins)
    hold(k, ch.eng, "vector")
    for t in (0, 1):
        ins = v.bn_aggr(st[:, 12 + 2 * t:14 + 2 * t], st[:, 6 * t:6 * t + 6])
    ch.link(ins)
    ch.link(v.tensor_scalar(st[:, 16:18], st[:, 13:16:2], LN_EPS, None, ALU.add))
    rsqrt(k, ch.link, st[:, 18:20], st[:, 16:18], st[:, 20:22])
    for t in (0, 1):
        ins = v.tensor_scalar(dst[:, t, :], src[:, t, :], st[:, 12 + 2 * t:13 + 2 * t], st[:, 18 + t:19 + t],
                              ALU.subtract, ALU.mult)
    return ins


def norms_plan(k, stage):
    return Bag(stats=Signals(k.signals, stage, TILES // 2, 1, dve_step=1),
                           rest=Signals(k.signals, stage, 1, 1, dve_step=2 + RSQRT_STEPS))


def norms_vector(k, dve, s):
    v = k.nc.vector
    with dve.Fori(0, s.stats.trips) as trip:
        for t in (0, 1):
            ins = v.bn_stats(k.stats[:, bass.ds((trip * 2 + t) * 6, 6)], x_of(k, trip, 0, 1)[:, t, :])
        ins.then_inc(*s.stats.up("dve_step"))
    dve.wait_ge(*s.stats.at("dve_step", 0, s.stats.trips - 1, 1))
    hold(k, dve, "vector")
    ch = Chain(dve, s.rest, 0, 0)
    for t in range(TILES):
        ins = v.bn_aggr(k.norm[:, t, :], k.stats[:, 6 * t:6 * t + 6])
    ch.link(ins)
    ch.link(v.tensor_scalar(k.var, k.norm[:, :, 1:2].rearrange("p t o -> p (t o)"), LN_EPS, None, ALU.add))
    rsqrt(k, ch.link, k.rstd, k.var, k.newton)
    ch.close()


def ln_apply(k, trip, lane, lanes, dst):
    x, tiles = x_of(k, trip, lane, lanes), bass.ts(trip * lanes + lane, 2)
    norm, rstd = k.norm[:, tiles, :], k.rstd[:, tiles]
    for t in (0, 1):
        ins = k.nc.vector.tensor_scalar(dst[:, t, :], x[:, t, :], norm[:, t, 0:1], rstd[:, t:t + 1], ALU.subtract,
                                        ALU.mult)
    return ins


def ln_vector(k, dve, sig, lane, trip, buf):
    dve.wait_ge(*sig.at("done", lane, trip, 0))
    hold(k, dve, "vector")
    ln_apply(k, trip, lane, 2, buf.z).then_inc(*sig.up("z", lane))


def transpose_z_tensor(k, pe, sig, lane, trip, src, out):
    for c in range(KC):
        for t in (0, 1):
            ins = k.nc.tensor.transpose(out[:, (2 * c + t) * P:(2 * c + t + 1) * P], src[:, t, c * P:(c + 1) * P],
                                        k.ident[:, :])
    return ins


def products(k, out, pairs, row=None, start=True):
    n = len(pairs) + (row is not None)
    for i, (lhsT, rhs) in enumerate(pairs):
        ins = k.nc.tensor.matmul(out, lhsT, rhs, start=start and i == 0, stop=i == n - 1)
    if row is not None:
        ins = k.nc.tensor.matmul(out, k.ones[0:1, 0:out.shape[0]], row, start=False, stop=True)
    return ins


def proj_feature(k, out, w, src, cols, n):
    return products(k, out, [(w[:, c, cols:cols + n], src[:, c, :]) for c in range(KC)])


def proj_token(k, out, src, t, w, row=None, kc=KC):
    return products(k, out, [(src[:, c, t:t + P], w[:, c, :]) for c in range(kc)], row)



CROSS = [(0, (0, 1, 2, 3), 1), (1, (0, 1, 2, 3), 1)]
SELF = [(0, (0, 1, 2, 3), 1), (1, (0, 1), 2), (1, (2, 3), 2)]


def attention(kind, p="", hd=HD, vw=VW, scale=0.25, topk=False):
    return Bag(p=p, rounds=SELF if kind == "self" else CROSS, causal=kind == "self", hd=hd, vw=vw,
                           nk=P if kind == "self" else CTX, scale=scale, topk=topk)


def attention_signals(a):
    n = len(a.rounds)
    return {a.p + s: n for s in ("s_ps", "s_sb", "prob", "probT_ps", "probT_a", "probT_v", "o_ps", "o")}


def attention_buffers(c, a, buf):
    nkb = 2 if a.causal else 1
    buf.qT = c.take(HC, SEQ)
    buf.kT = c.take(HC, SEQ if a.causal else CTX)
    buf.v = c.take(nkb, H * a.vw)
    buf.s = c.take(4, 512)
    buf.probT = c.take(4, 512)
    buf.o = c.take(2, H * (a.vw - 1))
    buf.oT = c.take(H * (a.vw - 1) // P, SEQ)
    buf.m = c.take(2 * H)
    if a.topk:
        buf.left = c.take(4, 512)
        buf.top = c.take(H, 4 * 8)


def scores_tensor(k, pe, sig, lane, trip, a, buf, r):
    t, chunks, nkb = a.rounds[r]
    if r:
        pe.wait_ge(*sig.at(a.p + "o", lane, trip, r))
    nk = nkb * a.nk
    if a.causal:
        for i in range(4):
            k.nc.tensor.matmul(bank(k, lane, i), k.identb[:, :], mask_of(k, "selfA" if nkb == 1 else "selfB"),
                               start=True, stop=False, skip_group_check=True)
    for ci, c in enumerate(chunks):
        for i in range(4):
            at = ci * nkb * P
            ins = k.nc.tensor.matmul(bank(k, lane, i)[:, at:at + nk],
                                     buf.qT[PAD * i:PAD * i + a.hd, c, t * P:(t + 1) * P],
                                     buf.kT[PAD * i:PAD * i + a.hd, c, 0:nk],
                                     start=not a.causal, stop=True, skip_group_check=a.causal)
    ins.then_inc(*sig.up(a.p + "s_ps", lane))


def softmax_vector(k, dve, sig, lane, trip, ch, a, buf, r):
    v = k.nc.vector
    t, chunks, nkb = a.rounds[r]
    nk, n = nkb * a.nk, 4 * len(chunks)
    s_ps = banks(k, lane, 0, 4).rearrange("p b f -> p (b f)").rearrange("p (h f) -> p h f", h=n)[:, :, 0:nk]
    s_sb = buf.s.rearrange("p b f -> p (b f)").rearrange("p (h f) -> p h f", h=n)[:, :, 0:nk]
    m = buf.m[:, 0:n]
    dve.wait_ge(*sig.at(a.p + "s_ps", lane, trip, r + 1))
    if r:
        dve.wait_ge(*sig.at(a.p + "probT_ps", lane, trip, r))
    if not a.topk:
        ch.link(v.tensor_reduce(m, s_ps, AX, ALU.max))
        v.tensor_tensor(s_sb, s_ps, m.unsqueeze(2).broadcast_to([P, n, nk]), ALU.subtract)\
            .then_inc(*sig.up(a.p + "s_sb", lane))
        return
    left = buf.left.rearrange("p b f -> p (b f)").rearrange("p (h f) -> p h f", h=n)[:, :, 0:nk]
    ch.link(v.tensor_copy(left, s_ps))
    for i in range(TOPK // 8):
        if i == 0:
            hold(k, dve, "vector")
        for h in range(n):
            ins = v.max(buf.top[:, h, 8 * i:8 * i + 8], left[:, h, :])
        ch.link(ins)
        hold(k, dve, "vector")
        for h in range(n):
            ins = v.match_replace(left[:, h, :], buf.top[:, h, 8 * i:8 * i + 8], left[:, h, :], -BIG)
        ch.link(ins)
        hold(k, dve, "vector")
    v.tensor_tensor(s_sb, s_ps, buf.top[:, :, 0:1].broadcast_to([P, n, nk]), ALU.subtract)\
        .then_inc(*sig.up(a.p + "s_sb", lane))


def probs_scalar(k, act, sig, lane, trip, a, buf, r):
    t, chunks, nkb = a.rounds[r]
    nk, n = nkb * a.nk, 4 * len(chunks)
    s_sb = buf.s.rearrange("p b f -> p (b f)").rearrange("p (h f) -> p h f", h=n)[:, :, 0:nk]
    act.wait_ge(*sig.at(a.p + "s_sb", lane, trip, r + 1))
    k.nc.scalar.activation(s_sb, s_sb, ACT.Exp, scale=a.scale).then_inc(*sig.up(a.p + "prob", lane))


def topk_vector(k, dve, sig, lane, trip, ch, a, buf, r):
    n = H
    left = buf.left.rearrange("p b f -> p (b f)").rearrange("p (h f) -> p h f", h=n)[:, :, 0:a.nk]
    s_sb = buf.s.rearrange("p b f -> p (b f)").rearrange("p (h f) -> p h f", h=n)[:, :, 0:a.nk]
    dve.wait_ge(*sig.at(a.p + "prob", lane, trip, r + 1))
    k.nc.vector.scalar_tensor_tensor(s_sb, left, -BIG, s_sb, ALU.is_equal, ALU.mult)\
        .then_inc(*sig.up(a.p + "kept", lane))


def probs_tensor(k, pe, sig, lane, trip, a, buf, r):
    t, chunks, nkb = a.rounds[r]
    pe.wait_ge(*sig.at(a.p + ("kept" if a.topk else "prob"), lane, trip, r + 1))
    for s in range(len(chunks) * nkb):
        for i in range(4):
            ins = k.nc.tensor.transpose(bank(k, lane, i)[0:a.nk, s * P:(s + 1) * P],
                                        buf.s[:, i, s * P:s * P + a.nk], k.ident[:, :])
    ins.then_inc(*sig.up(a.p + "probT_ps", lane))


def probsT_scalar(k, act, sig, lane, trip, a, buf, r):
    act.wait_ge(*sig.at(a.p + "probT_ps", lane, trip, r + 1))
    if r:
        act.wait_ge(*sig.at(a.p + "o_ps", lane, trip, r))
    k.nc.scalar.activation(buf.probT[0:a.nk, 0:2, :], banks(k, lane, 0, 2)[0:a.nk], ACT.Copy)\
        .then_inc(*sig.up(a.p + "probT_a", lane))


def probsT_vector(k, dve, sig, lane, trip, a, buf, r):
    dve.wait_ge(*sig.at(a.p + "probT_ps", lane, trip, r + 1))
    if r:
        dve.wait_ge(*sig.at(a.p + "o_ps", lane, trip, r))
    k.nc.vector.tensor_copy(buf.probT[0:a.nk, 2:4, :], banks(k, lane, 2, 2)[0:a.nk])\
        .then_inc(*sig.up(a.p + "probT_v", lane))


def outputs_tensor(k, pe, sig, lane, trip, a, buf, r):
    t, chunks, nkb = a.rounds[r]
    pe.wait_ge(*sig.at(a.p + "probT_a", lane, trip, r + 1))
    pe.wait_ge(*sig.at(a.p + "probT_v", lane, trip, r + 1))
    for ci, c in enumerate(chunks):
        for i in range(4):
            h = 4 * c + i
            out = bank(k, lane, h // 8)[:, h % 8 * a.vw:(h % 8 + 1) * a.vw]
            for kb in range(nkb):
                s = ci * nkb + kb
                ins = k.nc.tensor.matmul(out, buf.probT[0:a.nk, i, s * P:(s + 1) * P],
                                         buf.v[0:a.nk, kb, h * a.vw:(h + 1) * a.vw], start=kb == 0,
                                         stop=kb == nkb - 1)
    ins.then_inc(*sig.up(a.p + "o_ps", lane))


def outputs_vector(k, dve, sig, lane, trip, ch, a, buf, r):
    v = k.nc.vector
    t, chunks, nkb = a.rounds[r]
    halves = sorted({c // 2 for c in chunks})
    e = a.vw - 1
    rec = buf.m[:, H:2 * H]
    dve.wait_ge(*sig.at(a.p + "o_ps", lane, trip, r + 1))
    view = {g: bank(k, lane, g)[:, 0:8 * a.vw].rearrange("p (h e) -> p h e", h=8) for g in halves}
    for g in halves:
        ins = v.reciprocal(rec[:, 8 * g:8 * g + 8].unsqueeze(2), view[g][:, :, e:e + 1])
    ch.link(ins)
    for g in halves:
        ins = v.tensor_tensor(buf.o[:, t, 8 * g * e:8 * (g + 1) * e].rearrange("p (h e) -> p h e", h=8),
                              view[g][:, :, 0:e],
                              rec[:, 8 * g:8 * g + 8].unsqueeze(2).broadcast_to([P, 8, e]), ALU.mult)
    ins.then_inc(*sig.up(a.p + "o", lane))


def attention_tensor(k, pe, sig, trip, a, bufs):
    for r in range(len(a.rounds)):
        for lane, buf in enumerate(bufs):
            scores_tensor(k, pe, sig, lane, trip, a, buf, r)
        for lane, buf in enumerate(bufs):
            probs_tensor(k, pe, sig, lane, trip, a, buf, r)
        for lane, buf in enumerate(bufs):
            outputs_tensor(k, pe, sig, lane, trip, a, buf, r)


def attention_scalar(k, act, sig, trip, a, bufs):
    for r in range(len(a.rounds)):
        for lane, buf in enumerate(bufs):
            probs_scalar(k, act, sig, lane, trip, a, buf, r)
        for lane, buf in enumerate(bufs):
            probsT_scalar(k, act, sig, lane, trip, a, buf, r)


def attention_vector(k, dve, sig, trip, chains, a, bufs):
    for r in range(len(a.rounds)):
        for lane, buf in enumerate(bufs):
            softmax_vector(k, dve, sig, lane, trip, chains[lane], a, buf, r)
        if a.topk:
            for lane, buf in enumerate(bufs):
                topk_vector(k, dve, sig, lane, trip, chains[lane], a, buf, r)
        for lane, buf in enumerate(bufs):
            probsT_vector(k, dve, sig, lane, trip, a, buf, r)
        for lane, buf in enumerate(bufs):
            outputs_vector(k, dve, sig, lane, trip, chains[lane], a, buf, r)


def oT_tensor(k, pe, sig, lane, trip, a, buf):
    pe.wait_ge(*sig.at(a.p + "o", lane, trip, len(a.rounds)))
    for c in range(H * (a.vw - 1) // P):
        for t in (0, 1):
            at = (2 * c + t) * P
            ins = k.nc.tensor.transpose(bank(k, lane, 2 + at // 512)[:, at % 512:at % 512 + P],
                                        buf.o[:, t, c * P:(c + 1) * P], k.ident[:, :])
    ins.then_inc(*sig.up(a.p + "oT_ps", lane))


def oT_scalar(k, act, sig, lane, trip, a, buf):
    n = H * (a.vw - 1) // 256
    act.wait_ge(*sig.at(a.p + "oT_ps", lane, trip, 1))
    k.nc.scalar.activation(buf.oT.rearrange("p c t -> p (c t)"), banks(k, lane, 2, n).rearrange("p b f -> p (b f)"),
                           ACT.Copy).then_inc(*sig.up(a.p + "oT", lane))


def out_tensor(k, pe, sig, lane, trip, a, buf, w, row, kc=KC):
    pe.wait_ge(*sig.at(a.p + "oT", lane, trip, 1))
    for t in (0, 1):
        ins = proj_token(k, bank(k, lane, 0)[:, t * D:(t + 1) * D], buf.oT, t * P, w, row, kc)
    ins.then_inc(*sig.up("out_ps", lane))


def residual_vector(k, dve, sig, lane, trip, i=0):
    x = x_of(k, trip, lane)
    dve.wait_ge(*sig.at("out_ps", lane, trip, 1))
    k.nc.vector.tensor_tensor(x, x, bank(k, lane, i).rearrange("p (t d) -> p t d", t=2), ALU.add)\
        .then_inc(*sig.up("done", lane))


def zT_tensor(k, pe, sig, lane, trip, buf):
    pe.wait_ge(*sig.at("z", lane, trip, 1))
    transpose_z_tensor(k, pe, sig, lane, trip, buf.z, bank(k, lane, 0)).then_inc(*sig.up("zT_ps", lane))


def zT_scalar(k, act, sig, lane, trip, buf):
    act.wait_ge(*sig.at("zT_ps", lane, trip, 1))
    k.nc.scalar.activation(buf.zT.rearrange("p c t -> p (c t)"), bank(k, lane, 0), ACT.Copy)\
        .then_inc(*sig.up("zT", lane))


def lane_buffers(k, lanes=2):
    c = Carve(k.arena, k.arena_size)
    bufs = []
    for _ in range(lanes):
        bufs.append(Bag(z=c.take(2, D), zT=c.take(KC, SEQ), st=c.take(22)))
    return c, bufs


def cross_qkv_tensor(k, pe, sig, lane, trip, a, buf, stage, n=""):
    pe.wait_ge(*sig.at("zT" + n.replace("1", ""), lane, trip, 1))
    pe.wait_ge(*sig.at("ctx", lane, trip, 1))
    wq, wk, wv = (w_of(k, stage, w + n, KC) for w in ("wq", "wk", "wv"))
    for c in range(HC):
        proj_feature(k, bank(k, lane, c // 2)[:, c % 2 * SEQ:(c % 2 + 1) * SEQ], wq, buf.zT, c * P, P)
    for c in range(HC):
        proj_feature(k, bank(k, lane, 2)[:, c * P:c * P + CTX], wk, buf.ctxT, c * P, P)
    products(k, bank(k, lane, 3)[0:CTX, 0:H * VW], [(buf.ctxT[:, c, :], wv[:, c, :]) for c in range(KC)],
             row_of(k, stage, "bv" + n)).then_inc(*sig.up(a.p + "qkv_ps", lane))


def q_scalar(k, act, sig, lane, trip, a, buf, bq):
    act.wait_ge(*sig.at(a.p + "qkv_ps", lane, trip, 1))
    for c in range(HC):
        ins = k.nc.scalar.activation(buf.qT[:, c, :], bank(k, lane, c // 2)[:, c % 2 * SEQ:(c % 2 + 1) * SEQ],
                                     ACT.Identity, bias=col_of(k, bq, c))
    ins.then_inc(*sig.up(a.p + "q", lane))


def cross_kv_vector(k, dve, sig, lane, trip, a, buf, bk):
    v = k.nc.vector
    dve.wait_ge(*sig.at(a.p + "qkv_ps", lane, trip, 1))
    for c in range(HC):
        v.tensor_scalar(buf.kT[:, c, 0:CTX], bank(k, lane, 2)[:, c * P:c * P + CTX], col_of(k, bk, c), None, ALU.add)
    v.tensor_copy(buf.v[0:CTX, 0, :], bank(k, lane, 3)[0:CTX, 0:H * VW]).then_inc(*sig.up(a.p + "kv", lane))


def qkv_wait_tensor(k, pe, sig, lane, trip, a):
    pe.wait_ge(*sig.at(a.p + "q", lane, trip, 1))
    pe.wait_ge(*sig.at(a.p + "kv", lane, trip, 1))


def context_gpsimd(k, pool, sig, lane, trip, buf):
    pool.wait_ge(*sig.at("done", lane, trip, 0))
    hold(k, pool, "gpsimd")
    k.nc.gpsimd.tensor_copy(buf.ctxT, k.ctxT[:, :, bass.ts(trip * 2 + lane, CTX)]).then_inc(*sig.up("ctx", lane))


def xattn_plan(k, stage, topk):
    a = attention("cross", topk=topk)
    c, bufs = lane_buffers(k)
    for buf in bufs:
        buf.ctxT = c.take(KC, CTX)
        attention_buffers(c, a, buf)
    more = {"kept": 2} if topk else {}
    norms = norms_plan(k, stage)
    sig = Signals(k.signals, stage, B // 2, 2, z=1, zT_ps=1, zT=1, ctx=1, qkv_ps=1, q=1, kv=1, oT_ps=1, oT=1,
                  out_ps=1, done=1, dve_step=k.steps[stage], **attention_signals(a), **more)
    return Bag(norms=norms, a=a, bufs=bufs, sig=sig, stage=stage)


def xattn_tensor(k, pe, s):
    enter(k, pe, s.sig)
    with pe.Fori(0, s.sig.trips) as trip:
        for lane, buf in enumerate(s.bufs):
            zT_tensor(k, pe, s.sig, lane, trip, buf)
        for lane, buf in enumerate(s.bufs):
            cross_qkv_tensor(k, pe, s.sig, lane, trip, s.a, buf, s.stage)
        for lane in (0, 1):
            qkv_wait_tensor(k, pe, s.sig, lane, trip, s.a)
        attention_tensor(k, pe, s.sig, trip, s.a, s.bufs)
        for lane, buf in enumerate(s.bufs):
            oT_tensor(k, pe, s.sig, lane, trip, s.a, buf)
        for lane, buf in enumerate(s.bufs):
            out_tensor(k, pe, s.sig, lane, trip, s.a, buf, w_of(k, s.stage, "wo", KC), row_of(k, s.stage, "bo"))


def xattn_scalar(k, act, s):
    enter(k, act, s.sig)
    with act.Fori(0, s.sig.trips) as trip:
        for lane, buf in enumerate(s.bufs):
            zT_scalar(k, act, s.sig, lane, trip, buf)
        for lane, buf in enumerate(s.bufs):
            q_scalar(k, act, s.sig, lane, trip, s.a, buf, s.stage + "_bq")
        attention_scalar(k, act, s.sig, trip, s.a, s.bufs)
        for lane, buf in enumerate(s.bufs):
            oT_scalar(k, act, s.sig, lane, trip, s.a, buf)


def xattn_vector(k, dve, s):
    enter(k, dve, s.sig)
    norms_vector(k, dve, s.norms)
    with dve.Fori(0, s.sig.trips) as trip:
        chains = [Chain(dve, s.sig, lane, trip) for lane in (0, 1)]
        for lane, buf in enumerate(s.bufs):
            ln_vector(k, dve, s.sig, lane, trip, buf)
        for lane, buf in enumerate(s.bufs):
            cross_kv_vector(k, dve, s.sig, lane, trip, s.a, buf, s.stage + "_bk")
        attention_vector(k, dve, s.sig, trip, chains, s.a, s.bufs)
        for lane, buf in enumerate(s.bufs):
            residual_vector(k, dve, s.sig, lane, trip)
        for ch in chains:
            ch.close()


def xattn_gpsimd(k, pool, s):
    enter(k, pool, s.sig)
    with pool.Fori(0, s.sig.trips) as trip:
        for lane, buf in enumerate(s.bufs):
            context_gpsimd(k, pool, s.sig, lane, trip, buf)



def memory_plan(k):
    c = Carve(k.arena, k.arena_size)
    buf = Bag(
        zT_all=c.take(KC, B * SEQ + MEM), z_all=c.take((TILES + 1) * D), swa_all=c.take((TILES + 1) * D),
        kT_mem=c.take(KC, MEM), v_mem=c.take(SH * SVW), dw1=c.take(KC, HID), dw2=c.take(HID // P, D),
        db1=c.take(HID // P), db2=c.take(D), keep=c.take(1))
    start = c.at
    buf.z, buf.zT, buf.st = c.take(2, D), c.take(KC, SEQ), c.take(22)
    buf.qT, buf.kT, buf.v = c.take(KC, SEQ), c.take(KC, SEQ), c.take(2, SH * SVW)
    buf.s, buf.probT, buf.o, buf.oT, buf.m = c.take(4, SEQ), c.take(2, 512), c.take(D), c.take(KC, P), c.take(8)
    c.at = start
    grad = Bag(zT=c.take(KC, P), z=c.take(D), sg=c.take(HID), a=c.take(HID), g=c.take(HID),
                           aT=c.take(HID // P, P), e=c.take(D), eT=c.take(KC, P))
    c.at = start
    mem = Bag(zT=c.take(KC, SEQ), swa=c.take(2, D), swaT=c.take(KC, SEQ), aT=c.take(HID // P, SEQ),
                          om=c.take(2, D), omT=c.take(KC, SEQ), g1=c.take(2, D), g2=c.take(2, D))
    buf.grad, buf.mem = grad, mem
    window = dict(z=1, zT_ps=1, zT=1, z_kept=1, qkv_ps=1, q=1, kv=1, s_ps=2, s_sb=2, prob=2, probT_ps=2, probT_a=2,
                  o_ps=2, o=2, oT_ps=2, oT=2, out_ps=2, swa=2, done=1)
    gradient = dict(tok=1, h_ps=1, sg=1, a=1, aT_ps=1, aT=1, pred_ps=1, e=1, eT_ps=1, eT=1, da_ps=1, dh=1, dw2_ps=1, dw2=1,
                    dw1_ps=1, db_ps=1, done=1)
    n = k.steps
    first = dict(window)
    for name in ("s_ps", "s_sb", "prob", "probT_ps", "probT_a", "o_ps", "o", "oT_ps", "oT", "out_ps", "swa"):
        first[name] = 1
    for name in ("z", "z_kept", "zT_ps", "zT"):
        del first[name]
    sig = lambda trips, **per: Signals(k.signals, "L0_attn", trips, 1, **per)
    norms = norms_plan(k, "L0_attn")
    return Bag(
        buf=buf, norms=norms, first=Signals(k.signals, "L0_attn", 1, 2, done=1),
        window_mem=sig(1, dve_step=n["window_mem"], **first), window=sig(B, dve_step=n["window"], **window),
        grad_mem=sig(1, dve_step=n["grad_mem"], **gradient), grad=sig(TILES, dve_step=n["grad"], **gradient),
        update=sig(1, dve_step=n["update"], done=1),
        memory=sig(B, dve_step=n["memory"], tok=1, h_ps=4, sg=4, aT=4, om_ps=1, om=1, omT_ps=1, omT=1, gate_ps=1,
                   gate=1, done=1))


class WindowTile:

    def __init__(self, k, buf, t):
        self.t = t
        if t == "mem":
            self.rows, self.mask, self.q = MEM, "swam", slice(0, MEM)
            self.keys = [(buf.kT_mem, slice(0, MEM), MEM, buf.v_mem)]
        elif t == 0:
            self.rows, self.mask, self.q = P, "swa0", slice(0, P)
            self.keys = [(buf.kT_mem, slice(0, MEM), MEM, buf.v_mem), (buf.kT, slice(0, P), P, buf.v[:, 0, :])]
        else:
            self.rows, self.mask, self.q = P, "swa1", slice(P, SEQ)
            self.keys = [(buf.kT, slice(0, P), P, buf.v[:, 0, :]), (buf.kT, slice(P, SEQ), P, buf.v[:, 1, :])]
        self.nk = sum(n for _, _, n, _ in self.keys)


def window_scores_view(k, buf, w):
    s_ps = k.ps[0:w.rows, 5:7, :].rearrange("p b (c f) -> p (b c) f", c=2)[:, :, 0:w.nk]
    return s_ps, buf.s[0:w.rows, :, 0:w.nk]


def window_tensor(k, pe, sig, buf, trip, mem=False):
    mm, tr = k.nc.tensor.matmul, k.nc.tensor.transpose
    wq, wk, wv = (w_of(k, "L0_attn", n, KC) for n in ("wq", "wk", "wv"))
    n = MEM if mem else SEQ
    if mem:
        zT = buf.zT_all[:, :, B * SEQ:B * SEQ + MEM]
    else:
        zT = buf.zT
        pe.wait_ge(*sig.at("z", 0, trip, 1))
        transpose_z_tensor(k, pe, sig, 0, trip, buf.z, k.ps[:, 0, :]).then_inc(*sig.up("zT_ps"))
        pe.wait_ge(*sig.at("zT", 0, trip, 1))
    for c in range(KC):
        proj_feature(k, k.ps[:, 1, c * SEQ:c * SEQ + n], wq, zT, c * P, P)
        proj_feature(k, k.ps[:, 2, c * SEQ:c * SEQ + n], wk, zT, c * P, P)
    for t in range(1 if mem else 2):
        ins = products(k, k.ps[0:min(n, P), 3 + t, 0:SH * SVW],
                       [(zT[:, c, t * P:t * P + min(n, P)], wv[:, c, :]) for c in range(KC)],
                       row_of(k, "L0_attn", "v1"))
    ins.then_inc(*sig.up("qkv_ps"))
    pe.wait_ge(*sig.at("q", 0, trip, 1))
    pe.wait_ge(*sig.at("kv", 0, trip, 1))
    for r, w in enumerate(window_tiles(k, buf, mem)):
        if r:
            pe.wait_ge(*sig.at("swa", 0, trip, r))
        mask = mask_of(k, w.mask)
        for i in (0, 1):
            mm(k.ps[0:w.rows, 5 + i, :].rearrange("p (c f) -> p c f", c=2)[:, :, 0:w.nk], k.identb[:, 0:w.rows],
               mask.rearrange("p (c f) -> p c f", c=2), start=True, stop=False, skip_group_check=True)
        for c in (0, 1):
            for i in (0, 1):
                at = c * SEQ
                half = slice(SD_ * i, SD_ * (i + 1))
                for kT, cols, nk, _ in w.keys:
                    ins = mm(k.ps[0:w.rows, 5 + i, at:at + nk], buf.qT[half, c, w.q], kT[half, c, cols],
                             start=False, stop=True, skip_group_check=True)
                    at += nk
        ins.then_inc(*sig.up("s_ps"))
        pe.wait_ge(*sig.at("prob", 0, trip, r + 1))
        hold(k, pe, "tensor")
        for c in (0, 1):
            for i in (0, 1):
                at = 0
                for kb, (_, _, nk, _) in enumerate(w.keys):
                    s = 2 * c + kb
                    ins = tr(k.ps[0:nk, 1 + i, s * P:s * P + w.rows], buf.s[0:w.rows, 2 * i + c, at:at + nk],
                             k.ident[0:w.rows, 0:w.rows])
                    at += nk
        ins.then_inc(*sig.up("probT_ps"))
        pe.wait_ge(*sig.at("probT_a", 0, trip, r + 1))
        for c in (0, 1):
            for i in (0, 1):
                h = 2 * c + i
                for kb, (_, _, nk, v) in enumerate(w.keys):
                    s = 2 * c + kb
                    ins = mm(k.ps[0:w.rows, 7, h * SVW:(h + 1) * SVW], buf.probT[0:nk, i, s * P:s * P + w.rows],
                             v[0:nk, h * SVW:(h + 1) * SVW], start=kb == 0, stop=kb == len(w.keys) - 1)
        ins.then_inc(*sig.up("o_ps"))
        pe.wait_ge(*sig.at("o", 0, trip, r + 1))
        for c in range(KC):
            ins = tr(k.ps[:, 3, c * P:c * P + w.rows], buf.o[0:w.rows, c * P:(c + 1) * P],
                     k.ident[0:w.rows, 0:w.rows])
        ins.then_inc(*sig.up("oT_ps"))
        pe.wait_ge(*sig.at("oT", 0, trip, r + 1))
        products(k, k.ps[0:w.rows, 4, 0:D],
                 [(buf.oT[:, c, 0:w.rows], w_of(k, "L0_attn", "wo", KC)[:, c, :]) for c in range(KC)])\
            .then_inc(*sig.up("out_ps"))


def window_tiles(k, buf, mem):
    return [WindowTile(k, buf, "mem")] if mem else [WindowTile(k, buf, 0), WindowTile(k, buf, 1)]


def window_scalar(k, act, sig, buf, trip, mem=False):
    n = MEM if mem else SEQ
    if not mem:
        act.wait_ge(*sig.at("zT_ps", 0, trip, 1))
        k.nc.scalar.activation(buf.zT.rearrange("p c t -> p (c t)"), k.ps[:, 0, :], ACT.Copy).then_inc(*sig.up("zT"))
    act.wait_ge(*sig.at("qkv_ps", 0, trip, 1))
    for c in range(KC):
        ins = k.nc.scalar.activation(buf.qT[:, c, 0:n], k.ps[:, 1, c * SEQ:c * SEQ + n], ACT.Copy)
    ins.then_inc(*sig.up("q"))
    for r, w in enumerate(window_tiles(k, buf, mem)):
        _, s_sb = window_scores_view(k, buf, w)
        act.wait_ge(*sig.at("s_sb", 0, trip, r + 1))
        k.nc.scalar.activation(s_sb, s_sb, ACT.Exp, scale=SD_ ** -0.5).then_inc(*sig.up("prob"))
        act.wait_ge(*sig.at("probT_ps", 0, trip, r + 1))
        for kb, (_, _, nk, _) in enumerate(w.keys):
            sel = lambda ap: ap.rearrange("p b (c kb q) -> p (b c) kb q", c=2, kb=2)[0:nk, :, kb, 0:w.rows]
            ins = k.nc.scalar.activation(sel(buf.probT), sel(k.ps[:, 1:3, :]), ACT.Copy)
        ins.then_inc(*sig.up("probT_a"))
        act.wait_ge(*sig.at("oT_ps", 0, trip, r + 1))
        k.nc.scalar.activation(buf.oT[:, :, 0:w.rows],
                               k.ps[:, 3, 0:KC * P].rearrange("p (c q) -> p c q", c=KC)[:, :, 0:w.rows],
                               ACT.Copy).then_inc(*sig.up("oT"))


def window_vector(k, dve, sig, buf, trip, mem=False):
    v = k.nc.vector
    ch = Chain(dve, sig, 0, trip)
    n = MEM if mem else SEQ
    if not mem:
        dve.wait_ge(*sig.at("done", 0, trip, 0))
        hold(k, dve, "vector")
        ln_apply(k, trip, 0, 1, buf.z).then_inc(*sig.up("z"))
    dve.wait_ge(*sig.at("qkv_ps", 0, trip, 1))
    kT, vv = (buf.kT_mem, buf.v_mem.unsqueeze(1)) if mem else (buf.kT, buf.v)
    rows, nt = (MEM, 1) if mem else (P, 2)
    v.tensor_copy(kT[:, :, 0:n], k.ps[:, 2, :].rearrange("p (c q) -> p c q", c=KC)[:, :, 0:n])
    v.tensor_copy(vv[0:rows, 0:nt, :], k.ps[0:rows, 3:3 + nt, 0:SH * SVW]).then_inc(*sig.up("kv"))
    for r, w in enumerate(window_tiles(k, buf, mem)):
        s_ps, s_sb = window_scores_view(k, buf, w)
        m, rec = buf.m[0:w.rows, 0:SH], buf.m[0:w.rows, SH:2 * SH]
        dve.wait_ge(*sig.at("s_ps", 0, trip, r + 1))
        ch.link(v.tensor_reduce(m, s_ps, AX, ALU.max))
        v.tensor_tensor(s_sb, s_ps, m.unsqueeze(2).broadcast_to([w.rows, SH, w.nk]), ALU.subtract)\
            .then_inc(*sig.up("s_sb"))
        dve.wait_ge(*sig.at("o_ps", 0, trip, r + 1))
        o_ps = k.ps[0:w.rows, 7, 0:SH * SVW].rearrange("p (h e) -> p h e", h=SH)
        ch.link(v.reciprocal(rec.unsqueeze(2), o_ps[:, :, SD_:SVW]))
        v.tensor_tensor(buf.o[0:w.rows, :].rearrange("p (h e) -> p h e", h=SH), o_ps[:, :, 0:SD_],
                        rec.unsqueeze(2).broadcast_to([w.rows, SH, SD_]), ALU.mult).then_inc(*sig.up("o"))
        dve.wait_ge(*sig.at("out_ps", 0, trip, r + 1))
        hold(k, dve, "vector")
        if mem:
            ins = v.tensor_copy(buf.swa_all[0:w.rows, TILES * D:], k.ps[0:w.rows, 4, 0:D])
        else:
            ins = v.tensor_copy(buf.swa_all[:, bass.ds((trip * 2 + r) * D, D)], k.ps[:, 4, 0:D])
        ins.then_inc(*sig.up("swa"))
    if not mem:
        dve.wait_ge(*sig.at("z_kept", 0, trip, 1))
    dve.wait_ge(*sig.at("swa", 0, trip, 1 if mem else 2))
    v.memset(buf.keep, 0.0).then_inc(*sig.up("done"))
    ch.close()


def window_gpsimd(k, pool, sig, buf, trip):
    pool.wait_ge(*sig.at("zT", 0, trip, 1))
    hold(k, pool, "gpsimd")
    k.nc.gpsimd.tensor_copy(buf.z_all[:, bass.ts(trip, 2 * D)], buf.z.rearrange("p t d -> p (t d)"))
    k.nc.gpsimd.tensor_copy(buf.zT_all[:, :, bass.ts(trip, SEQ)], buf.zT).then_inc(*sig.up("z_kept"))


def grad_tensor(k, pe, sig, buf, trip, rows):
    mm, tr, g = k.nc.tensor.matmul, k.nc.tensor.transpose, buf.grad
    w = lambda n, r: w_of(k, "L0_attn", n, r)
    pe.wait_ge(*sig.at("tok", 0, trip, 1))
    for i in (0, 1):
        ins = products(k, k.ps[0:rows, i, :], [(g.zT[:, c, 0:rows], w("w1T", KC)[:, c, i * 512:(i + 1) * 512])
                                               for c in range(KC)],
                       row_of(k, "L0_attn", "b1")[:, i * 512:(i + 1) * 512])
    ins.then_inc(*sig.up("h_ps"))
    pe.wait_ge(*sig.at("a", 0, trip, 1))
    for c in range(HID // P):
        ins = tr(k.ps[:, 2 + c // 4, c % 4 * P:c % 4 * P + rows], g.a[0:rows, c * P:(c + 1) * P],
                 k.ident[0:rows, 0:rows])
    ins.then_inc(*sig.up("aT_ps"))
    pe.wait_ge(*sig.at("aT", 0, trip, 1))
    products(k, k.ps[0:rows, 4, 0:D], [(g.aT[:, c, 0:rows], w("w2T", HID // P)[:, c, :]) for c in range(HID // P)],
             row_of(k, "L0_attn", "b2")).then_inc(*sig.up("pred_ps"))
    pe.wait_ge(*sig.at("e", 0, trip, 1))
    for c in range(KC):
        ins = tr(k.ps[:, 5, c * P:c * P + rows], g.e[0:rows, c * P:(c + 1) * P], k.ident[0:rows, 0:rows])
    ins.then_inc(*sig.up("eT_ps"))
    pe.wait_ge(*sig.at("eT", 0, trip, 1))
    for i in (0, 1):
        ins = products(k, k.ps[0:rows, 6 + i, :], [(g.eT[:, c, 0:rows], w("w2", KC)[:, c, i * 512:(i + 1) * 512])
                                                   for c in range(KC)])
    ins.then_inc(*sig.up("da_ps"))
    for c in range(HID // P):
        ins = mm(k.ps[:, c // 2, c % 2 * D:(c % 2 + 1) * D], g.a[0:rows, c * P:(c + 1) * P], g.e[0:rows, :])
    ins.then_inc(*sig.up("dw2_ps"))
    pe.wait_ge(*sig.at("dh", 0, trip, 1))
    for c in range(KC):
        for i in (0, 1):
            ins = mm(k.ps[:, 4 + 2 * c + i, :], g.z[0:rows, c * P:(c + 1) * P], g.g[0:rows, i * 512:(i + 1) * 512])
    ins.then_inc(*sig.up("dw1_ps"))
    pe.wait_ge(*sig.at("dw2", 0, trip, 1))
    for c in range(HID // P):
        mm(k.ps[:, 0, c:c + 1], g.g[0:rows, c * P:(c + 1) * P], col_of(k, "one", 0, rows))
    mm(k.ps[0:1, 1, 0:D], col_of(k, "one", 0, rows), g.e[0:rows, :]).then_inc(*sig.up("db_ps"))


def grad_scalar(k, act, sig, buf, trip, rows):
    g, a = buf.grad, k.nc.scalar.activation
    act.wait_ge(*sig.at("h_ps", 0, trip, 1))
    a(g.sg[0:rows, :], k.ps[0:rows, 0:2, :].rearrange("p b f -> p (b f)"), ACT.Sigmoid).then_inc(*sig.up("sg"))
    act.wait_ge(*sig.at("aT_ps", 0, trip, 1))
    a(g.aT[:, :, 0:rows], k.ps[:, 2:4, :].rearrange("p b (c q) -> p (b c) q", c=4)[:, :, 0:rows], ACT.Copy)\
        .then_inc(*sig.up("aT"))
    act.wait_ge(*sig.at("eT_ps", 0, trip, 1))
    a(g.eT[:, :, 0:rows], k.ps[:, 5, 0:KC * P].rearrange("p (c q) -> p c q", c=KC)[:, :, 0:rows], ACT.Copy)\
        .then_inc(*sig.up("eT"))


def grad_vector(k, dve, sig, buf, trip, rows, mem=False):
    v, g = k.nc.vector, buf.grad
    ch = Chain(dve, sig, 0, trip)
    sg, a, dg, e = g.sg[0:rows, :], g.a[0:rows, :], g.g[0:rows, :], g.e[0:rows, :]
    dve.wait_ge(*sig.at("sg", 0, trip, 1))
    v.tensor_tensor(a, k.ps[0:rows, 0:2, :].rearrange("p b f -> p (b f)"), sg, ALU.mult).then_inc(*sig.up("a"))
    dve.wait_ge(*sig.at("a", 0, trip, 1))
    ch.link(v.tensor_tensor(dg, a, sg, ALU.mult))
    ch.link(v.tensor_tensor(dg, a, dg, ALU.subtract))
    ch.link(v.tensor_tensor(dg, dg, sg, ALU.add))
    dve.wait_ge(*sig.at("pred_ps", 0, trip, 1))
    if mem:
        ch.link(v.tensor_tensor(e, k.ps[0:rows, 4, 0:D], buf.swa_all[0:rows, TILES * D:], ALU.subtract))
        v.tensor_scalar(e, e, float(B), None, ALU.mult).then_inc(*sig.up("e"))
    else:
        v.tensor_tensor(e, k.ps[:, 4, 0:D], buf.swa_all[:, bass.ts(trip, D)], ALU.subtract).then_inc(*sig.up("e"))
    dve.wait_ge(*sig.at("da_ps", 0, trip, 1))
    v.tensor_tensor(dg, k.ps[0:rows, 6:8, :].rearrange("p b f -> p (b f)"), dg, ALU.mult).then_inc(*sig.up("dh"))
    dw2 = buf.dw2.rearrange("p c d -> p (c d)")
    dw1 = buf.dw1.rearrange("p c n -> p (c n)")

    def add(sum_, part):
        return v.tensor_copy(sum_, part) if mem else v.tensor_tensor(sum_, sum_, part, ALU.add)

    dve.wait_ge(*sig.at("dw2_ps", 0, trip, 1))
    add(dw2, k.ps[:, 0:4, :].rearrange("p b f -> p (b f)")).then_inc(*sig.up("dw2"))
    dve.wait_ge(*sig.at("dw1_ps", 0, trip, 1))
    add(dw1, k.ps[:, 4:8, :].rearrange("p b f -> p (b f)"))
    dve.wait_ge(*sig.at("db_ps", 0, trip, 1))
    add(buf.db1, k.ps[:, 0, 0:HID // P])
    add(buf.db2[0:1, :], k.ps[0:1, 1, 0:D]).then_inc(*sig.up("done"))
    ch.close()


def grad_gpsimd(k, pool, sig, buf, trip, rows, mem=False):
    g, copy = buf.grad, k.nc.gpsimd.tensor_copy
    pool.wait_ge(*sig.at("done", 0, trip, 0))
    hold(k, pool, "gpsimd")
    if mem:
        copy(g.zT[:, :, 0:rows], buf.zT_all[:, :, B * SEQ:B * SEQ + MEM])
        copy(g.z[0:rows, :], buf.z_all[0:rows, TILES * D:]).then_inc(*sig.up("tok"))
    else:
        copy(g.zT, buf.zT_all[:, :, bass.ts(trip, P)])
        copy(g.z, buf.z_all[:, bass.ts(trip, D)]).then_inc(*sig.up("tok"))


def update_vector(k, dve, sig, buf):
    v = k.nc.vector
    ch = Chain(dve, sig, 0, 0)
    enter(k, dve, sig)
    keep, theta = buf.keep, scalar_of(k, "theta")
    ch.link(v.tensor_scalar(keep, scalar_of(k, "alpha"), -1.0, 1.0, ALU.mult, ALU.add))
    at, n = k.colpos["L0_attn_b1"]
    pairs = [(buf.dw1.rearrange("p c n -> p (c n)"), w_of(k, "L0_attn", "w1T")),
             (buf.dw2.rearrange("p c n -> p (c n)"), w_of(k, "L0_attn", "w2T")), (buf.db1, k.cols[:, at:at + n]),
             (buf.db2[0:1, :], row_of(k, "L0_attn", "b2"))]
    for grad, p in pairs:
        parts = grad.shape[0]
        ins = v.tensor_scalar(grad, grad, theta[0:parts], None, ALU.mult)
    ch.link(ins)
    for grad, p in pairs:
        parts = grad.shape[0]
        ins = v.scalar_tensor_tensor(grad, p, keep[0:parts], grad, ALU.mult, ALU.subtract)
    ins.then_inc(*sig.up("done"))
    ch.close()


def memory_tensor(k, pe, sig, buf, trip):
    m, tr = buf.mem, k.nc.tensor.transpose
    pe.wait_ge(*sig.at("tok", 0, trip, 1))
    for i in range(4):
        for c in (2 * i, 2 * i + 1):
            ins = proj_feature(k, k.ps[:, i, c % 2 * SEQ:(c % 2 + 1) * SEQ], buf.dw1, m.zT, c * P, P)
        ins.then_inc(*sig.up("h_ps"))
    for t in (0, 1):
        for c in range(KC):
            tr(k.ps[:, 5, (2 * c + t) * P:(2 * c + t + 1) * P], m.swa[:, t, c * P:(c + 1) * P], k.ident[:, :])
    pe.wait_ge(*sig.at("aT", 0, trip, 4))
    for t in (0, 1):
        ins = proj_token(k, k.ps[:, 4, t * D:(t + 1) * D], m.aT, t * P, buf.dw2, buf.db2[0:1, :], HID // P)
    ins.then_inc(*sig.up("om_ps"))
    pe.wait_ge(*sig.at("om", 0, trip, 1))
    transpose_z_tensor(k, pe, sig, 0, trip, m.om, k.ps[:, 0, :]).then_inc(*sig.up("omT_ps"))
    pe.wait_ge(*sig.at("omT", 0, trip, 1))
    for t in (0, 1):
        proj_token(k, k.ps[:, 6, t * D:(t + 1) * D], m.swaT, t * P, w_of(k, "L0_attn", "lin1", KC))
        ins = proj_token(k, k.ps[:, 7, t * D:(t + 1) * D], m.omT, t * P, w_of(k, "L0_attn", "lin2", KC))
    ins.then_inc(*sig.up("gate_ps"))


def memory_scalar(k, act, sig, buf, trip):
    m, a = buf.mem, k.nc.scalar.activation
    flat = lambda ap: ap.rearrange("p c t -> p (c t)")
    for i in range(4):
        act.wait_ge(*sig.at("h_ps", 0, trip, i + 1))
        for c in (2 * i, 2 * i + 1):
            ins = a(m.aT[:, c, :], k.ps[:, i, c % 2 * SEQ:(c % 2 + 1) * SEQ], ACT.Sigmoid, bias=buf.db1[:, c:c + 1])
        ins.then_inc(*sig.up("sg"))
    act.wait_ge(*sig.at("om_ps", 0, trip, 1))
    a(flat(m.swaT), k.ps[:, 5, :], ACT.Copy)
    a(flat(m.om), k.ps[:, 4, :], ACT.Copy).then_inc(*sig.up("om"))
    act.wait_ge(*sig.at("omT_ps", 0, trip, 1))
    a(flat(m.omT), k.ps[:, 0, :], ACT.Copy).then_inc(*sig.up("omT"))
    act.wait_ge(*sig.at("gate_ps", 0, trip, 1))
    a(flat(m.g1), k.ps[:, 6, :], ACT.Sigmoid)
    a(flat(m.g2), k.ps[:, 7, :], ACT.Sigmoid).then_inc(*sig.up("gate"))


def memory_vector(k, dve, sig, buf, trip):
    v, m = k.nc.vector, buf.mem
    ch = Chain(dve, sig, 0, trip)
    for i in range(4):
        dve.wait_ge(*sig.at("sg", 0, trip, i + 1))
        for c in (2 * i, 2 * i + 1):
            ins = v.scalar_tensor_tensor(m.aT[:, c, :], k.ps[:, i, c % 2 * SEQ:(c % 2 + 1) * SEQ],
                                         buf.db1[:, c:c + 1], m.aT[:, c, :], ALU.add, ALU.mult)
        ins.then_inc(*sig.up("aT"))
    dve.wait_ge(*sig.at("gate", 0, trip, 1))
    v.tensor_tensor(m.g1, m.g1, m.swa, ALU.mult)
    ch.link(v.tensor_tensor(m.g2, m.g2, m.om, ALU.mult))
    ch.link(v.tensor_tensor(m.g1, m.g1, m.g2, ALU.add))
    x = x_of(k, trip, 0, 1)
    v.tensor_tensor(x, x, m.g1, ALU.add).then_inc(*sig.up("done"))
    ch.close()


def memory_gpsimd(k, pool, sig, buf, trip):
    m, copy = buf.mem, k.nc.gpsimd.tensor_copy
    pool.wait_ge(*sig.at("done", 0, trip, 0))
    hold(k, pool, "gpsimd")
    copy(m.zT, buf.zT_all[:, :, bass.ts(trip, SEQ)])
    copy(m.swa.rearrange("p t d -> p (t d)"), buf.swa_all[:, bass.ts(trip, 2 * D)]).then_inc(*sig.up("tok"))


def L0_attn_tensor(k, pe, s):
    enter(k, pe, s.window_mem)
    pe.wait_ge(k.mem_loaded, 32)
    window_tensor(k, pe, s.window_mem, s.buf, 0, mem=True)
    enter(k, pe, s.window)
    with pe.Fori(0, B) as trip:
        window_tensor(k, pe, s.window, s.buf, trip)
    enter(k, pe, s.grad_mem)
    grad_tensor(k, pe, s.grad_mem, s.buf, 0, MEM)
    enter(k, pe, s.grad)
    with pe.Fori(0, TILES) as trip:
        grad_tensor(k, pe, s.grad, s.buf, trip, P)
    enter(k, pe, s.memory)
    with pe.Fori(0, B) as trip:
        memory_tensor(k, pe, s.memory, s.buf, trip)


def L0_attn_scalar(k, act, s):
    enter(k, act, s.window_mem)
    window_scalar(k, act, s.window_mem, s.buf, 0, mem=True)
    enter(k, act, s.window)
    with act.Fori(0, B) as trip:
        window_scalar(k, act, s.window, s.buf, trip)
    enter(k, act, s.grad_mem)
    grad_scalar(k, act, s.grad_mem, s.buf, 0, MEM)
    enter(k, act, s.grad)
    with act.Fori(0, TILES) as trip:
        grad_scalar(k, act, s.grad, s.buf, trip, P)
    enter(k, act, s.memory)
    with act.Fori(0, B) as trip:
        memory_scalar(k, act, s.memory, s.buf, trip)


def L0_attn_vector(k, dve, s):
    for lane in (0, 1):
        dve.sem_inc(s.first.sems["done"][lane], 1)
    enter(k, dve, s.window_mem)
    norms_vector(k, dve, s.norms)
    window_vector(k, dve, s.window_mem, s.buf, 0, mem=True)
    enter(k, dve, s.window)
    with dve.Fori(0, B) as trip:
        window_vector(k, dve, s.window, s.buf, trip)
    enter(k, dve, s.grad_mem)
    grad_vector(k, dve, s.grad_mem, s.buf, 0, MEM, mem=True)
    enter(k, dve, s.grad)
    with dve.Fori(0, TILES) as trip:
        grad_vector(k, dve, s.grad, s.buf, trip, P)
    update_vector(k, dve, s.update, s.buf)
    enter(k, dve, s.memory)
    with dve.Fori(0, B) as trip:
        memory_vector(k, dve, s.memory, s.buf, trip)


def L0_attn_gpsimd(k, pool, s):
    enter(k, pool, s.window)
    with pool.Fori(0, B) as trip:
        window_gpsimd(k, pool, s.window, s.buf, trip)
    enter(k, pool, s.grad_mem)
    grad_gpsimd(k, pool, s.grad_mem, s.buf, 0, MEM, mem=True)
    enter(k, pool, s.grad)
    with pool.Fori(0, TILES) as trip:
        grad_gpsimd(k, pool, s.grad, s.buf, trip, P)
    enter(k, pool, s.memory)
    with pool.Fori(0, B) as trip:
        memory_gpsimd(k, pool, s.memory, s.buf, trip)


def experts_plan(k):
    c, bufs = lane_buffers(k)
    for buf in bufs:
        buf.l, buf.gate, buf.m, buf.rank = c.take(2, 8), c.take(2, 8), c.take(4), c.take(2, 8)
        buf.gt, buf.eq = c.take(128), c.take(128)
        buf.th, buf.aT = c.take(2, SEQ), c.take(2, SEQ)
    norms = norms_plan(k, "L0_ffn")
    sig = Signals(k.signals, "L0_ffn", B // 2, 2, z=1, zT_ps=1, zT=1, router_ps=1, logit=1, gate=1, h_ps=E_ALL,
                  th=E_ALL, aT=E_ALL, out_ps=E_ROUTED + 1, added=E_ROUTED, done=1, dve_step=k.steps["L0_ffn"])
    return Bag(bufs=bufs, norms=norms, sig=sig)


def experts_up_tensor(k, pe, sig, lane, trip, buf, e):
    w1, w3 = (w_of(k, "L0_ffn", n, E_ALL * KC) for n in ("w1", "w3"))
    if e >= 2:
        pe.wait_ge(*sig.at("aT", lane, trip, e - 1))
    for i, w in enumerate((w1, w3)):
        ins = products(k, bank(k, lane, e % 2)[:, i * SEQ:(i + 1) * SEQ],
                       [(w[:, e * KC + c, :], buf.zT[:, c, :]) for c in range(KC)])
    ins.then_inc(*sig.up("h_ps", lane))


def experts_down_tensor(k, pe, sig, lane, trip, buf, e):
    w2 = w_of(k, "L0_ffn", "w2", E_ALL)
    shared = e >= E_ROUTED
    out = bank(k, lane, 2 + e % 2 if not shared else 2)
    pe.wait_ge(*sig.at("aT", lane, trip, e + 1))
    if e == 1:
        pe.wait_ge(*sig.at("logit", lane, trip, 1))
    if 2 <= e <= E_ROUTED:
        pe.wait_ge(*sig.at("added", lane, trip, e - 1))
    for t in (0, 1):
        ins = k.nc.tensor.matmul(out[:, t * D:(t + 1) * D], buf.aT[:, e % 2, t * P:(t + 1) * P], w2[:, e, :],
                                 start=not shared or (e == E_ROUTED and t == 0), stop=not shared or e == E_ALL - 1,
                                 skip_group_check=shared)
    if e != E_ROUTED:
        ins.then_inc(*sig.up("out_ps", lane))


def L0_ffn_tensor(k, pe, s):
    enter(k, pe, s.sig)
    with pe.Fori(0, s.sig.trips) as trip:
        for lane, buf in enumerate(s.bufs):
            zT_tensor(k, pe, s.sig, lane, trip, buf)
        for lane, buf in enumerate(s.bufs):
            pe.wait_ge(*s.sig.at("zT", lane, trip, 1))
            for t in (0, 1):
                ins = proj_token(k, bank(k, lane, 3)[:, t * 8:(t + 1) * 8], buf.zT, t * P,
                                 w_of(k, "L0_ffn", "router", KC), row_of(k, "L0_ffn", "rb"))
            ins.then_inc(*s.sig.up("router_ps", lane))
        for e in range(E_ALL + 1):
            for lane, buf in enumerate(s.bufs):
                if e < E_ALL:
                    experts_up_tensor(k, pe, s.sig, lane, trip, buf, e)
            for lane, buf in enumerate(s.bufs):
                if e:
                    experts_down_tensor(k, pe, s.sig, lane, trip, buf, e - 1)


def L0_ffn_scalar(k, act, s):
    a = k.nc.scalar.activation
    enter(k, act, s.sig)
    with act.Fori(0, s.sig.trips) as trip:
        for lane, buf in enumerate(s.bufs):
            zT_scalar(k, act, s.sig, lane, trip, buf)
        for lane, buf in enumerate(s.bufs):
            act.wait_ge(*s.sig.at("logit", lane, trip, 1))
            a(buf.gate, buf.gate, ACT.Exp).then_inc(*s.sig.up("gate", lane))
        for e in range(E_ALL):
            for lane, buf in enumerate(s.bufs):
                act.wait_ge(*s.sig.at("h_ps", lane, trip, e + 1))
                if e >= 2:
                    act.wait_ge(*s.sig.at("aT", lane, trip, e - 1))
                a(buf.th[:, e % 2, :], bank(k, lane, e % 2)[:, 0:SEQ], ACT.Tanh, scale=0.5)\
                    .then_inc(*s.sig.up("th", lane))


def logits_vector(k, dve, sig, lane, trip, ch, buf):
    v = k.nc.vector
    dve.wait_ge(*sig.at("router_ps", lane, trip, 1))
    ch.link(v.tensor_copy(buf.l, bank(k, lane, 3)[:, 0:16].rearrange("p (t e) -> p t e", t=2)))
    ch.link(v.tensor_reduce(buf.m[:, 0:2], buf.l, AX, ALU.max))
    v.tensor_tensor(buf.gate, buf.l, buf.m[:, 0:2].unsqueeze(2).broadcast_to([P, 2, 8]), ALU.subtract)\
        .then_inc(*sig.up("logit", lane))


def gates_vector(k, dve, sig, lane, trip, ch, buf):
    v = k.nc.vector
    gt, eq = (b.rearrange("p (t e f) -> p t e f", t=2, e=8) for b in (buf.gt, buf.eq))
    for t in (0, 1):
        mine = buf.l[:, t, :].unsqueeze(2).broadcast_to([P, 8, 8])
        other = buf.l[:, t, :].unsqueeze(1).broadcast_to([P, 8, 8])
        v.tensor_tensor(gt[:, t], other, mine, ALU.is_gt)
        ins = v.tensor_tensor(eq[:, t], other, mine, ALU.is_equal)
    ch.link(ins)
    for t in (0, 1):
        ins = v.tensor_tensor(eq[:, t], eq[:, t], k.earlier.rearrange("p (e f) -> p e f", e=8), ALU.mult)
    ch.link(ins)
    ch.link(v.tensor_tensor(buf.gt, buf.gt, buf.eq, ALU.add))
    ch.link(v.tensor_reduce(buf.rank.rearrange("p t e -> p (t e)"), buf.gt.rearrange("p (a f) -> p a f", f=8), AX, ALU.add))
    dve.wait_ge(*sig.at("gate", lane, trip, 1))
    ch.link(v.scalar_tensor_tensor(buf.gate, buf.rank, 2.0, buf.gate, ALU.is_lt, ALU.mult))
    ch.link(v.tensor_reduce(buf.m[:, 0:2], buf.gate, AX, ALU.add))
    ch.link(v.reciprocal(buf.m[:, 2:4], buf.m[:, 0:2]))
    ch.link(v.tensor_tensor(buf.gate, buf.gate, buf.m[:, 2:4].unsqueeze(2).broadcast_to([P, 2, 8]), ALU.mult))


def expert_act_vector(k, dve, sig, lane, trip, ch, buf, e):
    v = k.nc.vector
    h = bank(k, lane, e % 2)
    aT = buf.aT[:, e % 2, :]
    dve.wait_ge(*sig.at("th", lane, trip, e + 1))
    if e == 2:
        dve.wait_ge(*sig.at("out_ps", lane, trip, 1))
    elif 2 < e <= 9:
        dve.wait_ge(*sig.at("out_ps", lane, trip, e - 1))
    ch.link(v.scalar_tensor_tensor(aT, buf.th[:, e % 2, :], 1.0, h[:, 0:SEQ], ALU.add, ALU.mult))
    v.scalar_tensor_tensor(aT, aT, 0.5, h[:, SEQ:2 * SEQ], ALU.mult, ALU.mult).then_inc(*sig.up("aT", lane))


def expert_add_vector(k, dve, sig, lane, trip, buf, e):
    v = k.nc.vector
    x = x_of(k, trip, lane)
    out = bank(k, lane, 2 + e % 2).rearrange("p (t d) -> p t d", t=2)
    dve.wait_ge(*sig.at("out_ps", lane, trip, e + 1))
    if e:
        dve.wait_ge(*sig.at("added", lane, trip, e))
    hold(k, dve, "vector")
    for t in (0, 1):
        ins = v.scalar_tensor_tensor(x[:, t, :], out[:, t, :], buf.gate[:, t, e:e + 1], x[:, t, :], ALU.mult, ALU.add)
    ins.then_inc(*sig.up("added", lane))


def L0_ffn_vector(k, dve, s):
    enter(k, dve, s.sig)
    norms_vector(k, dve, s.norms)
    with dve.Fori(0, s.sig.trips) as trip:
        chains = [Chain(dve, s.sig, lane, trip) for lane in (0, 1)]
        for lane, buf in enumerate(s.bufs):
            ln_vector(k, dve, s.sig, lane, trip, buf)
        for lane, buf in enumerate(s.bufs):
            logits_vector(k, dve, s.sig, lane, trip, chains[lane], buf)
        for lane, buf in enumerate(s.bufs):
            gates_vector(k, dve, s.sig, lane, trip, chains[lane], buf)
        for e in range(E_ALL + 1):
            for lane, buf in enumerate(s.bufs):
                if e < E_ALL:
                    expert_act_vector(k, dve, s.sig, lane, trip, chains[lane], buf, e)
            for lane, buf in enumerate(s.bufs):
                if 1 <= e <= E_ROUTED:
                    expert_add_vector(k, dve, s.sig, lane, trip, buf, e - 1)
        for lane in (0, 1):
            x = x_of(k, trip, lane)
            dve.wait_ge(*s.sig.at("added", lane, trip, E_ROUTED))
            dve.wait_ge(*s.sig.at("out_ps", lane, trip, E_ROUTED + 1))
            k.nc.vector.tensor_tensor(x, x, bank(k, lane, 2).rearrange("p (t d) -> p t d", t=2), ALU.add)\
                .then_inc(*s.sig.up("done", lane))
            chains[lane].close()


def self_qk_tensor(k, pe, sig, lane, trip, a, buf, stage, n=""):
    pe.wait_ge(*sig.at("zT", lane, trip, 1))
    for i, w in enumerate((w_of(k, stage, "wq" + n, KC), w_of(k, stage, "wk" + n, KC))):
        for c in range(HC):
            ins = proj_feature(k, bank(k, lane, 2 * i + c // 2)[:, c % 2 * SEQ:(c % 2 + 1) * SEQ], w, buf.zT,
                               c * P, P)
    ins.then_inc(*sig.up(a.p + "qkv_ps", lane))


def self_v_tensor(k, pe, sig, lane, trip, a, buf, stage, n=""):
    pe.wait_ge(*sig.at(a.p + "q", lane, trip, 1))
    for t in (0, 1):
        ins = proj_token(k, bank(k, lane, t)[:, 0:H * VW], buf.zT, t * P, w_of(k, stage, "wv" + n, KC),
                         row_of(k, stage, "bv" + n))
    ins.then_inc(*sig.up(a.p + "v_ps", lane))


def self_kv_vector(k, dve, sig, lane, trip, a, buf, bk):
    v = k.nc.vector
    dve.wait_ge(*sig.at(a.p + "qkv_ps", lane, trip, 1))
    for c in range(HC):
        v.tensor_scalar(buf.kT[:, c, :], bank(k, lane, 2 + c // 2)[:, c % 2 * SEQ:(c % 2 + 1) * SEQ],
                        col_of(k, bk, c), None, ALU.add)
    dve.wait_ge(*sig.at(a.p + "v_ps", lane, trip, 1))
    v.tensor_copy(buf.v, banks(k, lane, 0, 2)[:, :, 0:H * VW]).then_inc(*sig.up(a.p + "kv", lane))


def block_plan(k):
    a = attention("self")
    c, bufs = lane_buffers(k)
    for buf in bufs:
        attention_buffers(c, a, buf)
        buf.x1, buf.x1T = c.take(2, D), c.take(KC, SEQ)
        buf.f = buf.s.rearrange("p c t -> p (c t)")[:, 0:FF // P * SEQ].rearrange("p (c t) -> p c t", t=SEQ)
    norms = norms_plan(k, "L1_attn")
    sig = Signals(k.signals, "L1_attn", B // 2, 2, z=1, zT_ps=1, zT=1, qkv_ps=1, q=1, v_ps=1, kv=1, x1=1, x1T_ps=1,
                  x1T=1, f_ps=1, f=1, out_ps=1, done=1, dve_step=k.steps["L1_attn"], **attention_signals(a))
    return Bag(norms=norms, a=a, bufs=bufs, sig=sig)


def L1_attn_tensor(k, pe, s):
    sig, st = s.sig, "L1_attn"
    enter(k, pe, sig)
    with pe.Fori(0, sig.trips) as trip:
        for lane, buf in enumerate(s.bufs):
            zT_tensor(k, pe, sig, lane, trip, buf)
        for lane, buf in enumerate(s.bufs):
            self_qk_tensor(k, pe, sig, lane, trip, s.a, buf, st)
        for lane, buf in enumerate(s.bufs):
            self_v_tensor(k, pe, sig, lane, trip, s.a, buf, st)
        for lane in (0, 1):
            qkv_wait_tensor(k, pe, sig, lane, trip, s.a)
        attention_tensor(k, pe, sig, trip, s.a, s.bufs)
        for lane, buf in enumerate(s.bufs):
            pe.wait_ge(*sig.at("x1", lane, trip, 1))
            transpose_z_tensor(k, pe, sig, lane, trip, buf.x1, bank(k, lane, 2)).then_inc(*sig.up("x1T_ps", lane))
        for lane, buf in enumerate(s.bufs):
            pe.wait_ge(*sig.at("x1T", lane, trip, 1))
            for c in range(FF // P):
                ins = proj_feature(k, bank(k, lane, c // 2)[:, c % 2 * SEQ:(c % 2 + 1) * SEQ],
                                   w_of(k, st, "ff1", KC), buf.x1T, c * P, P)
            ins.then_inc(*sig.up("f_ps", lane))
        for lane, buf in enumerate(s.bufs):
            pe.wait_ge(*sig.at("f", lane, trip, 1))
            for t in (0, 1):
                ins = proj_token(k, bank(k, lane, 3)[:, t * D:(t + 1) * D], buf.f, t * P,
                                 w_of(k, st, "ff2", FF // P), row_of(k, st, "ff2b"), FF // P)
            ins.then_inc(*sig.up("out_ps", lane))


def L1_attn_scalar(k, act, s):
    sig = s.sig
    enter(k, act, sig)
    with act.Fori(0, sig.trips) as trip:
        for lane, buf in enumerate(s.bufs):
            zT_scalar(k, act, sig, lane, trip, buf)
        for lane, buf in enumerate(s.bufs):
            q_scalar(k, act, sig, lane, trip, s.a, buf, "L1_attn_bq")
        attention_scalar(k, act, sig, trip, s.a, s.bufs)
        for lane, buf in enumerate(s.bufs):
            act.wait_ge(*sig.at("x1T_ps", lane, trip, 1))
            k.nc.scalar.activation(buf.x1T.rearrange("p c t -> p (c t)"), bank(k, lane, 2), ACT.Copy)\
                .then_inc(*sig.up("x1T", lane))
        for lane, buf in enumerate(s.bufs):
            act.wait_ge(*sig.at("f_ps", lane, trip, 1))
            for c in range(FF // P):
                ins = k.nc.scalar.activation(buf.f[:, c, :],
                                             bank(k, lane, c // 2)[:, c % 2 * SEQ:(c % 2 + 1) * SEQ], ACT.Relu,
                                             bias=col_of(k, "L1_attn_ff1b", c))
            ins.then_inc(*sig.up("f", lane))


def gained_ln_vector(k, ch, src, dst, st, gain, shift):
    v = k.nc.vector
    ch.link(layernorm(k, ch, src, dst, st))
    ch.link(v.tensor_tensor(dst, dst, gain.unsqueeze(1).broadcast_to([P, 2, D]), ALU.mult))
    return v.tensor_tensor(dst, dst, shift.unsqueeze(1).broadcast_to([P, 2, D]), ALU.add)


def L1_attn_vector(k, dve, s):
    v, sig = k.nc.vector, s.sig
    g1, b1, g2, b2 = (spread_of(k, "L1_attn", n) for n in SPREAD["L1_attn"])
    enter(k, dve, sig)
    norms_vector(k, dve, s.norms)
    with dve.Fori(0, sig.trips) as trip:
        chains = [Chain(dve, sig, lane, trip) for lane in (0, 1)]
        for lane, buf in enumerate(s.bufs):
            ln_vector(k, dve, sig, lane, trip, buf)
        for lane, buf in enumerate(s.bufs):
            self_kv_vector(k, dve, sig, lane, trip, s.a, buf, "L1_attn_bk")
        attention_vector(k, dve, sig, trip, chains, s.a, s.bufs)
        for lane, buf in enumerate(s.bufs):
            ch = chains[lane]
            dve.wait_ge(*sig.at("o", lane, trip, len(s.a.rounds)))
            ch.link(v.tensor_tensor(buf.z, buf.z, buf.o, ALU.add))
            gained_ln_vector(k, ch, buf.z, buf.x1, buf.st, g1, b1).then_inc(*sig.up("x1", lane))
        for lane, buf in enumerate(s.bufs):
            ch = chains[lane]
            dve.wait_ge(*sig.at("out_ps", lane, trip, 1))
            ch.link(v.tensor_tensor(buf.x1, buf.x1, bank(k, lane, 3).rearrange("p (t d) -> p t d", t=2), ALU.add))
            ch.link(gained_ln_vector(k, ch, buf.x1, buf.z, buf.st, g2, b2))
            x = x_of(k, trip, lane)
            v.tensor_tensor(x, x, buf.z, ALU.add).then_inc(*sig.up("done", lane))
            ch.close()


def two_attentions_plan(k):
    a, b = attention("self"), attention("cross", p="c_")
    c, bufs = lane_buffers(k)
    for buf in bufs:
        attention_buffers(c, a, buf)
        buf.second = Bag(zT=buf.zT, ctxT=c.take(KC, CTX), qT=buf.qT, kT=buf.kT, v=buf.v, s=buf.s,
                                     probT=buf.probT, o=buf.o, oT=buf.oT, m=buf.m)
        buf.ctxT = buf.second.ctxT
    norms = norms_plan(k, "L1_xattn")
    sig = Signals(k.signals, "L1_xattn", B // 2, 2, z=1, zT_ps=1, zT=1, ctx=1, qkv_ps=1, q=1, v_ps=1, kv=1, oT_ps=1,
                  oT=1, hT_ps=1, zT2=1, c_qkv_ps=1, c_q=1, c_kv=1, c_oT_ps=1, c_oT=1, out_ps=1, done=1,
                  dve_step=k.steps["L1_xattn"], **attention_signals(a), **attention_signals(b))
    return Bag(norms=norms, a=a, b=b, bufs=bufs, seconds=[buf.second for buf in bufs], sig=sig)


def L1_xattn_tensor(k, pe, s):
    sig, st = s.sig, "L1_xattn"
    enter(k, pe, sig)
    with pe.Fori(0, sig.trips) as trip:
        for lane, buf in enumerate(s.bufs):
            zT_tensor(k, pe, sig, lane, trip, buf)
        for lane, buf in enumerate(s.bufs):
            self_qk_tensor(k, pe, sig, lane, trip, s.a, buf, st, "1")
        for lane, buf in enumerate(s.bufs):
            self_v_tensor(k, pe, sig, lane, trip, s.a, buf, st, "1")
        for lane in (0, 1):
            qkv_wait_tensor(k, pe, sig, lane, trip, s.a)
        attention_tensor(k, pe, sig, trip, s.a, s.bufs)
        for lane, buf in enumerate(s.bufs):
            oT_tensor(k, pe, sig, lane, trip, s.a, buf)
        for lane, buf in enumerate(s.bufs):
            pe.wait_ge(*sig.at("oT", lane, trip, 1))
            for c in range(KC):
                ins = proj_feature(k, bank(k, lane, 0)[:, c * SEQ:(c + 1) * SEQ], w_of(k, st, "wo1", KC), buf.oT,
                                   c * P, P)
            ins.then_inc(*sig.up("hT_ps", lane))
        for lane, buf in enumerate(s.seconds):
            cross_qkv_tensor(k, pe, sig, lane, trip, s.b, buf, st, "2")
        for lane in (0, 1):
            qkv_wait_tensor(k, pe, sig, lane, trip, s.b)
        attention_tensor(k, pe, sig, trip, s.b, s.seconds)
        for lane, buf in enumerate(s.seconds):
            oT_tensor(k, pe, sig, lane, trip, s.b, buf)
        for lane, buf in enumerate(s.seconds):
            out_tensor(k, pe, sig, lane, trip, s.b, buf, w_of(k, st, "wo2", KC), row_of(k, st, "bo2"))


def L1_xattn_scalar(k, act, s):
    sig = s.sig
    enter(k, act, sig)
    with act.Fori(0, sig.trips) as trip:
        for lane, buf in enumerate(s.bufs):
            zT_scalar(k, act, sig, lane, trip, buf)
        for lane, buf in enumerate(s.bufs):
            q_scalar(k, act, sig, lane, trip, s.a, buf, "L1_xattn_bq1")
        attention_scalar(k, act, sig, trip, s.a, s.bufs)
        for lane, buf in enumerate(s.bufs):
            oT_scalar(k, act, sig, lane, trip, s.a, buf)
        for lane, buf in enumerate(s.bufs):
            act.wait_ge(*sig.at("hT_ps", lane, trip, 1))
            for c in range(KC):
                ins = k.nc.scalar.activation(buf.zT[:, c, :], bank(k, lane, 0)[:, c * SEQ:(c + 1) * SEQ],
                                             ACT.Identity, bias=col_of(k, "L1_xattn_bo1", c))
            ins.then_inc(*sig.up("zT2", lane))
        for lane, buf in enumerate(s.seconds):
            q_scalar(k, act, sig, lane, trip, s.b, buf, "L1_xattn_bq2")
        attention_scalar(k, act, sig, trip, s.b, s.seconds)
        for lane, buf in enumerate(s.seconds):
            oT_scalar(k, act, sig, lane, trip, s.b, buf)


def L1_xattn_vector(k, dve, s):
    sig = s.sig
    enter(k, dve, sig)
    norms_vector(k, dve, s.norms)
    with dve.Fori(0, sig.trips) as trip:
        chains = [Chain(dve, sig, lane, trip) for lane in (0, 1)]
        for lane, buf in enumerate(s.bufs):
            ln_vector(k, dve, sig, lane, trip, buf)
        for lane, buf in enumerate(s.bufs):
            self_kv_vector(k, dve, sig, lane, trip, s.a, buf, "L1_xattn_bk1")
        attention_vector(k, dve, sig, trip, chains, s.a, s.bufs)
        for lane, buf in enumerate(s.seconds):
            cross_kv_vector(k, dve, sig, lane, trip, s.b, buf, "L1_xattn_bk2")
        attention_vector(k, dve, sig, trip, chains, s.b, s.seconds)
        for lane, buf in enumerate(s.bufs):
            residual_vector(k, dve, sig, lane, trip)
            chains[lane].close()


def round_e4m3(k, link, u, power, near, out):
    v = k.nc.vector
    link(v.tensor_scalar(power.bitcast(U32), u.bitcast(U32), 0x7F800000, None, ALU.bitwise_and))
    link(v.tensor_scalar(power, power, 2.0 ** -6, 1.5 * 2.0 ** 20, ALU.max, ALU.mult))
    link(v.tensor_tensor(near, u, power, ALU.add))
    link(v.tensor_tensor(near, near, power, ALU.subtract))
    link(v.tensor_tensor(power, near, near, ALU.mult))
    link(v.tensor_scalar(power, power, 448.0 ** 2, BIG, ALU.is_gt, ALU.mult))
    link(v.tensor_scalar(power, power, BIG, 0.0, ALU.mult, ALU.mult))
    return v.tensor_tensor(out, power, near, ALU.add)


def inverses(k, link, s, w):
    v = k.nc.vector

    def top(out, src, bits):
        link(v.tensor_scalar(out.bitcast(U32), src.bitcast(U32), 0xFFFFFFFF - (1 << (24 - bits)) + 1, None,
                             ALU.bitwise_and))

    link(v.reciprocal(w.r, s))
    top(w.rh, w.r, 12)
    link(v.tensor_tensor(w.rl, w.r, w.rh, ALU.subtract))
    top(w.sh, s, 12)
    link(v.tensor_tensor(w.sl, s, w.sh, ALU.subtract))
    link(v.tensor_tensor(w.e, w.rh, w.sh, ALU.mult))
    link(v.tensor_scalar(w.e, w.e, -1.0, 1.0, ALU.mult, ALU.add))
    for i, j in ((w.rh, w.sl), (w.rl, w.sh), (w.rl, w.sl)):
        link(v.tensor_tensor(w.part, i, j, ALU.mult))
        link(v.tensor_tensor(w.e, w.e, w.part, ALU.subtract))
    top(w.r1, w.r, 16)
    link(v.tensor_tensor(w.r2, w.r, w.r1, ALU.subtract))
    link(v.tensor_tensor(w.e, w.e, w.r, ALU.mult))
    link(v.tensor_tensor(w.r2, w.r2, w.e, ALU.add))


def over(k, link, out, src, w, i):
    v = k.nc.vector
    link(v.tensor_scalar(out, src, w.r2[:, i:i + 1], None, ALU.mult))
    link(v.scalar_tensor_tensor(out, src, w.r1[:, i:i + 1], out, ALU.mult, ALU.add))


def fp8_plan(k):
    c, bufs = lane_buffers(k)
    for buf in bufs:
        buf.zb, buf.q = c.take(KC, SEQ, dt=BF16), c.take(KC, SEQ, dt=BF16)
        buf.u, buf.power, buf.near = c.take(KC * SEQ), c.take(KC * SEQ), c.take(KC * SEQ)
        buf.y = c.take(2, D, dt=BF16)
    w = Bag(q=c.take(KC, D, dt=BF16), u=c.take(KC * D), power=c.take(KC * D), near=c.take(KC * D),
                        scale=c.take(1), **{n: c.take(2) for n in ("r", "rh", "rl", "sh", "sl", "e", "part", "r1", "r2")})
    norms = norms_plan(k, "L1_ffn")
    prep = Signals(k.signals, "L1_ffn", 1, 1, dve_step=k.steps["fp8_prep"], done=1)
    sig = Signals(k.signals, "L1_ffn", B // 2, 2, z=1, zT_ps=1, zT=1, q=1, out_ps=1, done=1,
                  dve_step=k.steps["L1_ffn"])
    return Bag(norms=norms, bufs=bufs, w=w, prep=prep, sig=sig)


def L1_ffn_tensor(k, pe, s):
    sig = s.sig
    enter(k, pe, sig)
    with pe.Fori(0, sig.trips) as trip:
        for lane, buf in enumerate(s.bufs):
            zT_tensor(k, pe, sig, lane, trip, buf)
        for lane, buf in enumerate(s.bufs):
            pe.wait_ge(*sig.at("q", lane, trip, 1))
            for t in (0, 1):
                ins = proj_token(k, bank(k, lane, 1)[:, t * D:(t + 1) * D], buf.q, t * P, s.w.q)
            ins.then_inc(*sig.up("out_ps", lane))


def L1_ffn_scalar(k, act, s):
    enter(k, act, s.sig)
    with act.Fori(0, s.sig.trips) as trip:
        for lane, buf in enumerate(s.bufs):
            act.wait_ge(*s.sig.at("zT_ps", lane, trip, 1))
            k.nc.scalar.activation(buf.zb.rearrange("p c t -> p (c t)"), bank(k, lane, 0), ACT.Copy)\
                .then_inc(*s.sig.up("zT", lane))


def L1_ffn_vector(k, dve, s):
    v, sig, w = k.nc.vector, s.sig, s.w
    enter(k, dve, s.prep)
    norms_vector(k, dve, s.norms)
    ch = Chain(dve, s.prep, 0, 0)
    i = SCALARS.index("s_in")
    inverses(k, ch.link, k.scalars[:, i:i + 2], w)
    over(k, ch.link, w.u, k.fp8_kernel, w, 1)
    round_e4m3(k, ch.link, w.u, w.power, w.near, w.q.rearrange("p c d -> p (c d)"))
    v.tensor_tensor(w.scale, scalar_of(k, "s_in"), scalar_of(k, "s_k"), ALU.mult).then_inc(*s.prep.up("done"))
    ch.close()
    enter(k, dve, sig)
    with dve.Fori(0, sig.trips) as trip:
        chains = [Chain(dve, sig, lane, trip) for lane in (0, 1)]
        for lane, buf in enumerate(s.bufs):
            ln_vector(k, dve, sig, lane, trip, buf)
        for lane, buf in enumerate(s.bufs):
            ch = chains[lane]
            dve.wait_ge(*sig.at("zT", lane, trip, 1))
            over(k, ch.link, buf.u, buf.zb.rearrange("p c t -> p (c t)"), w, 0)
            round_e4m3(k, ch.link, buf.u, buf.power, buf.near, buf.q.rearrange("p c t -> p (c t)"))\
                .then_inc(*sig.up("q", lane))
        for lane, buf in enumerate(s.bufs):
            ch = chains[lane]
            x = x_of(k, trip, lane)
            dve.wait_ge(*sig.at("out_ps", lane, trip, 1))
            ch.link(v.tensor_scalar(buf.y.rearrange("p t d -> p (t d)"), bank(k, lane, 1), w.scale, None, ALU.mult))
            ch.link(v.tensor_tensor(buf.y, buf.y, k.fp8_bias.unsqueeze(1).broadcast_to([P, 2, D]), ALU.add))
            v.tensor_tensor(x, x, buf.y, ALU.add).then_inc(*sig.up("done", lane))
            ch.close()


GROUPS = NH1 // 4


def width_one_plan(k):
    c, bufs = lane_buffers(k)
    for buf in bufs:
        buf.qk, buf.kmax, buf.kmin = c.take(2, SEQ), c.take(SEQ), c.take(SEQ)
        buf.nm = c.take(SEQ)
        buf.v1 = c.take(2, NH1, 2)
        buf.o, buf.oT, buf.rec = c.take(2, NH1), c.take(SEQ), c.take(2, NH1)
        buf.qrows, buf.krows = c.take(16, SEQ), c.take(16, SEQ)
    prob = c.take(2, 3, 512)
    norms = norms_plan(k, "L2_attn")
    prep = Signals(k.signals, "L2_attn", 1, 2, done=1)
    sig = Signals(k.signals, "L2_attn", B // 2, 2, z=1, zT_ps=1, zT=1, qkv_ps=1, kv=1, nm=1, s_ps=GROUPS,
                  prob=GROUPS, pv_ps=GROUPS, o=1, oT_ps=1, oT=1, out_ps=1, done=1, dve_step=k.steps["L2_attn"])
    rows = Signals(k.signals, "L2_attn", B // 2, 2, rows=3 * 4 * 16)
    return Bag(norms=norms, bufs=bufs, prob=prob, prep=prep, sig=sig, rows=rows)


def L2_attn_sync(k, sp, s):
    with sp.Fori(0, s.sig.trips) as trip:
        for lane, buf in enumerate(s.bufs):
            sp.wait_ge(*s.sig.at("nm", lane, trip, 1))
            for r in range(4):
                heads = slice(16 * r, 16 * r + 16)
                for dst, part, src in ((buf.qrows, 0, buf.qk[heads, 0, :]), (buf.qrows, 1, buf.nm[heads, :]),
                                       (buf.krows, 0, buf.qk[heads, 1, :])):
                    sp.dma_start(dst[PAD * r + part:PAD * r + part + 1, :, :], src)\
                        .then_inc(s.rows.sems["rows"][lane], 16)


def group_tensor(k, pe, s, lane, trip, buf, g):
    mm, r = k.nc.tensor.matmul, g // 4
    base = 3 * (g % 2)
    if g >= 2:
        pe.wait_ge(*s.sig.at("prob", lane, trip, g - 1))
    elif lane == 1:
        pe.wait_ge(*s.sig.at("prob", 0, trip, GROUPS - 1 + g))
    for i, mask in ((0, "keyA"), (1, "keyA"), (2, "keyC")):
        mm(k.ps[:, base + i, :], k.identb[:, :], mask_of(k, mask), start=True, stop=False, skip_group_check=True)
    for u in range(4):
        hh = g % 4 * 4 + u
        q, kk = (ap[PAD * r:PAD * r + 2, hh, :] for ap in (buf.qrows, buf.krows))
        mm(k.ps[:, base + u // 2, u % 2 * SEQ:(u % 2 + 1) * SEQ], kk[:, 0:P], q, start=False, stop=True,
           skip_group_check=True)
        ins = mm(k.ps[:, base + 2, u * P:(u + 1) * P], kk[:, P:SEQ], q[:, P:SEQ], start=False, stop=True,
                 skip_group_check=True)
    ins.then_inc(*s.sig.up("s_ps", lane))


def group_out_tensor(k, pe, s, lane, trip, buf, g):
    mm, prob = k.nc.tensor.matmul, s.prob[:, g % 2]
    pe.wait_ge(*s.sig.at("prob", lane, trip, g + 1))
    if g == 0 and lane == 1:
        pe.wait_ge(*s.sig.at("o", 0, trip, 1))
    for u in range(4):
        h = 16 * (g // 4) + g % 4 * 4 + u
        at = u % 2 * SEQ
        out = lambda t: k.ps[:, 6, (t * NH1 + h) * 2:(t * NH1 + h) * 2 + 2]
        mm(out(0), prob[:, u // 2, at:at + P], buf.v1[:, 0, h, :], start=True, stop=True)
        mm(out(1), prob[:, u // 2, at + P:at + SEQ], buf.v1[:, 0, h, :], start=True, stop=False)
        ins = mm(out(1), prob[:, 2, u * P:(u + 1) * P], buf.v1[:, 1, h, :], start=False, stop=True)
    ins.then_inc(*s.sig.up("pv_ps", lane))


def L2_attn_tensor(k, pe, s):
    sig, st = s.sig, "L2_attn"
    enter(k, pe, sig)
    wqkv = w_of(k, st, "wqkv", KC)
    with pe.Fori(0, sig.trips) as trip:
        for lane, buf in enumerate(s.bufs):
            if lane == 0:
                pe.wait_ge(*sig.at("done", 1, trip, 0))
            pe.wait_ge(*sig.at("z", lane, trip, 1))
            transpose_z_tensor(k, pe, sig, lane, trip, buf.z, k.ps[:, 3 * lane, :]).then_inc(*sig.up("zT_ps", lane))
        for lane, buf in enumerate(s.bufs):
            pe.wait_ge(*sig.at("zT", lane, trip, 1))
            for i in (0, 1):
                proj_feature(k, k.ps[0:NH1, 3 * lane, i * SEQ:(i + 1) * SEQ], wqkv, buf.zT, i * NH1, NH1)
            for t in (0, 1):
                ins = proj_token(k, k.ps[:, 3 * lane + 1, t * NH1:(t + 1) * NH1], buf.zT, t * P,
                                 wqkv[:, :, 2 * NH1:3 * NH1])
            ins.then_inc(*sig.up("qkv_ps", lane))
        for lane in (0, 1):
            pe.wait_ge(*sig.at("kv", lane, trip, 1))
        for lane, buf in enumerate(s.bufs):
            pe.wait_ge(*s.rows.at("rows", lane, trip, 3 * 4 * 16))
            group_tensor(k, pe, s, lane, trip, buf, 0)
            for g in range(GROUPS):
                if g + 1 < GROUPS:
                    group_tensor(k, pe, s, lane, trip, buf, g + 1)
                group_out_tensor(k, pe, s, lane, trip, buf, g)
            pe.wait_ge(*sig.at("o", lane, trip, 1))
            if lane:
                pe.wait_ge(*sig.at("done", 0, trip, 1))
            hold(k, pe, "tensor")
            for t in (0, 1):
                ins = k.nc.tensor.transpose(k.ps[0:NH1, 7, t * P:(t + 1) * P], buf.o[:, t, :], k.ident[:, :])
            ins.then_inc(*sig.up("oT_ps", lane))
            pe.wait_ge(*sig.at("oT", lane, trip, 1))
            for t in (0, 1):
                ins = products(k, k.ps[:, 7, t * D:(t + 1) * D],
                               [(buf.oT[0:NH1, t * P:(t + 1) * P], w_of(k, st, "wout")[0:NH1, :])])
            ins.then_inc(*sig.up("out_ps", lane))


def L2_attn_scalar(k, act, s):
    sig, a = s.sig, k.nc.scalar.activation
    enter(k, act, sig)
    with act.Fori(0, sig.trips) as trip:
        for lane, buf in enumerate(s.bufs):
            act.wait_ge(*sig.at("zT_ps", lane, trip, 1))
            a(buf.zT.rearrange("p c t -> p (c t)"), k.ps[:, 3 * lane, :], ACT.Copy).then_inc(*sig.up("zT", lane))
        for lane, buf in enumerate(s.bufs):
            for g in range(GROUPS):
                act.wait_ge(*sig.at("s_ps", lane, trip, g + 1))
                if g >= 2:
                    act.wait_ge(*sig.at("pv_ps", lane, trip, g - 1))
                elif lane == 1:
                    act.wait_ge(*sig.at("pv_ps", 0, trip, GROUPS - 1 + g))
                a(s.prob[:, g % 2], k.ps[:, 3 * (g % 2):3 * (g % 2) + 3, :], ACT.Exp, scale=NH1 ** -0.5)\
                    .then_inc(*sig.up("prob", lane))
            act.wait_ge(*sig.at("oT_ps", lane, trip, 1))
            a(buf.oT[0:NH1, :], k.ps[0:NH1, 7, 0:SEQ], ACT.Copy).then_inc(*sig.up("oT", lane))


def L2_attn_vector(k, dve, s):
    v, sig = k.nc.vector, s.sig
    enter(k, dve, s.prep)
    norms_vector(k, dve, s.norms)
    for lane, buf in enumerate(s.bufs):
        v.memset(buf.v1, 1.0)
        v.memset(buf.krows, 1.0).then_inc(*s.prep.up("done", lane))
    enter(k, dve, sig)
    with dve.Fori(0, sig.trips) as trip:
        chains = [Chain(dve, sig, lane, trip) for lane in (0, 1)]
        for lane, buf in enumerate(s.bufs):
            ln_vector(k, dve, sig, lane, trip, buf)
        for lane, buf in enumerate(s.bufs):
            ch = chains[lane]
            dve.wait_ge(*sig.at("qkv_ps", lane, trip, 1))
            qk, kmax, kmin, nm = buf.qk[0:NH1], buf.kmax[0:NH1], buf.kmin[0:NH1], buf.nm[0:NH1]
            ch.link(v.tensor_copy(qk.rearrange("p c t -> p (c t)"), k.ps[0:NH1, 3 * lane, :]))
            v.tensor_copy(buf.v1[:, :, :, 0:1],
                          k.ps[:, 3 * lane + 1, 0:2 * NH1].rearrange("p (t h o) -> p t h o", t=2, o=1))\
                .then_inc(*sig.up("kv", lane))
            v.tensor_tensor_scan(kmax, qk[:, 1, :], qk[:, 1, :], -BIG, ALU.max, ALU.max)
            ch.link(v.tensor_tensor_scan(kmin, qk[:, 1, :], qk[:, 1, :], BIG, ALU.min, ALU.min))
            v.scalar_tensor_tensor(kmax, qk[:, 0, :], -1.0, kmax, ALU.mult, ALU.mult)
            ch.link(v.scalar_tensor_tensor(kmin, qk[:, 0, :], -1.0, kmin, ALU.mult, ALU.mult))
            v.tensor_tensor(nm, kmax, kmin, ALU.min).then_inc(*sig.up("nm", lane))
        for lane, buf in enumerate(s.bufs):
            ch = chains[lane]
            o_ps = k.ps[:, 6, 0:2 * NH1 * 2].rearrange("p (t h e) -> p t h e", t=2, e=2)
            dve.wait_ge(*sig.at("pv_ps", lane, trip, GROUPS))
            ch.link(v.reciprocal(buf.rec.unsqueeze(3), o_ps[:, :, :, 1:2]))
            v.tensor_tensor(buf.o.unsqueeze(3), o_ps[:, :, :, 0:1], buf.rec.unsqueeze(3), ALU.mult)\
                .then_inc(*sig.up("o", lane))
            x = x_of(k, trip, lane)
            dve.wait_ge(*sig.at("out_ps", lane, trip, 1))
            v.tensor_tensor(x, x, k.ps[:, 7, :].rearrange("p (t d) -> p t d", t=2), ALU.add)\
                .then_inc(*sig.up("done", lane))
            ch.close()


SC = SLOTS // P
SH_HALF = SLOTS // 2


def slots_plan(k):
    c, bufs = lane_buffers(k, 1)
    buf = bufs[0]
    buf.seT, buf.norm, buf.slots = c.take(KC, SLOTS), c.take(3 * SC), w_of(k, "L2_ffn", "slots", SC)
    buf.ex = c.take(SC, SEQ)
    buf.disp = c.take(2, SLOTS)
    buf.slotsT, buf.hT, buf.out = c.take(KC, SLOTS), c.take(E_SLOT_HID // P, SH_HALF), c.take(SC, D)
    buf.m = c.take(4 * SC)
    buf.zn = c.take(2, D)
    norms = norms_plan(k, "L2_ffn")
    prep = Signals(k.signals, "L2_ffn", 1, 1, se=1, seT_ps=1, seT=1, done=1, dve_step=k.steps["slots_prep"])
    sig = Signals(k.signals, "L2_ffn", B, 1, z=1, zT_ps=1, zT=1, lT_ps=1, lmax=1, ex=1, disp=1, dispT_ps=1, dispT_a=1,
                  dispT_v=1, slots_ps=1, slots=1, hid_ps=16, hid=16, proc_ps=2, proc=2, l_ps=1, cmax=1, comb=1,
                  combT_ps=1, combT_a=1, combT_v=1, out_ps=1, done=1, dve_step=k.steps["L2_ffn"])
    return Bag(norms=norms, buf=buf, prep=prep, sig=sig)


def rms_vector(k, ch, src, dst, squares, st, n):
    v = k.nc.vector
    ch.link(v.tensor_tensor(squares, src, src, ALU.mult))
    ch.link(v.tensor_reduce(st[:, 0:n], squares, AX, ALU.add))
    rsqrt(k, ch.link, st[:, n:2 * n], st[:, 0:n], st[:, 2 * n:3 * n])
    ch.link(v.tensor_scalar(st[:, n:2 * n], st[:, n:2 * n], 1e12, None, ALU.min))
    for i in range(n):
        ins = v.tensor_scalar(dst[:, i, :], src[:, i, :], st[:, n + i:n + i + 1], float(D) ** 0.5, ALU.mult, ALU.mult)
    return ins


def L2_ffn_tensor(k, pe, s):
    sig, buf, tr, mm = s.sig, s.buf, k.nc.tensor.transpose, k.nc.tensor.matmul
    enter(k, pe, s.prep)
    pe.wait_ge(*s.prep.at("se", 0, 0, 1))
    for n in range(SC):
        for c in range(KC):
            ins = tr(k.ps[:, 2 * c + n // 4, n % 4 * P:(n % 4 + 1) * P], buf.slots[:, n, c * P:(c + 1) * P],
                     k.ident[:, :])
    ins.then_inc(*s.prep.up("seT_ps"))
    enter(k, pe, sig)
    w1, w2 = w_of(k, "L2_ffn", "w1", KC), w_of(k, "L2_ffn", "w2", E_SLOT_HID // P)
    with pe.Fori(0, sig.trips) as trip:
        pe.wait_ge(*sig.at("z", 0, trip, 1))
        transpose_z_tensor(k, pe, sig, 0, trip, buf.zn, k.ps[:, 0, :]).then_inc(*sig.up("zT_ps"))
        pe.wait_ge(*sig.at("zT", 0, trip, 1))
        for n in range(SC):
            ins = proj_feature(k, k.ps[:, 4 + n // 2, n % 2 * SEQ:(n % 2 + 1) * SEQ], buf.seT, buf.zT, n * P, P)
        ins.then_inc(*sig.up("lT_ps"))
        for t in (0, 1):
            for half in (0, 1):
                ins = products(k, k.ps[:, 2 * t + half, :],
                               [(buf.zT[:, c, t * P:(t + 1) * P], buf.seT[:, c, half * 512:(half + 1) * 512])
                                for c in range(KC)])
        ins.then_inc(*sig.up("l_ps"))
        pe.wait_ge(*sig.at("disp", 0, trip, 1))
        for t in (0, 1):
            for n in range(SC):
                ins = tr(k.ps[:, 4 + 2 * t + n // 4, n % 4 * P:(n % 4 + 1) * P], buf.ex[:, n, t * P:(t + 1) * P],
                         k.ident[:, :])
        ins.then_inc(*sig.up("dispT_ps"))
        pe.wait_ge(*sig.at("dispT_a", 0, trip, 1))
        pe.wait_ge(*sig.at("dispT_v", 0, trip, 1))
        for c in range(KC):
            for half in (0, 1):
                ins = products(k, k.ps[:, 4 + 2 * c + half, :],
                               [(buf.zn[:, t, c * P:(c + 1) * P], buf.disp[:, t, half * 512:(half + 1) * 512])
                                for t in (0, 1)])
        ins.then_inc(*sig.up("slots_ps"))
        pe.wait_ge(*sig.at("slots", 0, trip, 1))
        for half in (0, 1):
            for j in range(E_SLOT_HID // P):
                n = 8 * half + j
                if n >= 4:
                    pe.wait_ge(*sig.at("hid", 0, trip, n - 3))
                proj_feature(k, k.ps[:, 4 + j % 4, :], w1, buf.slotsT[:, :, half * 512:(half + 1) * 512], j * P, P)\
                    .then_inc(*sig.up("hid_ps"))
            pe.wait_ge(*sig.at("hid", 0, trip, 8 * half + 8))
            for n in range(4):
                ins = products(k, k.ps[:, 4 + n // 2, n % 2 * D:(n % 2 + 1) * D],
                               [(buf.hT[:, j, n * P:(n + 1) * P], w2[:, j, :]) for j in range(E_SLOT_HID // P)])
            ins.then_inc(*sig.up("proc_ps"))
            pe.wait_ge(*sig.at("proc", 0, trip, half + 1))
        pe.wait_ge(*sig.at("comb", 0, trip, 1))
        for n in range(SC):
            for t in (0, 1):
                ins = tr(k.ps[:, 4 + n // 2, (n % 2 * 2 + t) * P:(n % 2 * 2 + t + 1) * P],
                         buf.disp[:, t, n * P:(n + 1) * P], k.ident[:, :])
        ins.then_inc(*sig.up("combT_ps"))
        pe.wait_ge(*sig.at("combT_a", 0, trip, 1))
        pe.wait_ge(*sig.at("combT_v", 0, trip, 1))
        for t in (0, 1):
            ins = products(k, k.ps[:, 0, t * D:(t + 1) * D],
                           [(buf.ex[:, n, t * P:(t + 1) * P], buf.out[:, n, :]) for n in range(SC)])
        ins.then_inc(*sig.up("out_ps"))


def L2_ffn_scalar(k, act, s):
    sig, buf, a = s.sig, s.buf, k.nc.scalar.activation
    enter(k, act, s.prep)
    act.wait_ge(*s.prep.at("seT_ps", 0, 0, 1))
    for c in range(KC):
        ins = a(buf.seT[:, c, :], k.ps[:, 2 * c:2 * c + 2, :].rearrange("p b f -> p (b f)"), ACT.Copy,
                scale=col_of(k, "L2_ffn_gs", c))
    ins.then_inc(*s.prep.up("seT"))
    enter(k, act, sig)
    with act.Fori(0, sig.trips) as trip:
        act.wait_ge(*sig.at("zT_ps", 0, trip, 1))
        for c in range(KC):
            ins = a(buf.zT[:, c, :], k.ps[:, 0, c * SEQ:(c + 1) * SEQ], ACT.Copy, scale=col_of(k, "L2_ffn_gx", c))
        ins.then_inc(*sig.up("zT"))
        act.wait_ge(*sig.at("lmax", 0, trip, 1))
        for n in range(SC):
            ins = a(buf.ex[:, n, :], k.ps[:, 4 + n // 2, n % 2 * SEQ:(n % 2 + 1) * SEQ], ACT.Exp,
                    bias=buf.m[:, n:n + 1], accum_out=buf.m[:, SC + n:SC + n + 1])
        ins.then_inc(*sig.up("ex"))
        act.wait_ge(*sig.at("dispT_ps", 0, trip, 1))
        a(buf.disp[:, 0, :], k.ps[:, 4:6, :].rearrange("p b f -> p (b f)"), ACT.Copy).then_inc(*sig.up("dispT_a"))
        act.wait_ge(*sig.at("slots_ps", 0, trip, 1))
        for c in range(KC):
            ins = a(buf.slotsT[:, c, :], k.ps[:, 4 + 2 * c:6 + 2 * c, :].rearrange("p b f -> p (b f)"), ACT.Copy,
                    scale=col_of(k, "L2_ffn_gx", c))
        ins.then_inc(*sig.up("slots"))
        for half in (0, 1):
            if half:
                act.wait_ge(*sig.at("proc_ps", 0, trip, 1))
            for j in range(E_SLOT_HID // P):
                act.wait_ge(*sig.at("hid_ps", 0, trip, 8 * half + j + 1))
                a(buf.hT[:, j, :], k.ps[:, 4 + j % 4, :], ACT.Gelu).then_inc(*sig.up("hid"))
        act.wait_ge(*sig.at("cmax", 0, trip, 1))
        for t in (0, 1):
            ins = a(buf.disp[:, t, :], k.ps[:, 2 * t:2 * t + 2, :].rearrange("p b f -> p (b f)"), ACT.Exp,
                    bias=buf.m[:, 2 * SC + t:2 * SC + t + 1], accum_out=buf.m[:, 2 * SC + 2 + t:2 * SC + 3 + t])
        ins.then_inc(*sig.up("comb"))
        act.wait_ge(*sig.at("combT_ps", 0, trip, 1))
        a(buf.ex[:, 0:SC // 2, :].rearrange("p n t -> p (n t)"), k.ps[:, 4:6, :].rearrange("p b f -> p (b f)"), ACT.Copy)\
            .then_inc(*sig.up("combT_a"))


def L2_ffn_vector(k, dve, s):
    sig, buf, v = s.sig, s.buf, k.nc.vector
    ch = Chain(dve, s.prep, 0, 0)
    enter(k, dve, s.prep)
    norms_vector(k, dve, s.norms)
    rms_vector(k, ch, buf.slots, buf.slots, buf.out, buf.norm, SC).then_inc(*s.prep.up("se"))
    dve.wait_ge(*s.prep.at("seT", 0, 0, 1))
    v.memset(buf.m, 0.0).then_inc(*s.prep.up("done"))
    ch.close()
    enter(k, dve, sig)
    with dve.Fori(0, sig.trips) as trip:
        ch = Chain(dve, sig, 0, trip)
        dve.wait_ge(*sig.at("done", 0, trip, 0))
        hold(k, dve, "vector")
        ch.link(ln_apply(k, trip, 0, 1, buf.z))
        rms_vector(k, ch, buf.z, buf.zn, buf.out[:, 0:2, :], buf.norm, 2).then_inc(*sig.up("z"))
        dve.wait_ge(*sig.at("lT_ps", 0, trip, 1))
        v.tensor_reduce(buf.m[:, 0:SC], k.ps[:, 4:8, :].rearrange("p b (c t) -> p (b c) t", c=2), AX, ALU.max,
                        negate=True).then_inc(*sig.up("lmax"))
        dve.wait_ge(*sig.at("l_ps", 0, trip, 1))
        v.tensor_reduce(buf.m[:, 2 * SC:2 * SC + 2], k.ps[:, 0:4, :].rearrange("p (t h) f -> p t (h f)", t=2), AX,
                        ALU.max, negate=True).then_inc(*sig.up("cmax"))
        dve.wait_ge(*sig.at("ex", 0, trip, 1))
        ch.link(v.reciprocal(buf.m[:, SC:2 * SC], buf.m[:, SC:2 * SC]))
        for n in range(SC):
            ins = v.tensor_scalar(buf.ex[:, n, :], buf.ex[:, n, :], buf.m[:, SC + n:SC + n + 1], None, ALU.mult)
        ins.then_inc(*sig.up("disp"))
        dve.wait_ge(*sig.at("dispT_ps", 0, trip, 1))
        v.tensor_copy(buf.disp[:, 1, :], k.ps[:, 6:8, :].rearrange("p b f -> p (b f)")).then_inc(*sig.up("dispT_v"))
        for half in (0, 1):
            dve.wait_ge(*sig.at("proc_ps", 0, trip, half + 1))
            v.tensor_copy(buf.out[:, 4 * half:4 * half + 4, :].rearrange("p n d -> p (n d)"),
                          k.ps[:, 4:6, :].rearrange("p b f -> p (b f)")).then_inc(*sig.up("proc"))
        dve.wait_ge(*sig.at("combT_ps", 0, trip, 1))
        v.tensor_copy(buf.ex[:, SC // 2:SC, :].rearrange("p n t -> p (n t)"),
                      k.ps[:, 6:8, :].rearrange("p b f -> p (b f)")).then_inc(*sig.up("combT_v"))
        ch.link(v.reciprocal(buf.m[:, 2 * SC + 2:2 * SC + 4], buf.m[:, 2 * SC + 2:2 * SC + 4]))
        dve.wait_ge(*sig.at("out_ps", 0, trip, 1))
        hold(k, dve, "vector")
        x = x_of(k, trip, 0, 1)
        for t in (0, 1):
            ins = v.scalar_tensor_tensor(x[:, t, :], k.ps[:, 0, t * D:(t + 1) * D],
                                         buf.m[:, 2 * SC + 2 + t:2 * SC + 3 + t], x[:, t, :], ALU.mult, ALU.add)
        ins.then_inc(*sig.up("done"))
        ch.close()


def scan_plan(k):
    c, bufs = lane_buffers(k)
    for buf in bufs:
        buf.zn = c.take(2, D)
        buf.a, buf.b, buf.c = c.take(KC, SEQ), c.take(KC, SEQ), c.take(KC, SEQ)
        buf.prod, buf.sum = c.take(KC, SEQ), c.take(KC, SEQ)
    ones = c.take(SEQ)
    norms = norms_plan(k, "L3_attn")
    prep = Signals(k.signals, "L3_attn", 1, 1, done=1)
    sig = Signals(k.signals, "L3_attn", B // 2, 2, z=1, zT_ps=1, zT=1, abc_ps=1, abc=1, o=1, out_ps=1, done=1,
                  dve_step=k.steps["L3_attn"])
    return Bag(norms=norms, bufs=bufs, ones=ones, prep=prep, sig=sig)


def L3_attn_tensor(k, pe, s):
    sig = s.sig
    enter(k, pe, sig)
    with pe.Fori(0, sig.trips) as trip:
        for lane, buf in enumerate(s.bufs):
            pe.wait_ge(*sig.at("z", lane, trip, 1))
            transpose_z_tensor(k, pe, sig, lane, trip, buf.zn, bank(k, lane, 3)).then_inc(*sig.up("zT_ps", lane))
        for lane, buf in enumerate(s.bufs):
            pe.wait_ge(*sig.at("zT", lane, trip, 1))
            for i, w in enumerate(("wa", "wb", "wc")):
                for c in range(KC):
                    ins = proj_feature(k, bank(k, lane, i)[:, c * SEQ:(c + 1) * SEQ], w_of(k, "L3_attn", w, KC),
                                       buf.zT, c * P, P)
            ins.then_inc(*sig.up("abc_ps", lane))
        for lane, buf in enumerate(s.bufs):
            pe.wait_ge(*sig.at("o", lane, trip, 1))
            for t in (0, 1):
                for c in range(KC):
                    ins = k.nc.tensor.transpose(bank(k, lane, 3)[:, (2 * t + c) * P:(2 * t + c + 1) * P],
                                                buf.b[:, c, t * P:(t + 1) * P], k.ident[:, :])
            ins.then_inc(*sig.up("out_ps", lane))


def L3_attn_scalar(k, act, s):
    sig, a = s.sig, k.nc.scalar.activation
    enter(k, act, sig)
    with act.Fori(0, sig.trips) as trip:
        for lane, buf in enumerate(s.bufs):
            act.wait_ge(*sig.at("zT_ps", lane, trip, 1))
            for c in range(KC):
                ins = a(buf.zT[:, c, :], bank(k, lane, 3)[:, c * SEQ:(c + 1) * SEQ], ACT.Identity,
                        bias=col_of(k, "L3_attn_be", c), scale=col_of(k, "L3_attn_g", c))
            ins.then_inc(*sig.up("zT", lane))
        for lane, buf in enumerate(s.bufs):
            act.wait_ge(*sig.at("abc_ps", lane, trip, 1))
            for i, (dst, fn, b) in enumerate(((buf.a, ACT.Sigmoid, "ba"), (buf.b, ACT.Identity, "bb"),
                                              (buf.c, ACT.Identity, "bc"))):
                for c in range(KC):
                    ins = a(dst[:, c, :], bank(k, lane, i)[:, c * SEQ:(c + 1) * SEQ], fn,
                            bias=col_of(k, "L3_attn_" + b, c))
            ins.then_inc(*sig.up("abc", lane))


def L3_attn_vector(k, dve, s):
    v, sig = k.nc.vector, s.sig
    enter(k, dve, s.prep)
    norms_vector(k, dve, s.norms)
    v.memset(s.ones, 1.0).then_inc(*s.prep.up("done"))
    enter(k, dve, sig)
    with dve.Fori(0, sig.trips) as trip:
        chains = [Chain(dve, sig, lane, trip) for lane in (0, 1)]
        for lane, buf in enumerate(s.bufs):
            ch = chains[lane]
            dve.wait_ge(*sig.at("done", lane, trip, 0))
            hold(k, dve, "vector")
            ch.link(ln_apply(k, trip, lane, 2, buf.z))
            layernorm(k, ch, buf.z, buf.zn, buf.st).then_inc(*sig.up("z", lane))
        for lane, buf in enumerate(s.bufs):
            ch = chains[lane]
            flat = lambda ap: ap.rearrange("p c t -> p (c t)")
            dve.wait_ge(*sig.at("abc", lane, trip, 1))
            for c in range(KC):
                ins = v.tensor_tensor_scan(buf.prod[:, c, :], buf.a[:, c, :], s.ones, 1.0, ALU.mult, ALU.mult)
            ch.link(ins)
            ch.link(v.tensor_scalar(flat(buf.a), flat(buf.prod), 1e-8, None, ALU.add))
            ch.link(v.reciprocal(flat(buf.a), flat(buf.a)))
            ch.link(v.tensor_tensor(flat(buf.a), flat(buf.b), flat(buf.a), ALU.mult))
            for c in range(KC):
                ins = v.tensor_tensor_scan(buf.sum[:, c, :], buf.a[:, c, :], s.ones, 0.0, ALU.add, ALU.mult)
            ch.link(ins)
            for c in range(KC):
                ins = v.scalar_tensor_tensor(buf.b[:, c, :], buf.sum[:, c, :], col_of(k, "L3_attn_h0", c),
                                             buf.prod[:, c, :], ALU.add, ALU.mult)
            ch.link(ins)
            v.tensor_tensor(flat(buf.b), flat(buf.b), flat(buf.c), ALU.mult).then_inc(*sig.up("o", lane))
        for lane, buf in enumerate(s.bufs):
            ch = chains[lane]
            x = x_of(k, trip, lane)
            dve.wait_ge(*sig.at("out_ps", lane, trip, 1))
            ch.link(v.tensor_tensor(buf.z, buf.z, bank(k, lane, 3).rearrange("p (t d) -> p t d", t=2), ALU.add))
            v.tensor_tensor(x, x, buf.z, ALU.add).then_inc(*sig.up("done", lane))
            ch.close()


FW = 2 * HD + 1


def features_plan(k):
    a = attention("cross", hd=2 * HD, vw=FW, scale=1.0 / 16.0)
    c, bufs = lane_buffers(k)
    for buf in bufs:
        buf.ctxT = c.take(KC, CTX)
        attention_buffers(c, a, buf)
    norms = norms_plan(k, "L3_xattn")
    prep = Signals(k.signals, "L3_xattn", 1, 2, done=1)
    sig = Signals(k.signals, "L3_xattn", B // 2, 2, z=1, zT_ps=1, zT=1, ctx=1, qkv_ps=1, q=1, kv=1, oT_ps=1, oT=1,
                  out_ps=1, done=1, dve_step=k.steps["L3_xattn"], **attention_signals(a))
    return Bag(norms=norms, a=a, bufs=bufs, prep=prep, sig=sig)


def L3_xattn_tensor(k, pe, s):
    sig, st = s.sig, "L3_xattn"
    enter(k, pe, sig)
    wf, wv, bf = w_of(k, st, "wf", KC), w_of(k, st, "wv", KC), row_of(k, st, "bf")
    with pe.Fori(0, sig.trips) as trip:
        for lane, buf in enumerate(s.bufs):
            zT_tensor(k, pe, sig, lane, trip, buf)
        for lane, buf in enumerate(s.bufs):
            pe.wait_ge(*sig.at("zT", lane, trip, 1))
            pe.wait_ge(*sig.at("ctx", lane, trip, 1))
            for src, n, at in ((buf.zT, SEQ, 0), (buf.ctxT, CTX, 2)):
                for c in range(HC):
                    out = bank(k, lane, c // 2)[:, c % 2 * SEQ:(c % 2 + 1) * SEQ] if at == 0 else \
                        bank(k, lane, 2)[:, c * P:c * P + CTX]
                    for d in range(KC):
                        k.nc.tensor.matmul(out, wf[:, d, c * P:(c + 1) * P], src[:, d, :], start=d == 0, stop=False)
                    k.nc.tensor.matmul(out, bf[:, c * P:(c + 1) * P], k.ones[0:1, 0:n], start=False, stop=True)
            products(k, bank(k, lane, 3)[0:CTX, 0:D], [(buf.ctxT[:, c, :], wv[:, c, :]) for c in range(KC)],
                     row_of(k, st, "bv")).then_inc(*sig.up("qkv_ps", lane))
        for lane in (0, 1):
            pe.wait_ge(*sig.at("q", lane, trip, 1))
        attention_tensor(k, pe, sig, trip, s.a, s.bufs)
        for lane, buf in enumerate(s.bufs):
            oT_tensor(k, pe, sig, lane, trip, s.a, buf)
        for lane, buf in enumerate(s.bufs):
            out_tensor(k, pe, sig, lane, trip, s.a, buf, w_of(k, st, "fc", 4), row_of(k, st, "fcb"), 4)


def L3_xattn_scalar(k, act, s):
    sig, a = s.sig, k.nc.scalar.activation
    enter(k, act, sig)
    with act.Fori(0, sig.trips) as trip:
        for lane, buf in enumerate(s.bufs):
            zT_scalar(k, act, sig, lane, trip, buf)
        for lane, buf in enumerate(s.bufs):
            act.wait_ge(*sig.at("qkv_ps", lane, trip, 1))
            a(buf.qT.rearrange("p c t -> p (c t)"), banks(k, lane, 0, 2).rearrange("p b f -> p (b f)"), ACT.Exp,
              scale=col_of(k, "sign"))
            a(buf.kT, bank(k, lane, 2).rearrange("p (c f) -> p c f", c=HC)[:, :, 0:CTX], ACT.Exp,
              scale=col_of(k, "sign"))
            v = buf.v[0:CTX, 0, :].rearrange("p (h e) -> p h e", h=H)
            v_ps = bank(k, lane, 3)[0:CTX, 0:D].rearrange("p (h e) -> p h e", h=H)
            a(v[:, :, 0:HD], v_ps, ACT.Exp)
            a(v[:, :, HD:2 * HD], v_ps, ACT.Exp, scale=-1.0).then_inc(*sig.up("q", lane))
        attention_scalar(k, act, sig, trip, s.a, s.bufs)
        for lane, buf in enumerate(s.bufs):
            oT_scalar(k, act, sig, lane, trip, s.a, buf)


def L3_xattn_vector(k, dve, s):
    sig = s.sig
    enter(k, dve, s.prep)
    norms_vector(k, dve, s.norms)
    for lane, buf in enumerate(s.bufs):
        k.nc.vector.memset(buf.v, 1.0).then_inc(*s.prep.up("done", lane))
    enter(k, dve, sig)
    with dve.Fori(0, sig.trips) as trip:
        chains = [Chain(dve, sig, lane, trip) for lane in (0, 1)]
        for lane, buf in enumerate(s.bufs):
            ln_vector(k, dve, sig, lane, trip, buf)
        attention_vector(k, dve, sig, trip, chains, s.a, s.bufs)
        for lane, buf in enumerate(s.bufs):
            residual_vector(k, dve, sig, lane, trip)
            chains[lane].close()


CYCLES = 3
GN = 4


def coupling_plan(k):
    c, bufs = lane_buffers(k)
    for buf in bufs:
        buf.o = [buf.z, c.take(2, D)]
        buf.gT, buf.g1, buf.g2, buf.g2b, buf.gf = c.take(KC), c.take(1), c.take(1), c.take(P), c.take(1)
        buf.h1, buf.h2, buf.h3, buf.tf = c.take(KC, SEQ), c.take(SEQ), c.take(SEQ), c.take(2)
        buf.c0, buf.cp, buf.cn = c.take(2), c.take(2), c.take(2)
    w = Bag(half_b=c.take(2), ar=c.take(3), zeros=c.take(P))
    norms = norms_plan(k, "L3_ffn")
    prep = Signals(k.signals, "L3_ffn", 1, 1, done=1)
    sig = Signals(k.signals, "L3_ffn", B // 2, 2, z=1, g_ps=GN, gT=GN, oT_ps=CYCLES, oT=CYCLES,
                  hid_ps=3 * CYCLES, hid=3 * CYCLES, tf_ps=CYCLES, tf=CYCLES, turn=CYCLES, done=1, stored=16,
                  dve_step=k.steps["L3_ffn"])
    return Bag(norms=norms, bufs=bufs, w=w, prep=prep, sig=sig)


def L3_ffn_tensor(k, pe, s):
    sig, mm, st = s.sig, k.nc.tensor.matmul, "L3_ffn"
    enter(k, pe, sig)
    gc1, gc2, gc3 = w_of(k, st, "gc1", KC), w_of(k, st, "gc2"), w_of(k, st, "gc3")
    cn1, cn2, cn3, cn4 = w_of(k, st, "cn1", KC), w_of(k, st, "cn2", KC), w_of(k, st, "cn3"), w_of(k, st, "cn4")
    with pe.Fori(0, sig.trips) as trip:
        for lane, buf in enumerate(s.bufs):
            g = bank(k, lane, 3)
            pe.wait_ge(*sig.at("z", lane, trip, 1))
            for c in range(KC):
                ins = products(k, g[:, c:c + 1], [(buf.z[:, t, c * P:(c + 1) * P], col_of(k, "mean"))
                                                  for t in (0, 1)])
            ins.then_inc(*sig.up("g_ps", lane))
        for lane, buf in enumerate(s.bufs):
            pe.wait_ge(*sig.at("gT", lane, trip, 1))
            products(k, bank(k, lane, 3)[:, 4:5], [(gc1[:, c, :], buf.gT[:, c:c + 1]) for c in range(KC)])\
                .then_inc(*sig.up("g_ps", lane))
        for lane, buf in enumerate(s.bufs):
            pe.wait_ge(*sig.at("gT", lane, trip, 2))
            products(k, bank(k, lane, 3)[0:64, 8:9], [(gc2, buf.g1)]).then_inc(*sig.up("g_ps", lane))
        for lane, buf in enumerate(s.bufs):
            pe.wait_ge(*sig.at("gT", lane, trip, 3))
            products(k, bank(k, lane, 3)[:, 12:13], [(buf.g2b[0:64, :], gc3[0:64, :])])\
                .then_inc(*sig.up("g_ps", lane))
        for i in range(CYCLES):
            for lane, buf in enumerate(s.bufs):
                if i:
                    pe.wait_ge(*sig.at("turn", lane, trip, i))
                transpose_z_tensor(k, pe, sig, lane, trip, buf.o[i % 2], bank(k, lane, 0))\
                    .then_inc(*sig.up("oT_ps", lane))
            for lane, buf in enumerate(s.bufs):
                pe.wait_ge(*sig.at("oT", lane, trip, i + 1))
                for c in range(KC):
                    ins = proj_feature(k, bank(k, lane, 1)[:, c * SEQ:(c + 1) * SEQ], cn1, buf.zT, c * P, P)
                ins.then_inc(*sig.up("hid_ps", lane))
            for lane, buf in enumerate(s.bufs):
                pe.wait_ge(*sig.at("hid", lane, trip, 3 * i + 1))
                proj_feature(k, bank(k, lane, 2)[:, 0:SEQ], cn2, buf.h1, 0, P).then_inc(*sig.up("hid_ps", lane))
            for lane, buf in enumerate(s.bufs):
                pe.wait_ge(*sig.at("hid", lane, trip, 3 * i + 2))
                products(k, bank(k, lane, 0)[0:64, 0:SEQ], [(cn3, buf.h2)]).then_inc(*sig.up("hid_ps", lane))
            for lane, buf in enumerate(s.bufs):
                pe.wait_ge(*sig.at("hid", lane, trip, 3 * i + 3))
                if i == 0:
                    pe.wait_ge(*sig.at("gT", lane, trip, GN))
                for t in (0, 1):
                    ins = products(k, bank(k, lane, 3)[:, t:t + 1], [(buf.h3[0:64, t * P:(t + 1) * P], cn4[0:64, :])])
                ins.then_inc(*sig.up("tf_ps", lane))


def L3_ffn_scalar(k, act, s):
    sig, a = s.sig, k.nc.scalar.activation
    enter(k, act, sig)
    with act.Fori(0, sig.trips) as trip:
        for lane, buf in enumerate(s.bufs):
            act.wait_ge(*sig.at("g_ps", lane, trip, 1))
            a(buf.gT, bank(k, lane, 3)[:, 0:KC], ACT.Copy).then_inc(*sig.up("gT", lane))
        for lane, buf in enumerate(s.bufs):
            act.wait_ge(*sig.at("g_ps", lane, trip, 2))
            a(buf.g1, bank(k, lane, 3)[:, 4:5], ACT.Gelu, bias=col_of(k, "L3_ffn_gb1")).then_inc(*sig.up("gT", lane))
        for lane, buf in enumerate(s.bufs):
            act.wait_ge(*sig.at("g_ps", lane, trip, 3))
            a(buf.g2b[0:64, :], bank(k, lane, 3)[0:64, 8:9].broadcast_to([64, P]), ACT.Gelu,
              bias=col_of(k, "L3_ffn_gb2", 0, 64)).then_inc(*sig.up("gT", lane))
        for lane, buf in enumerate(s.bufs):
            act.wait_ge(*sig.at("g_ps", lane, trip, 4))
            a(buf.gf, bank(k, lane, 3)[:, 12:13], ACT.Tanh, bias=s.w.half_b[:, 1:2], scale=0.5)\
                .then_inc(*sig.up("gT", lane))
        for i in range(CYCLES):
            for lane, buf in enumerate(s.bufs):
                act.wait_ge(*sig.at("oT_ps", lane, trip, i + 1))
                a(buf.zT.rearrange("p c t -> p (c t)"), bank(k, lane, 0), ACT.Copy).then_inc(*sig.up("oT", lane))
            for lane, buf in enumerate(s.bufs):
                act.wait_ge(*sig.at("hid_ps", lane, trip, 3 * i + 1))
                for c in range(KC):
                    ins = a(buf.h1[:, c, :], bank(k, lane, 1)[:, c * SEQ:(c + 1) * SEQ], ACT.Gelu,
                            bias=col_of(k, "L3_ffn_cb1", c))
                ins.then_inc(*sig.up("hid", lane))
            for lane, buf in enumerate(s.bufs):
                act.wait_ge(*sig.at("hid_ps", lane, trip, 3 * i + 2))
                a(buf.h2, bank(k, lane, 2)[:, 0:SEQ], ACT.Gelu, bias=col_of(k, "L3_ffn_cb2"))\
                    .then_inc(*sig.up("hid", lane))
            for lane, buf in enumerate(s.bufs):
                act.wait_ge(*sig.at("hid_ps", lane, trip, 3 * i + 3))
                a(buf.h3[0:64, :], bank(k, lane, 0)[0:64, 0:SEQ], ACT.Gelu, bias=col_of(k, "L3_ffn_cb3", 0, 64))\
                    .then_inc(*sig.up("hid", lane))
            for lane, buf in enumerate(s.bufs):
                act.wait_ge(*sig.at("tf_ps", lane, trip, i + 1))
                a(buf.tf, bank(k, lane, 3)[:, 0:2], ACT.Tanh, bias=s.w.half_b[:, 0:1], scale=0.5)\
                    .then_inc(*sig.up("tf", lane))


def L3_ffn_vector(k, dve, s):
    v, sig, w = k.nc.vector, s.sig, s.w
    enter(k, dve, s.prep)
    norms_vector(k, dve, s.norms)
    b4, b3 = scalar_of(k, "cn_b4"), scalar_of(k, "gc_b3")
    v.tensor_scalar(w.half_b[:, 0:1], b4, 0.5, None, ALU.mult)
    v.tensor_scalar(w.half_b[:, 1:2], b3, 0.5, None, ALU.mult)
    v.tensor_scalar(w.ar[:, 0:1], scalar_of(k, "ar"), 0.7, None, ALU.mult)
    v.tensor_scalar(w.ar[:, 1:2], scalar_of(k, "ar"), 0.3, None, ALU.mult).then_inc(*s.prep.up("done"))
    enter(k, dve, sig)
    with dve.Fori(0, sig.trips) as trip:
        chains = [Chain(dve, sig, lane, trip) for lane in (0, 1)]
        for lane, buf in enumerate(s.bufs):
            ln_vector(k, dve, sig, lane, trip, buf)
        for lane, buf in enumerate(s.bufs):
            ch = chains[lane]
            dve.wait_ge(*sig.at("gT", lane, trip, GN))
            ch.link(v.tensor_scalar(buf.c0[:, 0:1], buf.gf, w.ar[:, 0:1], 0.1, ALU.mult, ALU.add))
        for i in range(CYCLES):
            for lane, buf in enumerate(s.bufs):
                ch = chains[lane]
                o, n = buf.o[i % 2], buf.o[(i + 1) % 2]
                dve.wait_ge(*sig.at("tf", lane, trip, i + 1))
                ch.link(v.tensor_scalar(buf.cp, buf.tf, w.ar[:, 1:2], buf.c0[:, 0:1], ALU.mult, ALU.add))
                ch.link(v.tensor_scalar(buf.cn, buf.cp, -1.0, None, ALU.mult))
                q = D // 4
                for t in (0, 1):
                    for j, (src, c) in enumerate(((2, buf.cp), (3, buf.cn), (0, buf.cn), (1, buf.cp))):
                        ins = v.scalar_tensor_tensor(n[:, t, j * q:(j + 1) * q], o[:, t, src * q:(src + 1) * q],
                                                     c[:, t:t + 1], o[:, t, j * q:(j + 1) * q], ALU.mult, ALU.add)
                ins.then_inc(*sig.up("turn", lane))
        for lane, buf in enumerate(s.bufs):
            x = x_of(k, trip, lane)
            dve.wait_ge(*sig.at("turn", lane, trip, CYCLES))
            v.tensor_tensor(x, x, buf.o[CYCLES % 2], ALU.add).then_inc(*sig.up("done", lane))
            chains[lane].close()


def store_sync(k, sp, s, out):
    with sp.Fori(0, s.sig.trips) as trip:
        for lane in (0, 1):
            sp.wait_ge(*s.sig.at("done", lane, trip, 1))
            sp.dma_start(out[bass.ts(trip * 2 + lane, 2), :, :].rearrange("t p d -> p t d"), x_of(k, trip, lane))\
                .then_inc(s.sig.sems["stored"][lane], 16)
    for lane in (0, 1):
        sp.wait_ge(*s.sig.at("stored", lane, s.sig.trips - 1, 16))


STEPS = dict(window_mem=2, window=4, grad_mem=4, grad=3, update=2, memory=2, L0_xattn=20, L0_ffn=20, L1_attn=39,
             L1_xattn=10, fp8_prep=26, L1_ffn=11, L2_attn=4, L2_xattn=4, slots_prep=13, L2_ffn=16, L3_attn=21, L3_xattn=4,
             L3_ffn=7)


def build(nc, a):
    ctx = ExitStack()
    with ctx:
        sb = lambda name, shape, dt=F32: ctx.enter_context(nc.sbuf_tensor(name, shape, dt))
        k = Bag(nc=nc, pack={}, rows={}, spread={}, slot={}, loaded={}, steps=STEPS)
        sizes = {}
        for st in STAGES:
            k.pack[st], n = places(PACKS[st])
            rows, m = places(ROWS[st])
            k.rows[st] = {name: (at + n, w) for name, (at, w) in rows.items()}
            spread, d = places([(name, D) for name in SPREAD.get(st, [])])
            k.spread[st] = {name: (at + n + m, w) for name, (at, w) in spread.items()}
            sizes[st] = (n, m, d)
        slot_size = [max(sum(sizes[st]) for st in STAGES[i::2]) for i in (0, 1)]
        slots = [sb(f"weights_{i}", [P, slot_size[i]]) for i in (0, 1)]
        for i, st in enumerate(STAGES):
            k.slot[st] = slots[i % 2]
        k.x = sb("x", [P, TILES, D])
        k.norm, k.stats = sb("norm", [P, TILES, 2]), sb("stats", [P, TILES * 6])
        k.rstd, k.var, k.newton = (sb(n, [P, TILES])[:, :] for n in ("rstd", "var", "newton"))
        k.ctxT = sb("ctxT", [P, KC, B * CTX])
        k.ident, k.identb = sb("ident", [P, P]), sb("identb", [P, P], BF16)
        k.maskpos, n = places(MASKS)
        k.masks = sb("masks", [P, n], BF16)
        k.colpos, n = places(COLS)
        k.cols = sb("cols", [P, n])
        k.scalars = sb("scalars", [P, len(SCALARS)])
        k.earlier = sb("earlier", [P, 64])
        k.ones = sb("ones", [1, SEQ])
        k.fp8_kernel_t, k.fp8_bias_t = sb("fp8_kernel", [P, KC * D], BF16), sb("fp8_bias", [P, D], BF16)
        k.fp8_kernel, k.fp8_bias = k.fp8_kernel_t[:, :], k.fp8_bias_t[:, :]
        k.earlier = k.earlier[:, :]
        k.arena_size = ARENA
        k.arena = sb("arena", [P, ARENA])
        k.ps = ctx.enter_context(nc.psum_tensor("ps", [P, 8, 512], F32))
        k.signals = SignalPool(nc, ctx)
        k.signals.lanes("done", 2)
        sem = lambda name: ctx.enter_context(nc.semaphore(name))
        k.held = {e: sem("held_" + e) for e in ("vector", "gpsimd", "tensor")}
        x_loaded, const_loaded, k.mem_loaded = sem("x_loaded"), sem("const_loaded"), sem("mem_loaded")
        slot_loaded = [sem(f"weights_{i}_loaded") for i in (0, 1)]
        total = [0, 0]
        loads = {}
        for i, st in enumerate(STAGES):
            n, m, d = sizes[st]
            loads[st] = (n > 0) + (m > 0) + len(SPREAD.get(st, []))
            total[i % 2] += 16 * loads[st]
            k.loaded[st] = (slot_loaded[i % 2], total[i % 2])

        s = {}
        s["L0_attn"] = memory_plan(k)
        s["L0_xattn"] = xattn_plan(k, "L0_xattn", True)
        s["L0_ffn"] = experts_plan(k)
        s["L1_attn"] = block_plan(k)
        s["L1_xattn"] = two_attentions_plan(k)
        s["L1_ffn"] = fp8_plan(k)
        s["L2_attn"] = width_one_plan(k)
        s["L2_xattn"] = xattn_plan(k, "L2_xattn", False)
        s["L2_ffn"] = slots_plan(k)
        s["L3_attn"] = scan_plan(k)
        s["L3_xattn"] = features_plan(k)
        s["L3_ffn"] = coupling_plan(k)
        last = {st: (s[st].memory if st == "L0_attn" else s[st].sig) for st in STAGES}
        constants = [(k.ctxT, "ctxT"), (k.ident, "ident"), (k.identb, "identb"), (k.masks, "masks"), (k.cols, "cols"),
                     (k.ones, "ones"), (k.fp8_kernel_t, "fp8_kernel")]
        n_const = 16 * (len(constants) + 3)
        buf0 = s["L0_attn"].buf
        block = ctx.enter_context(nc.Block())

        @block.sync
        def _(sp):
            def load(st):
                i = STAGES.index(st)
                if i >= 2:
                    sig = last[STAGES[i - 2]]
                    for lane in range(2):
                        sp.wait_ge(sig.sems["done"][lane], sig.ends[lane])
                n, m, _ = sizes[st]
                sem, _ = k.loaded[st]
                if n:
                    sp.dma_start(k.slot[st][:, 0:n], a["w_" + st][:, :]).then_inc(sem, 16)
                if m:
                    sp.dma_start(k.slot[st][0:1, n:n + m], a["r_" + st][:, :]).then_inc(sem, 16)
                for name in SPREAD.get(st, []):
                    sp.dma_start(spread_of(k, st, name), a["L1_attn_" + name].unsqueeze(0).broadcast_to([P, D]))\
                        .then_inc(sem, 16)

            sp.dma_start(k.x[:, :, :], a["x"].rearrange("t p d -> p t d")).then_inc(x_loaded, 16)
            load("L0_attn")
            sp.dma_start(buf0.zT_all[:, :, B * SEQ:B * SEQ + MEM], a["memT"].rearrange("(c p) t -> p c t", p=P))\
                .then_inc(k.mem_loaded, 16)
            sp.dma_start(buf0.z_all[0:MEM, TILES * D:(TILES + 1) * D], a["mem"][:, :]).then_inc(k.mem_loaded, 16)
            for tile, name in constants:
                dst = tile[:, :, :] if name == "ctxT" else tile[:, :]
                src = a[name].rearrange("(c p) t -> p c t", p=P) if name == "ctxT" else a[name][:, :]
                sp.dma_start(dst, src).then_inc(const_loaded, 16)
            sp.dma_start(k.earlier, a["earlier"].broadcast_to([P, 64])).then_inc(const_loaded, 16)
            sp.dma_start(k.scalars[:, :], a["scalars"].broadcast_to([P, len(SCALARS)])).then_inc(const_loaded, 16)
            sp.dma_start(k.fp8_bias, a["fp8_bias"].unsqueeze(0).broadcast_to([P, D])).then_inc(const_loaded, 16)
            for i, st in enumerate(STAGES):
                if i + 1 < len(STAGES):
                    load(STAGES[i + 1])
                if st == "L2_attn":
                    L2_attn_sync(k, sp, s[st])
            store_sync(k, sp, s["L3_ffn"], a["out"])

        @block.gpsimd
        def _(pool):
            pool.wait_ge(const_loaded, n_const)
            L0_attn_gpsimd(k, pool, s["L0_attn"])
            xattn_gpsimd(k, pool, s["L0_xattn"])
            xattn_gpsimd(k, pool, s["L1_xattn"])
            xattn_gpsimd(k, pool, s["L2_xattn"])
            xattn_gpsimd(k, pool, s["L3_xattn"])

        @block.tensor
        def _(pe):
            pe.wait_ge(const_loaded, n_const)
            L0_attn_tensor(k, pe, s["L0_attn"])
            xattn_tensor(k, pe, s["L0_xattn"])
            L0_ffn_tensor(k, pe, s["L0_ffn"])
            L1_attn_tensor(k, pe, s["L1_attn"])
            L1_xattn_tensor(k, pe, s["L1_xattn"])
            L1_ffn_tensor(k, pe, s["L1_ffn"])
            L2_attn_tensor(k, pe, s["L2_attn"])
            xattn_tensor(k, pe, s["L2_xattn"])
            L2_ffn_tensor(k, pe, s["L2_ffn"])
            L3_attn_tensor(k, pe, s["L3_attn"])
            L3_xattn_tensor(k, pe, s["L3_xattn"])
            L3_ffn_tensor(k, pe, s["L3_ffn"])

        @block.scalar
        def _(act):
            act.wait_ge(const_loaded, n_const)
            L0_attn_scalar(k, act, s["L0_attn"])
            xattn_scalar(k, act, s["L0_xattn"])
            L0_ffn_scalar(k, act, s["L0_ffn"])
            L1_attn_scalar(k, act, s["L1_attn"])
            L1_xattn_scalar(k, act, s["L1_xattn"])
            L1_ffn_scalar(k, act, s["L1_ffn"])
            L2_attn_scalar(k, act, s["L2_attn"])
            xattn_scalar(k, act, s["L2_xattn"])
            L2_ffn_scalar(k, act, s["L2_ffn"])
            L3_attn_scalar(k, act, s["L3_attn"])
            L3_xattn_scalar(k, act, s["L3_xattn"])
            L3_ffn_scalar(k, act, s["L3_ffn"])

        @block.vector
        def _(dve):
            dve.wait_ge(x_loaded, 16)
            dve.wait_ge(const_loaded, n_const)
            L0_attn_vector(k, dve, s["L0_attn"])
            xattn_vector(k, dve, s["L0_xattn"])
            L0_ffn_vector(k, dve, s["L0_ffn"])
            L1_attn_vector(k, dve, s["L1_attn"])
            L1_xattn_vector(k, dve, s["L1_xattn"])
            L1_ffn_vector(k, dve, s["L1_ffn"])
            L2_attn_vector(k, dve, s["L2_attn"])
            xattn_vector(k, dve, s["L2_xattn"])
            L2_ffn_vector(k, dve, s["L2_ffn"])
            L3_attn_vector(k, dve, s["L3_attn"])
            L3_xattn_vector(k, dve, s["L3_xattn"])
            L3_ffn_vector(k, dve, s["L3_ffn"])


ARENA = 27000


def layouts(i):
    import numpy as np

    i = {n: np.asarray(v) for n, v in i.items()}
    f32, bf16 = np.float32, i["L1_ffn_kernel"].dtype

    def chunks(w):
        n = w.shape[0] // P
        return w.reshape(n, P, -1).transpose(1, 0, 2).reshape(P, -1)

    def padded(w):
        out = np.zeros((w.shape[0], H, PAD), f32)
        out[:, :, 0:HD] = w.reshape(w.shape[0], H, HD)
        return out.reshape(w.shape[0], H * PAD)

    def widened(w, heads, e):
        out = np.zeros((w.shape[0], heads, e + 1), f32)
        out[:, :, 0:e] = w.reshape(w.shape[0], heads, e)
        return out.reshape(w.shape[0], heads * (e + 1))

    def with_ones(b, heads, e):
        out = np.ones((heads, e + 1), f32)
        out[:, 0:e] = b.reshape(heads, e)
        return out.reshape(-1)

    def low(w):
        out = np.zeros((P, w.shape[1]), f32)
        out[0:w.shape[0]] = w
        return out

    heads = lambda w: w.transpose(1, 0, 2).reshape(D, H * HD)
    g = lambda st, n: i[f"{st}_{n}"]
    a = {}

    def put(st, **w):
        parts = [w[n] for n, _ in PACKS[st]]
        for (n, c), p in zip(PACKS[st], parts):
            assert p.shape == (P, c), (st, n, p.shape, c)
        if parts:
            a["w_" + st] = np.ascontiguousarray(np.concatenate(parts, 1), f32)

    def put_rows(st, **r):
        parts = [r[n].reshape(-1) for n, _ in ROWS[st]]
        for (n, c), p in zip(ROWS[st], parts):
            assert p.shape == (c,), (st, n, p.shape, c)
        a["r_" + st] = np.ascontiguousarray(np.concatenate(parts)[None], f32)

    st = "L0_attn"
    put(st, wq=chunks(g(st, "wq").T), wk=chunks(g(st, "wk").T), wv=chunks(widened(g(st, "wv").T, SH, SD_)),
        wo=chunks(g(st, "wo").T), lin1=chunks(g(st, "lin1").T), lin2=chunks(g(st, "lin2").T),
        w1T=chunks(g(st, "w1").T), w2T=chunks(g(st, "w2").T), w2=chunks(g(st, "w2")))
    put_rows(st, v1=with_ones(np.zeros(D, f32), SH, SD_), b1=g(st, "b1"), b2=g(st, "b2"))
    for st in ("L0_xattn", "L2_xattn"):
        put(st, wq=chunks(padded(g(st, "Wq").T)), wk=chunks(padded(g(st, "Wk").T)),
            wv=chunks(widened(g(st, "Wv").T, H, HD)), wo=chunks(g(st, "Wo").T))
        put_rows(st, bv=with_ones(g(st, "bv"), H, HD), bo=g(st, "bo"))
    st = "L0_ffn"
    up = lambda n: np.concatenate([chunks(w) for w in list(g(st, "routed_" + n)) + list(g(st, "shared_" + n))], 1)
    put(st, router=chunks(g(st, "router_w")), w1=up("w1"), w3=up("w3"), w2=up("w2"))
    put_rows(st, rb=g(st, "router_b"))
    st = "L1_attn"
    put(st, wq=chunks(padded(heads(g(st, "q_proj")))), wk=chunks(padded(heads(g(st, "k_proj")))),
        wv=chunks(widened(heads(g(st, "v_proj")), H, HD)), ff1=chunks(g(st, "ff1_w")), ff2=chunks(g(st, "ff2_w")))
    put_rows(st, bv=with_ones(g(st, "v_bias"), H, HD), ff2b=g(st, "ff2_b"))
    for n in SPREAD[st]:
        a[f"{st}_{n}"] = g(st, n)
    st = "L1_xattn"
    w = {}
    for n in "12":
        w["wq" + n], w["wk" + n] = (chunks(padded(heads(g(st, W + n)))) for W in ("Wq", "Wk"))
        w["wv" + n], w["wo" + n] = chunks(widened(heads(g(st, "Wv" + n)), H, HD)), chunks(g(st, "Wo" + n))
    put(st, **w)
    put_rows(st, bv1=with_ones(g(st, "bv1"), H, HD), bv2=with_ones(g(st, "bv2"), H, HD), bo2=g(st, "bo2"))
    st = "L2_attn"
    put(st, wqkv=chunks(g(st, "w_qkv").T), wout=low(g(st, "w_out").T))
    st = "L2_ffn"
    put(st, slots=chunks(g(st, "slot_embeds").reshape(SLOTS, D)), w1=chunks(g(st, "w1")), w2=chunks(g(st, "w2")))
    st = "L3_attn"
    put(st, wa=chunks(g(st, "Wa").T), wb=chunks(g(st, "Wb").T), wc=chunks(g(st, "Wc").T))
    st = "L3_xattn"
    fm, fb = g(st, "fm_w"), g(st, "fm_b")
    wf, wv = np.zeros((H, HD, H, 2, HD), f32), np.zeros((H, HD, H, HD), f32)
    for h in range(H):
        wf[h, :, h, 0], wf[h, :, h, 1], wv[h, :, h] = fm.T, fm.T, fm.T
    put(st, wf=chunks(wf.reshape(D, H * PAD)), wv=chunks(wv.reshape(D, D)), fc=chunks(g(st, "fc_w").T))
    put_rows(st, bf=np.tile(fb, 2 * H), bv=np.tile(fb, H), fcb=g(st, "fc_b"))
    st = "L3_ffn"
    put(st, cn1=chunks(g(st, "cn_w1")), cn2=chunks(g(st, "cn_w2")), cn3=low(g(st, "cn_w3")), cn4=low(g(st, "cn_w4")),
        gc1=chunks(g(st, "gc_w1")), gc2=low(g(st, "gc_w2")), gc3=low(g(st, "gc_w3")))

    col = lambda b: b.reshape(-1, P).T
    pad_col = lambda b: col(padded(b.reshape(1, D)).reshape(-1))
    c = {"L0_attn_b1": col(i["L0_attn_b1"]), "L1_attn_bq": pad_col(i["L1_attn_q_bias"]),
         "L1_attn_bk": pad_col(i["L1_attn_k_bias"]), "L1_attn_ff1b": col(i["L1_attn_ff1_b"]),
         "L1_xattn_bo1": col(i["L1_xattn_bo1"]), "L2_ffn_gx": col(i["L2_ffn_gamma_x"]),
         "L2_ffn_gs": col(i["L2_ffn_gamma_slot"]), "L3_attn_g": col(i["L3_attn_gamma"]),
         "L3_attn_be": col(i["L3_attn_beta"]), "L3_attn_h0": col(i["L3_attn_h0"]),
         "sign": np.where(np.arange(P) % PAD < HD, 1.0, -1.0)[:, None], "mean": np.full((P, 1), 1.0 / SEQ),
         "one": np.ones((P, 1))}
    for n in ("L0_xattn_bq", "L0_xattn_bk", "L1_xattn_bq1", "L1_xattn_bk1", "L1_xattn_bq2", "L1_xattn_bk2",
              "L2_xattn_bq", "L2_xattn_bk"):
        c[n] = pad_col(i[n])
    for n in ("ba", "bb", "bc"):
        c["L3_attn_" + n] = col(i["L3_attn_" + n])
    for n, src in (("cb1", "cn_b1"), ("cb2", "cn_b2"), ("cb3", "cn_b3"), ("gb1", "gc_b1"), ("gb2", "gc_b2")):
        b = i["L3_ffn_" + src]
        c["L3_ffn_" + n] = low(b[:, None]) if b.shape[0] < P else col(b)
    a["cols"] = np.ascontiguousarray(np.concatenate([c[n] for n, _ in COLS], 1), f32)
    assert a["cols"].shape[1] == sum(n for _, n in COLS)
    sc = {"alpha": "L0_attn_alpha", "theta": "L0_attn_theta", "s_in": "L1_ffn_input_scale",
          "s_k": "L1_ffn_kernel_scale", "cn_b4": "L3_ffn_cn_b4", "gc_b3": "L3_ffn_gc_b3",
          "ar": "L3_ffn_adaptive_range"}
    a["scalars"] = np.ascontiguousarray(np.concatenate([i[sc[n]].reshape(1, 1) for n in SCALARS], 1), f32)
    a["fp8_kernel"] = np.ascontiguousarray(chunks(i["L1_ffn_kernel"]))
    a["fp8_bias"] = i["L1_ffn_bias"]
    a["x"] = i["x"].reshape(TILES, P, D)
    a["ctxT"] = np.ascontiguousarray(i["ctx_1024"].reshape(B * CTX, D).T)
    a["mem"], a["memT"] = i["L0_attn_mem"], np.ascontiguousarray(i["L0_attn_mem"].T)

    a["ident"] = np.eye(P, dtype=f32)
    a["identb"] = np.eye(P).astype(bf16)
    a["ones"] = np.ones((1, SEQ), f32)
    a["earlier"] = np.tril(np.ones((8, 8), f32), -1).reshape(1, 64)
    r, q = np.arange(P)[:, None], np.arange(P)[None, :]
    seen, all_, m = q <= r, np.ones((P, P), bool), np.arange(MEM)[None, :]
    ahead = {"selfA": [seen] * 4, "selfB": [all_, seen] * 2, "keyA": [seen.T, all_] * 2, "keyC": [seen.T] * 4,
             "swa0": [m > r - MEM, seen] * 2, "swa1": [q > r, seen] * 2, "swam": [m <= r] * 2}
    mask = np.concatenate([np.concatenate(ahead[n], 1) for n, _ in MASKS], 1)
    a["masks"] = np.where(mask, 0.0, -1e30).astype(bf16)
    return a


def kernel(**inputs):
    import concourse.bacc as bacc
    from concourse.bass_utils import run_bass_kernel_spmd

    nc = bacc.Bacc("TRN2", target_bir_lowering=False, num_devices=1)
    arrays, args = {}, {}
    for name, v in layouts(inputs).items():
        arrays["in_" + name] = v
        args[name] = nc.dram_tensor("in_" + name, v.shape, mybir.dt.from_np(v.dtype), kind="ExternalInput").ap()
    args["out"] = nc.dram_tensor("out", (TILES, P, D), F32, kind="ExternalOutput").ap()
    build(nc, args)
    result = run_bass_kernel_spmd(nc, [arrays], core_ids=[0])
    return result.results[0]["out"].reshape(B, SEQ, D)
```

```python
from contextlib import ExitStack

import concourse.bass as bass
from concourse import mybir

F32 = mybir.dt.float32
BF16 = mybir.dt.bfloat16
U32 = mybir.dt.uint32
I32 = mybir.dt.int32
ALU = mybir.AluOpType
ACT = mybir.ActivationFunctionType
AX = mybir.AxisListType.X

P = 128
B, SEQ, D = 8, 256, 256
TILES = B * SEQ // P
SPARE = 4
KC = D // P
CTX = 77
H, HD, PAD = 16, 16, 32
HC = H // 4
VW = HD + 1
MEM, SH, SD_ = 64, 4, 64
SVW = SD_ + 1
HID = 1024
E_ROUTED, E_ALL, EH = 8, 10, 128
FF = 512
SLOTS, E_SLOT_HID = 1024, 1024
TOPK = 32
NH1 = 64
LN_EPS = 1e-5
BIG = 3.0e38

PACKS = {
    "L0_attn": [("wq", KC * D), ("wk", KC * D), ("wv", KC * SH * SVW), ("wo", KC * D), ("lin1", KC * D),
                ("lin2", KC * D), ("w1T", KC * HID), ("w2T", HID // P * D), ("w2", KC * HID)],
    "L0_xattn": [("wq", KC * H * PAD), ("wk", KC * H * PAD), ("wv", KC * H * VW), ("wo", KC * D)],
    "L0_ffn": [("router", KC * E_ROUTED), ("w1", E_ALL * KC * EH), ("w3", E_ALL * KC * EH), ("w2", E_ALL * D)],
    "L1_attn": [("wq", KC * H * PAD), ("wk", KC * H * PAD), ("wv", KC * H * VW), ("ff1", KC * FF),
                ("ff2", FF // P * D)],
    "L1_xattn": [(w + n, c) for n in "12" for w, c in (("wq", KC * H * PAD), ("wk", KC * H * PAD),
                                                       ("wv", KC * H * VW), ("wo", KC * D))],
    "L1_ffn": [],
    "L2_attn": [("wqkv", KC * 3 * NH1), ("wout", D)],
    "L2_xattn": [("wq", KC * H * PAD), ("wk", KC * H * PAD), ("wv", KC * H * VW), ("wo", KC * D)],
    "L2_ffn": [("slots", SLOTS // P * D), ("w1", KC * E_SLOT_HID), ("w2", E_SLOT_HID // P * D)],
    "L3_attn": [("wa", KC * D), ("wb", KC * D), ("wc", KC * D)],
    "L3_xattn": [("wf", KC * H * PAD), ("wv", KC * D), ("fc", 4 * D)],
    "L3_ffn": [("cn1", KC * D), ("cn2", KC * 128), ("cn3", 64), ("cn4", 1), ("gc1", KC * 128), ("gc2", 64),
               ("gc3", 1)],
}
ROWS = {
    "L0_attn": [("v1", SH * SVW), ("b1", HID), ("b2", D)],
    "L0_xattn": [("bv", H * VW), ("bo", D)],
    "L0_ffn": [("rb", E_ROUTED)],
    "L1_attn": [("bv", H * VW), ("ff2b", D)],
    "L1_xattn": [("bv1", H * VW), ("bv2", H * VW), ("bo2", D)],
    "L1_ffn": [], "L2_attn": [],
    "L2_xattn": [("bv", H * VW), ("bo", D)],
    "L2_ffn": [], "L3_attn": [],
    "L3_xattn": [("bf", H * PAD), ("bv", D), ("fcb", D)],
    "L3_ffn": [],
}
SPREAD = {"L1_attn": ["ln1_g", "ln1_b", "ln2_g", "ln2_b"]}
STAGES = list(PACKS)
COLS = [("L0_attn_b1", 8), ("L0_xattn_bq", HC), ("L0_xattn_bk", HC), ("L1_attn_bq", HC), ("L1_attn_bk", HC),
        ("L1_attn_ff1b", 4), ("L1_xattn_bq1", HC), ("L1_xattn_bk1", HC), ("L1_xattn_bo1", KC),
        ("L1_xattn_bq2", HC), ("L1_xattn_bk2", HC), ("L2_xattn_bq", HC), ("L2_xattn_bk", HC),
        ("L2_ffn_gx", KC), ("L2_ffn_gs", KC), ("L3_attn_ba", KC), ("L3_attn_bb", KC), ("L3_attn_bc", KC),
        ("L3_attn_g", KC), ("L3_attn_be", KC), ("L3_attn_h0", KC), ("L3_ffn_cb1", KC), ("L3_ffn_cb2", 1),
        ("L3_ffn_cb3", 1), ("L3_ffn_gb1", 1), ("L3_ffn_gb2", 1), ("sign", 1), ("mean", 1), ("one", 1)]
SCALARS = ["alpha", "theta", "s_in", "s_k", "cn_b4", "gc_b3", "ar"]
MASKS = [("selfA", 512), ("selfB", 512), ("keyA", 512), ("keyC", 512), ("swa0", 2 * (MEM + P)), ("swa1", 512),
         ("swam", 2 * MEM)]


def Bag(**things):
    return type("Bag", (), things)


def places(fields):
    at, out = 0, {}
    for name, n in fields:
        out[name] = (at, n)
        at += n
    return out, at


COMMON = ("done", "dve_step", "z", "zT_ps", "zT", "qkv_ps", "q", "kv", "s_ps", "s_sb", "prob", "probT_ps", "probT_a",
          "probT_v", "o_ps", "raw", "back_ps", "o", "oT_ps", "oT", "out_ps", "ctx")


class SignalPool:

    def __init__(self, nc, ctx):
        self.nc, self.ctx, self.sems, self.raised, self.own = nc, ctx, {}, {}, {}

    def called(self, stage, name):
        if name in COMMON:
            return name
        own = self.own.setdefault(stage, {})
        return own.setdefault(name, f"of_stage_{len(own)}")

    def lanes(self, name, n):
        sems = self.sems.setdefault(name, [])
        while len(sems) < n:
            sems.append(self.ctx.enter_context(self.nc.semaphore(f"{name}_{len(sems)}")))
        self.raised.setdefault(name, [0, 0])
        return sems


class Signals:

    def __init__(self, pool, stage, trips, lanes, ahead=(), **per):
        self.stage, self.trips, self.lanes, self.per = stage, trips, lanes, per
        at = {n: pool.called(stage, n) for n in per}
        self.sems = {n: pool.lanes(at[n], lanes) for n in per}
        self.before = [(sem, value) for n in ("done", "zT") if n in pool.sems
                       for sem, value in zip(pool.sems[n], pool.raised[n]) if value]
        self.base = {n: list(pool.raised[at[n]]) for n in per}
        for n, k in per.items():
            for lane in range(lanes):
                pool.raised[at[n]][lane] += trips * k + (n in ahead)
        self.ends = [pool.raised["done"][lane] for lane in (0, 1)]

    def up(self, name, lane=0):
        return self.sems[name][lane], 1

    def at(self, name, lane, trip, n):
        k = self.per[name]
        assert n <= k, (self.stage, name, n, k)
        return self.sems[name][lane], trip * k + (self.base[name][lane] + n)


class Chain:

    def __init__(self, eng, sig, lane, trip):
        self.eng, self.sig, self.lane, self.trip, self.n = eng, sig, lane, trip, 0

    def link(self, ins):
        self.n += 1
        ins.then_inc(*self.sig.up("dve_step", self.lane))
        self.eng.wait_ge(*self.sig.at("dve_step", self.lane, self.trip, self.n))

    def close(self):
        assert self.n == self.sig.per["dve_step"], (self.sig.stage, self.n)


def cut(ap, **sizes):
    (name, n), = sizes.items()
    return ap.rearrange(f"p ({name} f) -> p {name} f", **{name: n})


class Carve:

    def __init__(self, tensor, size):
        self.tensor, self.size, self.at = tensor, size, 0

    def take(self, *shape, dt=None):
        n = 1
        for s in shape:
            n *= s
        words = n if dt is None else (n + 1) // 2
        ap = self.tensor[:, self.at:self.at + words]
        self.at += words
        assert self.at <= self.size, (self.at, self.size)
        if dt is not None:
            ap = ap.bitcast(dt)
        if len(shape) == 2:
            ap = ap.rearrange("p (a b) -> p a b", a=shape[0])
        if len(shape) == 3:
            ap = ap.rearrange("p (a b c) -> p a b c", a=shape[0], b=shape[1])
        return ap



def enter(k, eng, sig):
    for sem, value in sig.before:
        eng.wait_ge(sem, value)
    sem, value = k.loaded[sig.stage]
    if value:
        eng.wait_ge(sem, value)


def hold(k, eng, name):
    eng.sem_inc(k.held[name], 1)


def x_of(k, trip, lane, lanes=2):
    return k.xs[:, bass.ts(trip * lanes + (lane + SPARE // 2), 2), :]


def bank(k, lane, i):
    return k.ps[:, 4 * lane + i, :]


def banks(k, lane, i, n):
    return k.ps[:, 4 * lane + i:4 * lane + i + n, :]


def w_of(k, stage, name, rows=None):
    at, n = k.pack[stage][name]
    ap = k.slot[stage][:, at:at + n]
    return ap if rows is None else ap.rearrange("p (r n) -> p r n", r=rows)


def row_of(k, stage, name):
    at, n = k.rows[stage][name]
    return k.rowslot[stage][0:1, at:at + n]


def spread_of(k, stage, name):
    at, n = k.spread[stage][name]
    return k.slot[stage][:, at:at + n]


def col_of(k, name, c=0, parts=P):
    at, _ = k.colpos[name]
    return k.cols[0:parts, at + c:at + c + 1]


def scalar_of(k, name, parts=P):
    i = SCALARS.index(name)
    return k.scalars[0:parts, i:i + 1]


def mask_of(k, name):
    at, n = k.maskpos[name]
    return k.masks[:, at:at + n]


RSQRT_STEPS = 10
RSQRT_GUESS = float(0x5F3759DF)


def rsqrt(k, link, y, v, t):
    dve = k.nc.vector
    link(dve.tensor_scalar(y.bitcast(I32), v.bitcast(I32), -0.5, RSQRT_GUESS, ALU.mult, ALU.add))
    for _ in range(3):
        link(dve.scalar_tensor_tensor(t, y, -0.5, y, ALU.mult, ALU.mult))
        link(dve.tensor_tensor(t, t, v, ALU.mult))
        link(dve.scalar_tensor_tensor(y, t, 1.5, y, ALU.add, ALU.mult))


def layernorm(k, ch, src, dst, st):
    v = k.nc.vector
    for t in (0, 1):
        ins = v.bn_stats(st[:, 6 * t:6 * t + 6], src[:, t, :])
    ch.link(ins)
    hold(k, ch.eng, "vector")
    for t in (0, 1):
        ins = v.bn_aggr(st[:, 12 + 2 * t:14 + 2 * t], st[:, 6 * t:6 * t + 6])
    ch.link(ins)
    ch.link(v.tensor_scalar(st[:, 16:18], st[:, 13:16:2], LN_EPS, None, ALU.add))
    rsqrt(k, ch.link, st[:, 18:20], st[:, 16:18], st[:, 20:22])
    for t in (0, 1):
        ins = v.tensor_scalar(dst[:, t, :], src[:, t, :], st[:, 12 + 2 * t:13 + 2 * t], st[:, 18 + t:19 + t],
                              ALU.subtract, ALU.mult)
    return ins


def norms_plan(k, stage):
    return Bag(sig=Signals(k.signals, stage, 1, 1, dve_step=3 + RSQRT_STEPS),
               fresh=TILES if stage == "L0_attn" else 2 if stage == "L3_attn" else 4)


def stats_vector(k, dve, sig, lane, trip, lanes=2):
    tile = trip * (2 * lanes) + (2 * lane + SPARE - 2 * lanes)
    dve.wait_ge(*sig.at("done", lane, trip, 0))
    hold(k, dve, "vector")
    for t in (0, 1):
        k.nc.vector.bn_stats(k.stats[:, bass.ds((tile + t) * 6, 6)], k.xs[:, bass.ds(tile + t, 1), :].squeeze(1))


def norms_vector(k, dve, s):
    v = k.nc.vector
    ch = Chain(dve, s.sig, 0, 0)
    hold(k, dve, "vector")
    of = lambda t: k.stats[:, 6 * (SPARE + t):6 * (SPARE + t + 1)]
    for t in range(TILES - s.fresh, TILES):
        ins = v.bn_stats(of(t), k.xs[:, SPARE + t, :])
    ch.link(ins)
    hold(k, dve, "vector")
    for t in range(TILES):
        ins = v.bn_aggr(k.norm[:, t, :], of(t))
    ch.link(ins)
    ch.link(v.tensor_scalar(k.var, k.norm[:, 0:TILES, 1:2].rearrange("p t o -> p (t o)"), LN_EPS, None, ALU.add))
    rsqrt(k, ch.link, k.rstd[:, 0:TILES], k.var, k.newton)
    ch.close()


def ln_apply(k, trip, lane, lanes, dst):
    x, tiles = x_of(k, trip, lane, lanes), bass.ts(trip * lanes + lane, 2)
    norm, rstd = k.norm[:, tiles, :], k.rstd[:, tiles]
    for t in (0, 1):
        ins = k.nc.vector.tensor_scalar(dst[:, t, :], x[:, t, :], norm[:, t, 0:1], rstd[:, t:t + 1], ALU.subtract,
                                        ALU.mult)
    return ins


def ln_vector(k, dve, sig, lane, trip, buf):
    dve.wait_ge(*sig.at("done", lane, trip, 0))
    hold(k, dve, "vector")
    ln_apply(k, trip, lane, 2, buf.z).then_inc(*sig.up("z", lane))


def next_z_vector(k, sig, lane, trip, buf):
    ln_apply(k, trip, lane, 2, buf.z).then_inc(*sig.up("z", lane))


def first_z_vector(k, sig, bufs):
    for lane, buf in enumerate(bufs):
        next_z_vector(k, sig, lane, 0, buf)


def later_z_vector(k, dve, sig, bufs, trip):
    for lane, buf in enumerate(bufs):
        dve.wait_ge(*sig.at("zT_ps", lane, trip, 1))
        hold(k, dve, "vector")
        next_z_vector(k, sig, lane, trip + 1, buf)


def transpose_z_tensor(k, pe, sig, lane, trip, src, out):
    for c in range(KC):
        for t in (0, 1):
            ins = k.nc.tensor.transpose(out[:, (2 * c + t) * P:(2 * c + t + 1) * P], src[:, t, c * P:(c + 1) * P],
                                        k.ident[:, :])
    return ins


def products(k, out, pairs, row=None, start=True):
    n = len(pairs) + (row is not None)
    for i, (lhsT, rhs) in enumerate(pairs):
        ins = k.nc.tensor.matmul(out, lhsT, rhs, start=start and i == 0, stop=i == n - 1)
    if row is not None:
        ins = k.nc.tensor.matmul(out, k.ones[0:1, 0:out.shape[0]], row, start=False, stop=True)
    return ins


def proj_feature(k, out, w, src, cols, n):
    return products(k, out, [(w[:, c, cols:cols + n], src[:, c, :]) for c in range(KC)])


def proj_token(k, out, src, t, w, row=None, kc=KC):
    return products(k, out, [(src[:, c, t:t + P], w[:, c, :]) for c in range(kc)], row)



CROSS = [(0, (0, 1, 2, 3), 1), (1, (0, 1, 2, 3), 1)]
SELF = [(0, (0, 1, 2, 3), 1), (1, (0, 1), 2), (1, (2, 3), 2)]


def attention(kind, p="", width=HD, scale=0.25, topk=False):
    return Bag(p=p, rounds=SELF if kind == "self" else CROSS, causal=kind == "self", width=width,
               ones=width < PAD, vw=width + (width < PAD), nk=P if kind == "self" else CTX, scale=scale, topk=topk)


def attention_signals(a):
    n = len(a.rounds)
    per = {"s_ps": 2 * n, "s_sb": 2 * n, "prob": 2 * n}
    if a.topk:
        per.update(left=2 * n)
    per.update({s: n for s in ("probT_ps", "probT_a", "probT_v", "o_ps", "raw", "back_ps", "o")})
    return {a.p + s: count for s, count in per.items()}


def attention_buffers(c, a, buf):
    nkb = 2 if a.causal else 1
    buf.qT = c.take(HC, SEQ)
    buf.kT = c.take(HC, SEQ if a.causal else 4 * CTX)
    buf.v = c.take(nkb, H * a.vw)
    buf.s = c.take(4, 512)
    buf.probT = c.take(4, 512)
    buf.raw = c.take(HC, P)
    buf.o = c.take(2, H * a.width)
    buf.oT = c.take(H * a.width // P, SEQ)
    buf.m, buf.rec, buf.sums = c.take(H), c.take(H), c.take(H)
    if a.topk:
        buf.left = c.take(4, 512)
        buf.top = c.take(H, 4 * 8)


def scores_tensor(k, pe, sig, lane, trip, a, buf, r, banks_):
    t, chunks, nkb = a.rounds[r]
    nk = nkb * a.nk
    if r and 1 in banks_:
        pe.wait_ge(*sig.at(a.p + "o", lane, trip, r))
    if a.causal:
        for i in banks_:
            k.nc.tensor.matmul(bank(k, lane, i), k.identb[:, :], mask_of(k, "selfA" if nkb == 1 else "selfB"),
                               start=True, stop=False, skip_group_check=True)
    if not a.causal:
        for c in banks_:
            ins = k.nc.tensor.matmul(cut(bank(k, lane, c), head=4)[:, :, 0:nk], buf.qT[:, c, t * P:(t + 1) * P],
                                     buf.kT[:, c, :].rearrange("p (h j) -> p h j", h=4), start=True, stop=True)
        return ins
    for ci, c in enumerate(chunks):
        for i in banks_:
            at = ci * nkb * P
            ins = k.nc.tensor.matmul(bank(k, lane, i)[:, at:at + nk],
                                     buf.qT[PAD * i:PAD * (i + 1), c, t * P:(t + 1) * P],
                                     buf.kT[PAD * i:PAD * (i + 1), c, 0:nk],
                                     start=False, stop=True, skip_group_check=True)
    return ins


def half_views(k, lane, a, buf, r, lo):
    t, chunks, nkb = a.rounds[r]
    n = len(chunks)
    view = lambda ap: ap.rearrange("p b (c f) -> p (b c) f", c=n)[:, :, 0:nkb * a.nk]
    return view(banks(k, lane, lo, 2)), view(buf.s[:, lo:lo + 2, :]), slice(lo * n, (lo + 2) * n)


def max_vector(k, dve, sig, lane, trip, ch, a, buf, r, half, lo):
    v = k.nc.vector
    s_ps, s_sb, at = half_views(k, lane, a, buf, r, lo)
    dve.wait_ge(*sig.at("left" if a.topk else a.p + "s_ps", lane, trip, 2 * r + half + 1))
    if not a.topk:
        ch.link(v.tensor_reduce(buf.m[:, at], s_ps, AX, ALU.max))
        return
    left, top = half_views(k, lane, a, Bag(s=buf.left), r, lo)[1], buf.top[:, at, :]
    n = 2 * len(a.rounds[r][1])
    hold(k, dve, "vector")
    for i in range(TOPK // 8):
        for h in range(n):
            ins = v.max(top[:, h, 8 * i:8 * i + 8], left[:, h, :])
        ch.link(ins)
        if i == 0:
            v.tensor_scalar(buf.m[:, at], top[:, :, 0], -a.scale, None, ALU.mult).then_inc(*sig.up(a.p + "s_sb", lane))
        else:
            hold(k, dve, "vector")
        for h in range(n):
            ins = v.match_replace(left[:, h, :], top[:, h, 8 * i:8 * i + 8], left[:, h, :], -BIG)
        ch.link(ins)
        hold(k, dve, "vector")


def shift_vector(k, dve, sig, lane, trip, a, buf, r, half, lo):
    s_ps, s_sb, at = half_views(k, lane, a, buf, r, lo)
    n = 2 * len(a.rounds[r][1])
    if r and half == 0:
        dve.wait_ge(*sig.at(a.p + "probT_ps", lane, trip, r))
    m = buf.m[:, at].unsqueeze(2)
    k.nc.vector.tensor_tensor(s_sb, s_ps, m.broadcast_to([P, n, s_sb.shape[2]]), ALU.subtract)\
        .then_inc(*sig.up(a.p + "s_sb", lane))


def left_scalar(k, act, sig, lane, trip, a, buf, r, half, lo):
    s_ps, left, _ = half_views(k, lane, a, Bag(s=buf.left), r, lo)
    act.wait_ge(*sig.at("s_ps", lane, trip, 2 * r + half + 1))
    if r:
        act.wait_ge(*sig.at("kept", lane, trip, r))
    k.nc.scalar.activation(left, s_ps, ACT.Copy).then_inc(*sig.up("left", lane))


def shifted_probs_scalar(k, act, sig, lane, trip, a, buf, r, half, lo):
    s_ps, s_sb, at = half_views(k, lane, a, buf, r, lo)
    act.wait_ge(*sig.at("s_sb", lane, trip, 2 * r + half + 1))
    if r and half == 0:
        act.wait_ge(*sig.at("probT_ps", lane, trip, r))
    for h in range(at.stop - at.start):
        m = buf.m[:, at.start + h:at.start + h + 1]
        ins = k.nc.scalar.activation(s_sb[:, h, :], s_ps[:, h, :], ACT.Exp, scale=a.scale, bias=m)
    ins.then_inc(*sig.up("prob", lane))


def probs_scalar(k, act, sig, lane, trip, a, buf, r, half, lo):
    _, s_sb, _ = half_views(k, lane, a, buf, r, lo)
    act.wait_ge(*sig.at(a.p + "s_sb", lane, trip, 2 * r + half + 1))
    k.nc.scalar.activation(s_sb, s_sb, ACT.Exp, scale=a.scale).then_inc(*sig.up(a.p + "prob", lane))


def topk_vector(k, dve, sig, lane, trip, a, buf, r):
    view = lambda ap: ap.rearrange("p b (c f) -> p (b c) f", c=len(a.rounds[r][1]))[:, :, 0:a.nk]
    dve.wait_ge(*sig.at(a.p + "prob", lane, trip, 2 * r + 2))
    k.nc.vector.scalar_tensor_tensor(view(buf.s), view(buf.left), -BIG, view(buf.s), ALU.is_equal, ALU.mult)\
        .then_inc(*sig.up(a.p + "kept", lane))


def probs_tensor(k, pe, sig, lane, trip, a, buf, r):
    t, chunks, nkb = a.rounds[r]
    pe.wait_ge(*(sig.at(a.p + "kept", lane, trip, r + 1) if a.topk else sig.at(a.p + "prob", lane, trip, 2 * r + 2)))
    for s in range(len(chunks) * nkb):
        for i in range(4):
            ins = k.nc.tensor.transpose(bank(k, lane, i)[0:a.nk, s * P:(s + 1) * P],
                                        buf.s[:, i, s * P:s * P + a.nk], k.ident[:, :])
    ins.then_inc(*sig.up(a.p + "probT_ps", lane))


def probsT_scalar(k, act, sig, lane, trip, a, buf, r):
    act.wait_ge(*sig.at(a.p + "probT_ps", lane, trip, r + 1))
    if r:
        act.wait_ge(*sig.at(a.p + "o_ps", lane, trip, r))
    k.nc.scalar.activation(buf.probT[0:a.nk, 0:2, :], banks(k, lane, 0, 2)[0:a.nk], ACT.Copy)\
        .then_inc(*sig.up(a.p + "probT_a", lane))
    if a.topk:
        k.nc.scalar.activation(buf.probT[0:a.nk, 2:4, :], banks(k, lane, 2, 2)[0:a.nk], ACT.Copy)\
            .then_inc(*sig.up(a.p + "probT_v", lane))


def probsT_vector(k, dve, sig, lane, trip, a, buf, r):
    t, chunks, nkb = a.rounds[r]
    if not a.ones:
        s_sb = buf.s.rearrange("p c (i f) -> p (c i) f", i=4)[:, :, 0:a.nk]
        dve.wait_ge(*sig.at(a.p + "prob", lane, trip, 2 * r + 2))
        k.nc.vector.tensor_reduce(buf.sums, s_sb, AX, ALU.add)
    dve.wait_ge(*sig.at(a.p + "probT_ps", lane, trip, r + 1))
    if r:
        dve.wait_ge(*sig.at(a.p + "o_ps", lane, trip, r))
    k.nc.vector.tensor_copy(buf.probT[0:a.nk, 2:4, :], banks(k, lane, 2, 2)[0:a.nk])\
        .then_inc(*sig.up(a.p + "probT_v", lane))


def outputs_tensor(k, pe, sig, lane, trip, a, buf, r):
    t, chunks, nkb = a.rounds[r]
    pe.wait_ge(*sig.at(a.p + "probT_a", lane, trip, r + 1))
    pe.wait_ge(*sig.at(a.p + "probT_v", lane, trip, r + 1))
    for ci, c in enumerate(chunks):
        for i in range(4):
            h = 4 * c + i
            for kb in range(nkb):
                b, s = (i, ci * nkb + kb) if a.causal else (c, i)
                ins = k.nc.tensor.matmul(bank(k, lane, 0)[PAD * i:PAD * i + a.vw, c * P:(c + 1) * P],
                                         buf.v[0:a.nk, kb, h * a.vw:(h + 1) * a.vw],
                                         buf.probT[0:a.nk, b, s * P:(s + 1) * P], start=kb == 0, stop=kb == nkb - 1,
                                         skip_group_check=True)
    ins.then_inc(*sig.up(a.p + "o_ps", lane))


def raw_scalar(k, act, sig, lane, trip, a, buf, r):
    t, chunks, nkb = a.rounds[r]
    at, n = chunks[0], len(chunks)
    act.wait_ge(*sig.at(a.p + "o_ps", lane, trip, r + 1))
    k.nc.scalar.activation(buf.raw[:, at:at + n, :].rearrange("p c q -> p (c q)"),
                           bank(k, lane, 0)[:, at * P:(at + n) * P], ACT.Copy).then_inc(*sig.up(a.p + "raw", lane))


def back_tensor(k, pe, sig, lane, trip, a, buf, r):
    pe.wait_ge(*sig.at(a.p + "raw", lane, trip, r + 1))
    for c in a.rounds[r][1]:
        ins = k.nc.tensor.transpose(bank(k, lane, 1)[:, c * P:(c + 1) * P], buf.raw[:, c, :], k.ident[:, :])
    ins.then_inc(*sig.up(a.p + "back_ps", lane))


def outputs_vector(k, dve, sig, lane, trip, ch, a, buf, r):
    v = k.nc.vector
    t, chunks, nkb = a.rounds[r]
    at, n = 4 * chunks[0], 4 * len(chunks)
    e = a.width
    rec = buf.rec[:, 0:n]
    dve.wait_ge(*sig.at(a.p + "back_ps", lane, trip, r + 1))
    view = bank(k, lane, 1).rearrange("p (h e) -> p h e", h=H)[:, at:at + n, :]
    sums = view[:, :, e:e + 1] if a.ones else buf.sums[:, 0:n].unsqueeze(2)
    ch.link(v.reciprocal(rec.unsqueeze(2), sums))
    v.tensor_tensor(buf.o[:, t, at * e:(at + n) * e].rearrange("p (h e) -> p h e", h=n), view[:, :, 0:e],
                    rec.unsqueeze(2).broadcast_to([P, n, e]), ALU.mult).then_inc(*sig.up(a.p + "o", lane))


def attention_units(a):
    n = len(a.rounds)
    real = lambda r: r if 0 <= r < n else None
    return [(lane, real(r), real(r - 1), 1 - lane, real(r if lane else r - 1)) for r in range(n + 1) for lane in (0, 1)]


HALVES = ((0, 2), (1, 0))


def attention_tensor(k, pe, sig, trip, a, bufs):
    for lane, r, before, other, turned in attention_units(a):
        buf = bufs[lane]
        if before is not None:
            outputs_tensor(k, pe, sig, lane, trip, a, buf, before)
        if r is not None:
            scores_tensor(k, pe, sig, lane, trip, a, buf, r, (2, 3)).then_inc(*sig.up(a.p + "s_ps", lane))
        if before is not None:
            back_tensor(k, pe, sig, lane, trip, a, buf, before)
        if r is not None:
            scores_tensor(k, pe, sig, lane, trip, a, buf, r, (0,))
        if turned is not None:
            probs_tensor(k, pe, sig, other, trip, a, bufs[other], turned)
        if r is not None:
            scores_tensor(k, pe, sig, lane, trip, a, buf, r, (1,)).then_inc(*sig.up(a.p + "s_ps", lane))


def attention_scalar(k, act, sig, trip, a, bufs):
    for lane, r, before, other, turned in attention_units(a):
        if before is not None:
            raw_scalar(k, act, sig, lane, trip, a, bufs[lane], before)
        if a.topk and r is not None:
            left_scalar(k, act, sig, lane, trip, a, bufs[lane], r, *HALVES[0])
            shifted_probs_scalar(k, act, sig, lane, trip, a, bufs[lane], r, *HALVES[0])
        elif r is not None:
            probs_scalar(k, act, sig, lane, trip, a, bufs[lane], r, *HALVES[0])
        if turned is not None:
            probsT_scalar(k, act, sig, other, trip, a, bufs[other], turned)
        if a.topk and r is not None:
            left_scalar(k, act, sig, lane, trip, a, bufs[lane], r, *HALVES[1])
            shifted_probs_scalar(k, act, sig, lane, trip, a, bufs[lane], r, *HALVES[1])
        elif r is not None:
            probs_scalar(k, act, sig, lane, trip, a, bufs[lane], r, *HALVES[1])


def attention_vector(k, dve, sig, trip, chains, a, bufs):
    for lane, r, before, other, turned in attention_units(a):
        ch, buf = chains[lane], bufs[lane]
        if a.topk and turned is not None:
            topk_vector(k, dve, sig, other, trip, a, bufs[other], turned)
        if r is not None:
            max_vector(k, dve, sig, lane, trip, ch, a, buf, r, *HALVES[0])
        if before is not None:
            outputs_vector(k, dve, sig, lane, trip, ch, a, buf, before)
        if r is not None and not a.topk:
            shift_vector(k, dve, sig, lane, trip, a, buf, r, *HALVES[0])
        if turned is not None and not a.topk:
            probsT_vector(k, dve, sig, other, trip, a, bufs[other], turned)
        if r is not None:
            max_vector(k, dve, sig, lane, trip, ch, a, buf, r, *HALVES[1])
            if not a.topk:
                shift_vector(k, dve, sig, lane, trip, a, buf, r, *HALVES[1])


def oT_tensor(k, pe, sig, lane, trip, a, buf):
    pe.wait_ge(*sig.at(a.p + "o", lane, trip, len(a.rounds)))
    for c in range(H * a.width // P):
        for t in (0, 1):
            at = (2 * c + t) * P
            ins = k.nc.tensor.transpose(bank(k, lane, 2 + at // 512)[:, at % 512:at % 512 + P],
                                        buf.o[:, t, c * P:(c + 1) * P], k.ident[:, :])
    ins.then_inc(*sig.up(a.p + "oT_ps", lane))


def oT_scalar(k, act, sig, lane, trip, a, buf):
    n = H * a.width // 256
    act.wait_ge(*sig.at(a.p + "oT_ps", lane, trip, 1))
    k.nc.scalar.activation(buf.oT.rearrange("p c t -> p (c t)"), banks(k, lane, 2, n).rearrange("p b f -> p (b f)"),
                           ACT.Copy).then_inc(*sig.up(a.p + "oT", lane))


def out_tensor(k, pe, sig, lane, trip, a, buf, w, row, kc=KC):
    pe.wait_ge(*sig.at(a.p + "oT", lane, trip, 1))
    for t in (0, 1):
        ins = proj_token(k, bank(k, lane, 0)[:, t * D:(t + 1) * D], buf.oT, t * P, w, row, kc)
    ins.then_inc(*sig.up("out_ps", lane))


def residual_vector(k, dve, sig, lane, trip, i=0):
    x = x_of(k, trip, lane)
    dve.wait_ge(*sig.at("out_ps", lane, trip, 1))
    k.nc.vector.tensor_tensor(x, x, bank(k, lane, i).rearrange("p (t d) -> p t d", t=2), ALU.add)\
        .then_inc(*sig.up("done", lane))


AHEAD = ("z", "zT_ps", "zT")


def zT_tensor(k, pe, sig, trip, bufs, at=1):
    for lane, buf in enumerate(bufs):
        pe.wait_ge(*sig.at("z", lane, trip, 1))
        transpose_z_tensor(k, pe, sig, lane, trip, buf.z, bank(k, lane, at)).then_inc(*sig.up("zT_ps", lane))


def zT_scalar(k, act, sig, trip, bufs, at=1):
    for lane, buf in enumerate(bufs):
        act.wait_ge(*sig.at("zT_ps", lane, trip, 1))
        k.nc.scalar.activation(buf.zT.rearrange("p c t -> p (c t)"), bank(k, lane, at), ACT.Copy)\
            .then_inc(*sig.up("zT", lane))


def lane_buffers(k, lanes=2):
    c = Carve(k.arena, k.arena_size)
    bufs = []
    for _ in range(lanes):
        bufs.append(Bag(z=c.take(2, D), zT=c.take(KC, SEQ), st=c.take(22)))
    return c, bufs


def cross_qkv_tensor(k, pe, sig, lane, trip, a, buf, stage, n=""):
    pe.wait_ge(*sig.at("zT" + n.replace("1", ""), lane, trip, 1))
    pe.wait_ge(*sig.at("ctx", lane, trip, 1))
    if n != "2":
        pe.wait_ge(*sig.at("done", lane, trip, 0))
    wq, wk, wv = (w_of(k, stage, w + n, KC) for w in ("wq", "wk", "wv"))
    for c in range(HC):
        proj_feature(k, bank(k, lane, c // 2)[:, c % 2 * SEQ:(c % 2 + 1) * SEQ], wq, buf.zT, c * P, P)
    for c in range(HC):
        proj_feature(k, bank(k, lane, 2)[:, c * P:c * P + CTX], wk, buf.ctxT, c * P, P)
    products(k, bank(k, lane, 3)[0:CTX, 0:H * VW], [(buf.ctxT[:, c, :], wv[:, c, :]) for c in range(KC)],
             row_of(k, stage, "bv" + n)).then_inc(*sig.up(a.p + "qkv_ps", lane))


def q_scalar(k, act, sig, lane, trip, a, buf, bq):
    act.wait_ge(*sig.at(a.p + "qkv_ps", lane, trip, 1))
    for c in range(HC):
        ins = k.nc.scalar.activation(buf.qT[:, c, :], bank(k, lane, c // 2)[:, c % 2 * SEQ:(c % 2 + 1) * SEQ],
                                     ACT.Identity, bias=col_of(k, bq, c))
    ins.then_inc(*sig.up(a.p + "q", lane))


def cross_kv_vector(k, dve, sig, lane, trip, a, buf, bk):
    v = k.nc.vector
    dve.wait_ge(*sig.at(a.p + "qkv_ps", lane, trip, 1))
    at, _ = k.colpos[bk]
    for i in range(4):
        rows = slice(PAD * i, PAD * (i + 1))
        v.tensor_tensor(buf.kT[rows, :, i * CTX:(i + 1) * CTX], cut(bank(k, lane, 2)[rows], chunk=HC)[:, :, 0:CTX],
                        k.cols[rows, at:at + HC].unsqueeze(2).broadcast_to([PAD, HC, CTX]), ALU.add)
    v.tensor_copy(buf.v[0:CTX, 0, :], bank(k, lane, 3)[0:CTX, 0:H * VW]).then_inc(*sig.up(a.p + "kv", lane))


def keys_vector(k, bufs):
    for buf in bufs:
        k.nc.vector.memset(buf.kT, 0.0)


def qkv_wait_tensor(k, pe, sig, lane, trip, a):
    pe.wait_ge(*sig.at(a.p + "q", lane, trip, 1))
    pe.wait_ge(*sig.at(a.p + "kv", lane, trip, 1))


def context_gpsimd(k, pool, sig, lane, trip, buf):
    pool.wait_ge(*sig.at("done", lane, trip, 0))
    hold(k, pool, "gpsimd")
    k.nc.gpsimd.tensor_copy(buf.ctxT, k.ctxT[:, :, bass.ts(trip * 2 + lane, CTX)]).then_inc(*sig.up("ctx", lane))


def xattn_plan(k, stage, topk):
    a = attention("cross", topk=topk)
    c, bufs = lane_buffers(k)
    for buf in bufs:
        buf.ctxT = c.take(KC, CTX)
        attention_buffers(c, a, buf)
    more = {"kept": 2} if topk else {}
    norms = norms_plan(k, stage)
    sig = Signals(k.signals, stage, B // 2, 2, AHEAD, z=1, zT_ps=1, zT=1, ctx=1, qkv_ps=1, q=1, kv=1, oT_ps=1, oT=1,
                  out_ps=1, done=1, dve_step=k.steps[stage], **attention_signals(a), **more)
    return Bag(norms=norms, a=a, bufs=bufs, sig=sig, stage=stage)


def xattn_tensor(k, pe, s):
    enter(k, pe, s.sig)
    zT_tensor(k, pe, s.sig, 0, s.bufs)
    with pe.Fori(0, s.sig.trips) as trip:
        for lane, buf in enumerate(s.bufs):
            cross_qkv_tensor(k, pe, s.sig, lane, trip, s.a, buf, s.stage)
        for lane in (0, 1):
            qkv_wait_tensor(k, pe, s.sig, lane, trip, s.a)
        attention_tensor(k, pe, s.sig, trip, s.a, s.bufs)
        for lane, buf in enumerate(s.bufs):
            oT_tensor(k, pe, s.sig, lane, trip, s.a, buf)
        zT_tensor(k, pe, s.sig, trip + 1, s.bufs)
        for lane, buf in enumerate(s.bufs):
            out_tensor(k, pe, s.sig, lane, trip, s.a, buf, w_of(k, s.stage, "wo", KC), row_of(k, s.stage, "bo"))


def xattn_scalar(k, act, s):
    enter(k, act, s.sig)
    zT_scalar(k, act, s.sig, 0, s.bufs)
    with act.Fori(0, s.sig.trips) as trip:
        for lane, buf in enumerate(s.bufs):
            q_scalar(k, act, s.sig, lane, trip, s.a, buf, s.stage + "_bq")
        attention_scalar(k, act, s.sig, trip, s.a, s.bufs)
        for lane, buf in enumerate(s.bufs):
            oT_scalar(k, act, s.sig, lane, trip, s.a, buf)
        zT_scalar(k, act, s.sig, trip + 1, s.bufs)


def xattn_vector(k, dve, s):
    enter(k, dve, s.sig)
    norms_vector(k, dve, s.norms)
    keys_vector(k, s.bufs)
    first_z_vector(k, s.sig, s.bufs)
    with dve.Fori(0, s.sig.trips) as trip:
        chains = [Chain(dve, s.sig, lane, trip) for lane in (0, 1)]
        for lane in (0, 1):
            stats_vector(k, dve, s.sig, lane, trip)
        for lane, buf in enumerate(s.bufs):
            cross_kv_vector(k, dve, s.sig, lane, trip, s.a, buf, s.stage + "_bk")
        attention_vector(k, dve, s.sig, trip, chains, s.a, s.bufs)
        later_z_vector(k, dve, s.sig, s.bufs, trip)
        for lane, buf in enumerate(s.bufs):
            residual_vector(k, dve, s.sig, lane, trip)
        for ch in chains:
            ch.close()


def xattn_gpsimd(k, pool, s):
    enter(k, pool, s.sig)
    with pool.Fori(0, s.sig.trips) as trip:
        for lane, buf in enumerate(s.bufs):
            context_gpsimd(k, pool, s.sig, lane, trip, buf)



def memory_plan(k):
    c = Carve(k.arena, k.arena_size)
    buf = Bag(zT_all=c.take(KC, B * SEQ + MEM), z_all=c.take((TILES + 1) * D), swa_all=c.take((TILES + 1) * D),
              kT_mem=c.take(KC, MEM), v_mem=c.take(SH * SVW), dw1=c.take(KC, HID), dw2=c.take(HID // P, D),
              db1=c.take(HID // P), db2=c.take(D), keep=c.take(1))
    start = c.at

    def window_buffers():
        s = c.take(4, SEQ)
        return Bag(z=c.take(2, D), zT=c.take(KC, SEQ), qT=c.take(KC, SEQ), kT=c.take(KC, SEQ), v=c.take(2, SH * SVW),
                   s=s, probT=c.take(2, 512), o=s[:, 0, :], oT=s[:, 1, :].rearrange("p (c q) -> p c q", c=KC),
                   m=c.take(8))

    def gradient_buffers():
        sg = c.take(HID)
        return Bag(zT=c.take(KC, P), z=c.take(D), sg=sg, a=c.take(HID), g=c.take(HID), aT=c.take(HID // P, P),
                   e=sg[:, 0:D], eT=sg[:, D:2 * D].rearrange("p (c q) -> p c q", c=KC))

    def memory_buffers():
        aT = c.take(HID // P, SEQ)
        return Bag(zT=c.take(KC, SEQ), swa=c.take(2, D), swaT=c.take(KC, SEQ), aT=aT, om=c.take(2, D),
                   omT=c.take(KC, SEQ), g1=aT[:, 0:2, :], g2=aT[:, 2:4, :])

    for name, make in (("windows", window_buffers), ("grads", gradient_buffers), ("mems", memory_buffers)):
        c.at = start
        lanes = [make(), make()]
        if name == "windows":
            buf.windows = lanes
        elif name == "grads":
            buf.grads = lanes
        else:
            buf.mems = lanes
    window = dict(z=1, zT_ps=1, zT=1, z_kept=1, qkv_ps=1, q=1, kv=1, s_ps=2, s_sb=2, prob=2, probT_ps=2, probT_a=2,
                  o_ps=2, o=2, oT_ps=2, oT=2, out_ps=2, swa=2, done=1)
    gradient = dict(tok=1, h_ps=1, sg=1, a=1, aT_ps=1, aT=1, pred_ps=1, e=1, eT_ps=1, eT=1, da_ps=1, dh=1, dw2_ps=1,
                    dw2=1, dw1_ps=1, dw1=1, db_ps=1, done=1)
    n = k.steps
    first = dict(window)
    for name in ("s_ps", "s_sb", "prob", "probT_ps", "probT_a", "o_ps", "o", "oT_ps", "oT", "out_ps", "swa"):
        first[name] = 1
    for name in ("z", "z_kept", "zT_ps", "zT"):
        del first[name]
    sig = lambda trips, lanes, **per: Signals(k.signals, "L0_attn", trips, lanes, **per)
    norms = norms_plan(k, "L0_attn")
    return Bag(
        buf=buf, norms=norms, first=sig(1, 2, done=1),
        window_mem=sig(1, 1, dve_step=n["window_mem"], **first),
        window=sig(B // 2, 2, dve_step=n["window"], **window),
        grad_mem=sig(1, 1, dve_step=n["grad_mem"], **gradient), grad=sig(TILES // 2, 2, dve_step=n["grad"], **gradient),
        update=sig(1, 1, dve_step=n["update"], done=1),
        memory=sig(B // 2, 2, dve_step=n["memory"], tok=1, h_ps=4, sg=4, aT=4, swaT_ps=1, om_ps=1, om=1, omT_ps=1,
                   omT=1, gate_ps=1, gate=1, done=1))


class WindowTile:

    def __init__(self, k, shared, buf, t):
        self.t = t
        if t == "mem":
            self.rows, self.mask, self.q = MEM, "swam", slice(0, MEM)
            self.keys = [(shared.kT_mem, slice(0, MEM), MEM, shared.v_mem)]
        elif t == 0:
            self.rows, self.mask, self.q = P, "swa0", slice(0, P)
            self.keys = [(shared.kT_mem, slice(0, MEM), MEM, shared.v_mem), (buf.kT, slice(0, P), P, buf.v[:, 0, :])]
        else:
            self.rows, self.mask, self.q = P, "swa1", slice(P, SEQ)
            self.keys = [(buf.kT, slice(0, P), P, buf.v[:, 0, :]), (buf.kT, slice(P, SEQ), P, buf.v[:, 1, :])]
        self.nk = sum(n for _, _, n, _ in self.keys)


def window_scores_view(k, lane, buf, w):
    s_ps = banks(k, lane, 1, 2)[0:w.rows].rearrange("p b (c f) -> p (b c) f", c=2)[:, :, 0:w.nk]
    return s_ps, buf.s[0:w.rows, :, 0:w.nk]


def outer_banks(k, lane):
    return k.ps[:, 4 * lane:4 * lane + 4:3, :]


def window_zT_tensor(k, pe, sig, lane, buf, trip):
    pe.wait_ge(*sig.at("z", lane, trip, 1))
    transpose_z_tensor(k, pe, sig, lane, trip, buf.z, bank(k, lane, 0)).then_inc(*sig.up("zT_ps", lane))


def window_qkv_tensor(k, pe, sig, lane, shared, buf, trip, mem):
    wq, wk, wv = (w_of(k, "L0_attn", n, KC) for n in ("wq", "wk", "wv"))
    n = MEM if mem else SEQ
    if mem:
        zT = shared.zT_all[:, :, B * SEQ:B * SEQ + MEM]
    else:
        zT = buf.zT
        pe.wait_ge(*sig.at("zT", lane, trip, 1))
    for c in range(KC):
        proj_feature(k, bank(k, lane, 1)[:, c * SEQ:c * SEQ + n], wq, zT, c * P, P)
        proj_feature(k, bank(k, lane, 2)[:, c * SEQ:c * SEQ + n], wk, zT, c * P, P)
    for t in range(1 if mem else 2):
        ins = products(k, bank(k, lane, 3 - 3 * t)[0:min(n, P), 0:SH * SVW],
                       [(zT[:, c, t * P:t * P + min(n, P)], wv[:, c, :]) for c in range(KC)],
                       row_of(k, "L0_attn", "v1"))
    ins.then_inc(*sig.up("qkv_ps", lane))


def window_scores_tensor(k, pe, sig, lane, buf, trip, r, w):
    mm = k.nc.tensor.matmul
    if r:
        pe.wait_ge(*sig.at("swa", lane, trip, r))
    else:
        pe.wait_ge(*sig.at("q", lane, trip, 1))
        pe.wait_ge(*sig.at("kv", lane, trip, 1))
    mask = mask_of(k, w.mask)
    for i in (0, 1):
        mm(bank(k, lane, 1 + i)[0:w.rows].rearrange("p (c f) -> p c f", c=2)[:, :, 0:w.nk], k.identb[:, 0:w.rows],
           mask.rearrange("p (c f) -> p c f", c=2), start=True, stop=False, skip_group_check=True)
    for c in (0, 1):
        for i in (0, 1):
            at = c * SEQ
            half = slice(SD_ * i, SD_ * (i + 1))
            for kT, cols, nk, _ in w.keys:
                ins = mm(bank(k, lane, 1 + i)[0:w.rows, at:at + nk], buf.qT[half, c, w.q], kT[half, c, cols],
                         start=False, stop=True, skip_group_check=True)
                at += nk
    ins.then_inc(*sig.up("s_ps", lane))


def window_probs_tensor(k, pe, sig, lane, buf, trip, r, w):
    pe.wait_ge(*sig.at("prob", lane, trip, r + 1))
    hold(k, pe, "tensor")
    for c in (0, 1):
        for i in (0, 1):
            at = 0
            for kb, (_, _, nk, _) in enumerate(w.keys):
                s = 2 * c + kb
                ins = k.nc.tensor.transpose(bank(k, lane, 3 * i)[0:nk, s * P:s * P + w.rows],
                                            buf.s[0:w.rows, 2 * i + c, at:at + nk], k.ident[0:w.rows, 0:w.rows])
                at += nk
    ins.then_inc(*sig.up("probT_ps", lane))


def window_outputs_tensor(k, pe, sig, lane, buf, trip, r, w):
    pe.wait_ge(*sig.at("probT_a", lane, trip, r + 1))
    for c in (0, 1):
        for i in (0, 1):
            h = 2 * c + i
            for kb, (_, _, nk, v) in enumerate(w.keys):
                s = 2 * c + kb
                ins = k.nc.tensor.matmul(bank(k, lane, 1)[0:w.rows, h * SVW:(h + 1) * SVW],
                                         buf.probT[0:nk, i, s * P:s * P + w.rows], v[0:nk, h * SVW:(h + 1) * SVW],
                                         start=kb == 0, stop=kb == len(w.keys) - 1)
    ins.then_inc(*sig.up("o_ps", lane))


def window_oT_tensor(k, pe, sig, lane, buf, trip, r, w):
    pe.wait_ge(*sig.at("o", lane, trip, r + 1))
    for c in range(KC):
        ins = k.nc.tensor.transpose(bank(k, lane, 2)[:, c * P:c * P + w.rows], buf.o[0:w.rows, c * P:(c + 1) * P],
                                    k.ident[0:w.rows, 0:w.rows])
    ins.then_inc(*sig.up("oT_ps", lane))


def window_out_tensor(k, pe, sig, lane, buf, trip, r, w):
    pe.wait_ge(*sig.at("oT", lane, trip, r + 1))
    products(k, bank(k, lane, 3)[0:w.rows, 0:D],
             [(buf.oT[:, c, 0:w.rows], w_of(k, "L0_attn", "wo", KC)[:, c, :]) for c in range(KC)])\
        .then_inc(*sig.up("out_ps", lane))


def window_tiles(k, shared, buf, mem):
    return [WindowTile(k, shared, buf, t) for t in (("mem",) if mem else (0, 1))]


def window_tensor(k, pe, sig, shared, bufs, trip, mem=False):
    lanes = list(enumerate(bufs))
    tiles = [window_tiles(k, shared, buf, mem) for buf in bufs]
    if not mem:
        for lane, buf in lanes:
            window_zT_tensor(k, pe, sig, lane, buf, trip)
    for lane, buf in lanes:
        window_qkv_tensor(k, pe, sig, lane, shared, buf, trip, mem)
    for r in range(len(tiles[0])):
        for phase in (window_scores_tensor, window_probs_tensor, window_outputs_tensor, window_oT_tensor,
                      window_out_tensor):
            for lane, buf in lanes:
                phase(k, pe, sig, lane, buf, trip, r, tiles[lane][r])


def window_scalar(k, act, sig, shared, bufs, trip, mem=False):
    n, a = MEM if mem else SEQ, k.nc.scalar.activation
    lanes = list(enumerate(bufs))
    tiles = [window_tiles(k, shared, buf, mem) for buf in bufs]
    if not mem:
        for lane, buf in lanes:
            act.wait_ge(*sig.at("zT_ps", lane, trip, 1))
            a(buf.zT.rearrange("p c t -> p (c t)"), bank(k, lane, 0), ACT.Copy).then_inc(*sig.up("zT", lane))
    for lane, buf in lanes:
        act.wait_ge(*sig.at("qkv_ps", lane, trip, 1))
        for c in range(KC):
            ins = a(buf.qT[:, c, 0:n], bank(k, lane, 1)[:, c * SEQ:c * SEQ + n], ACT.Copy)
        ins.then_inc(*sig.up("q", lane))
    for r in range(len(tiles[0])):
        for lane, buf in lanes:
            _, s_sb = window_scores_view(k, lane, buf, tiles[lane][r])
            act.wait_ge(*sig.at("s_sb", lane, trip, r + 1))
            a(s_sb, s_sb, ACT.Exp, scale=SD_ ** -0.5).then_inc(*sig.up("prob", lane))
        for lane, buf in lanes:
            w = tiles[lane][r]
            act.wait_ge(*sig.at("probT_ps", lane, trip, r + 1))
            for kb, (_, _, nk, _) in enumerate(w.keys):
                sel = lambda ap: ap.rearrange("p b (c kb q) -> p b c kb q", c=2, kb=2)[0:nk, :, :, kb, 0:w.rows]
                ins = a(sel(buf.probT), sel(outer_banks(k, lane)), ACT.Copy)
            ins.then_inc(*sig.up("probT_a", lane))
        for lane, buf in lanes:
            w = tiles[lane][r]
            act.wait_ge(*sig.at("oT_ps", lane, trip, r + 1))
            a(buf.oT[:, :, 0:w.rows], bank(k, lane, 2)[:, 0:KC * P].rearrange("p (c q) -> p c q", c=KC)[:, :, 0:w.rows],
              ACT.Copy).then_inc(*sig.up("oT", lane))


def window_vector(k, dve, sig, shared, bufs, trip, mem=False):
    v = k.nc.vector
    lanes = list(enumerate(bufs))
    tiles = [window_tiles(k, shared, buf, mem) for buf in bufs]
    chains = [Chain(dve, sig, lane, trip) for lane, _ in lanes]
    n, rows = (MEM, MEM) if mem else (SEQ, P)
    if not mem:
        for lane, buf in lanes:
            ln_vector(k, dve, sig, lane, trip, buf)
    for lane, buf in lanes:
        dve.wait_ge(*sig.at("qkv_ps", lane, trip, 1))
        kT, vv = (shared.kT_mem, shared.v_mem.unsqueeze(1)) if mem else (buf.kT, buf.v)
        v.tensor_copy(kT[:, :, 0:n], bank(k, lane, 2).rearrange("p (c q) -> p c q", c=KC)[:, :, 0:n])
        for t in range(1 if mem else 2):
            ins = v.tensor_copy(vv[0:rows, t, :], bank(k, lane, 3 - 3 * t)[0:rows, 0:SH * SVW])
        ins.then_inc(*sig.up("kv", lane))
    for r in range(len(tiles[0])):
        for lane, buf in lanes:
            w = tiles[lane][r]
            s_ps, s_sb = window_scores_view(k, lane, buf, w)
            m = buf.m[0:w.rows, 0:SH]
            dve.wait_ge(*sig.at("s_ps", lane, trip, r + 1))
            chains[lane].link(v.tensor_reduce(m, s_ps, AX, ALU.max))
            v.tensor_tensor(s_sb, s_ps, m.unsqueeze(2).broadcast_to([w.rows, SH, w.nk]), ALU.subtract)\
                .then_inc(*sig.up("s_sb", lane))
        for lane, buf in lanes:
            w = tiles[lane][r]
            rec = buf.m[0:w.rows, SH:2 * SH]
            dve.wait_ge(*sig.at("o_ps", lane, trip, r + 1))
            o_ps = bank(k, lane, 1)[0:w.rows, 0:SH * SVW].rearrange("p (h e) -> p h e", h=SH)
            chains[lane].link(v.reciprocal(rec.unsqueeze(2), o_ps[:, :, SD_:SVW]))
            v.tensor_tensor(buf.o[0:w.rows, :].rearrange("p (h e) -> p h e", h=SH), o_ps[:, :, 0:SD_],
                            rec.unsqueeze(2).broadcast_to([w.rows, SH, SD_]), ALU.mult).then_inc(*sig.up("o", lane))
        for lane, buf in lanes:
            w = tiles[lane][r]
            dve.wait_ge(*sig.at("out_ps", lane, trip, r + 1))
            hold(k, dve, "vector")
            if mem:
                ins = v.tensor_copy(shared.swa_all[0:w.rows, TILES * D:], bank(k, lane, 3)[0:w.rows, 0:D])
            else:
                ins = v.tensor_copy(shared.swa_all[:, bass.ds(((trip * 2 + lane) * 2 + r) * D, D)],
                                    bank(k, lane, 3)[:, 0:D])
            ins.then_inc(*sig.up("swa", lane))
    for lane, buf in lanes:
        if not mem:
            dve.wait_ge(*sig.at("z_kept", lane, trip, 1))
        dve.wait_ge(*sig.at("swa", lane, trip, 1 if mem else 2))
        dve.sem_inc(*sig.up("done", lane))
        chains[lane].close()


def window_gpsimd(k, pool, sig, shared, bufs, trip):
    for lane, buf in enumerate(bufs):
        pool.wait_ge(*sig.at("zT", lane, trip, 1))
        hold(k, pool, "gpsimd")
        at = trip * 2 + lane
        k.nc.gpsimd.tensor_copy(shared.z_all[:, bass.ts(at, 2 * D)], buf.z.rearrange("p t d -> p (t d)"))
        k.nc.gpsimd.tensor_copy(shared.zT_all[:, :, bass.ts(at, SEQ)], buf.zT).then_inc(*sig.up("z_kept", lane))


def grad_h_tensor(k, pe, sig, lane, g, trip, rows):
    pe.wait_ge(*sig.at("tok", lane, trip, 1))
    for i in (0, 1):
        ins = products(k, bank(k, lane, i)[0:rows, :],
                       [(g.zT[:, c, 0:rows], w_of(k, "L0_attn", "w1T", KC)[:, c, i * 512:(i + 1) * 512])
                        for c in range(KC)], row_of(k, "L0_attn", "b1")[:, i * 512:(i + 1) * 512])
    ins.then_inc(*sig.up("h_ps", lane))


def grad_aT_tensor(k, pe, sig, lane, g, trip, rows):
    pe.wait_ge(*sig.at("a", lane, trip, 1))
    for c in range(HID // P):
        ins = k.nc.tensor.transpose(bank(k, lane, 2 + c // 4)[:, c % 4 * P:c % 4 * P + rows],
                                    g.a[0:rows, c * P:(c + 1) * P], k.ident[0:rows, 0:rows])
    ins.then_inc(*sig.up("aT_ps", lane))


def grad_pred_tensor(k, pe, sig, lane, g, trip, rows):
    pe.wait_ge(*sig.at("aT", lane, trip, 1))
    products(k, bank(k, lane, 0)[0:rows, 0:D],
             [(g.aT[:, c, 0:rows], w_of(k, "L0_attn", "w2T", HID // P)[:, c, :]) for c in range(HID // P)],
             row_of(k, "L0_attn", "b2")).then_inc(*sig.up("pred_ps", lane))


def grad_eT_tensor(k, pe, sig, lane, g, trip, rows):
    pe.wait_ge(*sig.at("e", lane, trip, 1))
    for c in range(KC):
        ins = k.nc.tensor.transpose(bank(k, lane, 1)[:, c * P:c * P + rows], g.e[0:rows, c * P:(c + 1) * P],
                                    k.ident[0:rows, 0:rows])
    ins.then_inc(*sig.up("eT_ps", lane))


def grad_da_tensor(k, pe, sig, lane, g, trip, rows):
    pe.wait_ge(*sig.at("eT", lane, trip, 1))
    for i in (0, 1):
        ins = products(k, bank(k, lane, 2 + i)[0:rows, :],
                       [(g.eT[:, c, 0:rows], w_of(k, "L0_attn", "w2", KC)[:, c, i * 512:(i + 1) * 512])
                        for c in range(KC)])
    ins.then_inc(*sig.up("da_ps", lane))


def grad_dw2_tensor(k, pe, sig, lane, g, trip, rows):
    pe.wait_ge(*sig.at("dh", lane, trip, 1))
    for c in range(HID // P):
        ins = k.nc.tensor.matmul(bank(k, lane, c // 2)[:, c % 2 * D:(c % 2 + 1) * D], g.a[0:rows, c * P:(c + 1) * P],
                                 g.e[0:rows, :])
    ins.then_inc(*sig.up("dw2_ps", lane))


def grad_dw1_tensor(k, pe, sig, lane, g, trip, rows):
    pe.wait_ge(*sig.at("dw2", lane, trip, 1))
    for c in range(KC):
        for i in (0, 1):
            ins = k.nc.tensor.matmul(bank(k, lane, 2 * c + i), g.z[0:rows, c * P:(c + 1) * P],
                                     g.g[0:rows, i * 512:(i + 1) * 512])
    ins.then_inc(*sig.up("dw1_ps", lane))


def grad_db_tensor(k, pe, sig, lane, g, trip, rows):
    pe.wait_ge(*sig.at("dw1", lane, trip, 1))
    for c in range(HID // P):
        k.nc.tensor.matmul(bank(k, lane, 0)[:, c:c + 1], g.g[0:rows, c * P:(c + 1) * P], col_of(k, "one", 0, rows))
    k.nc.tensor.matmul(bank(k, lane, 1)[0:1, 0:D], col_of(k, "one", 0, rows), g.e[0:rows, :])\
        .then_inc(*sig.up("db_ps", lane))


def grad_tensor(k, pe, sig, grads, trip, rows):
    for phase in (grad_h_tensor, grad_aT_tensor, grad_pred_tensor, grad_eT_tensor, grad_da_tensor, grad_dw2_tensor,
                  grad_dw1_tensor, grad_db_tensor):
        for lane, g in enumerate(grads):
            phase(k, pe, sig, lane, g, trip, rows)


def grad_scalar(k, act, sig, grads, trip, rows):
    a = k.nc.scalar.activation
    lanes = list(enumerate(grads))
    for lane, g in lanes:
        act.wait_ge(*sig.at("h_ps", lane, trip, 1))
        a(g.sg[0:rows, :], banks(k, lane, 0, 2)[0:rows].rearrange("p b f -> p (b f)"), ACT.Sigmoid)\
            .then_inc(*sig.up("sg", lane))
    for lane, g in lanes:
        act.wait_ge(*sig.at("aT_ps", lane, trip, 1))
        a(g.aT[:, :, 0:rows], banks(k, lane, 2, 2).rearrange("p b (c q) -> p (b c) q", c=4)[:, :, 0:rows], ACT.Copy)\
            .then_inc(*sig.up("aT", lane))
    for lane, g in lanes:
        act.wait_ge(*sig.at("eT_ps", lane, trip, 1))
        a(g.eT[:, :, 0:rows], bank(k, lane, 1)[:, 0:KC * P].rearrange("p (c q) -> p c q", c=KC)[:, :, 0:rows],
          ACT.Copy).then_inc(*sig.up("eT", lane))


def grad_vector(k, dve, sig, shared, grads, trip, rows, mem=False):
    v = k.nc.vector
    lanes = list(enumerate(grads))
    chains = [Chain(dve, sig, lane, trip) for lane, _ in lanes]
    flat = lambda ap: ap.rearrange("p b f -> p (b f)")

    def add(sum_, part):
        return v.tensor_copy(sum_, part) if mem else v.tensor_tensor(sum_, sum_, part, ALU.add)

    def in_turn(name, lane):
        if not mem:
            dve.wait_ge(*(sig.at(name, 0, trip, 1) if lane else sig.at(name, 1, trip, 0)))

    for lane, g in lanes:
        dve.wait_ge(*sig.at("sg", lane, trip, 1))
        v.tensor_tensor(g.a[0:rows, :], flat(banks(k, lane, 0, 2)[0:rows]), g.sg[0:rows, :], ALU.mult)\
            .then_inc(*sig.up("a", lane))
    for lane, g in lanes:
        ch, sg, a, dg = chains[lane], g.sg[0:rows, :], g.a[0:rows, :], g.g[0:rows, :]
        dve.wait_ge(*sig.at("a", lane, trip, 1))
        ch.link(v.tensor_tensor(dg, a, sg, ALU.mult))
        ch.link(v.tensor_tensor(dg, a, dg, ALU.subtract))
        ch.link(v.tensor_tensor(dg, dg, sg, ALU.add))
    for lane, g in lanes:
        e, pred = g.e[0:rows, :], bank(k, lane, 0)[0:rows, 0:D]
        dve.wait_ge(*sig.at("pred_ps", lane, trip, 1))
        if mem:
            chains[lane].link(v.tensor_tensor(e, pred, shared.swa_all[0:rows, TILES * D:], ALU.subtract))
            ins = v.tensor_scalar(e, e, float(B), None, ALU.mult)
        else:
            hold(k, dve, "vector")
            ins = v.tensor_tensor(e, pred, shared.swa_all[:, bass.ts(trip * 2 + lane, D)], ALU.subtract)
        ins.then_inc(*sig.up("e", lane))
    for lane, g in lanes:
        dg = g.g[0:rows, :]
        dve.wait_ge(*sig.at("da_ps", lane, trip, 1))
        v.tensor_tensor(dg, flat(banks(k, lane, 2, 2)[0:rows]), dg, ALU.mult).then_inc(*sig.up("dh", lane))
    for lane, g in lanes:
        dve.wait_ge(*sig.at("dw2_ps", lane, trip, 1))
        in_turn("dw2", lane)
        add(flat(shared.dw2), flat(banks(k, lane, 0, 4))).then_inc(*sig.up("dw2", lane))
    for lane, g in lanes:
        dve.wait_ge(*sig.at("dw1_ps", lane, trip, 1))
        in_turn("dw1", lane)
        add(flat(shared.dw1), flat(banks(k, lane, 0, 4))).then_inc(*sig.up("dw1", lane))
    for lane, g in lanes:
        dve.wait_ge(*sig.at("db_ps", lane, trip, 1))
        in_turn("done", lane)
        add(shared.db1, bank(k, lane, 0)[:, 0:HID // P])
        add(shared.db2[0:1, :], bank(k, lane, 1)[0:1, 0:D]).then_inc(*sig.up("done", lane))
        chains[lane].close()


def grad_gpsimd(k, pool, sig, shared, grads, trip, rows, mem=False):
    copy = k.nc.gpsimd.tensor_copy
    for lane, g in enumerate(grads):
        pool.wait_ge(*sig.at("done", lane, trip, 0))
        hold(k, pool, "gpsimd")
        if mem:
            copy(g.zT[:, :, 0:rows], shared.zT_all[:, :, B * SEQ:B * SEQ + MEM])
            copy(g.z[0:rows, :], shared.z_all[0:rows, TILES * D:]).then_inc(*sig.up("tok", lane))
        else:
            copy(g.zT, shared.zT_all[:, :, bass.ts(trip * 2 + lane, P)])
            copy(g.z, shared.z_all[:, bass.ts(trip * 2 + lane, D)]).then_inc(*sig.up("tok", lane))


def update_vector(k, dve, sig, buf):
    v = k.nc.vector
    ch = Chain(dve, sig, 0, 0)
    enter(k, dve, sig)
    keep, theta = buf.keep, scalar_of(k, "theta")
    ch.link(v.tensor_scalar(keep, scalar_of(k, "alpha"), -1.0, 1.0, ALU.mult, ALU.add))
    at, n = k.colpos["L0_attn_b1"]
    pairs = [(buf.dw1.rearrange("p c n -> p (c n)"), w_of(k, "L0_attn", "w1T")),
             (buf.dw2.rearrange("p c n -> p (c n)"), w_of(k, "L0_attn", "w2T")), (buf.db1, k.cols[:, at:at + n]),
             (buf.db2[0:1, :], row_of(k, "L0_attn", "b2"))]
    for grad, p in pairs:
        parts = grad.shape[0]
        ins = v.tensor_scalar(grad, grad, theta[0:parts], None, ALU.mult)
    ch.link(ins)
    for grad, p in pairs:
        parts = grad.shape[0]
        ins = v.scalar_tensor_tensor(grad, p, keep[0:parts], grad, ALU.mult, ALU.subtract)
    ins.then_inc(*sig.up("done"))
    ch.close()


def memory_hidden_tensor(k, pe, sig, lane, shared, m, trip):
    pe.wait_ge(*sig.at("tok", lane, trip, 1))
    for i in range(4):
        for c in (2 * i, 2 * i + 1):
            ins = proj_feature(k, bank(k, lane, i)[:, c % 2 * SEQ:(c % 2 + 1) * SEQ], shared.dw1, m.zT, c * P, P)
        ins.then_inc(*sig.up("h_ps", lane))


def memory_out_tensor(k, pe, sig, lane, shared, m, trip):
    pe.wait_ge(*sig.at("aT", lane, trip, 4))
    transpose_z_tensor(k, pe, sig, lane, trip, m.swa, bank(k, lane, 0)).then_inc(*sig.up("swaT_ps", lane))
    for t in (0, 1):
        ins = proj_token(k, bank(k, lane, 1)[:, t * D:(t + 1) * D], m.aT, t * P, shared.dw2, shared.db2[0:1, :],
                         HID // P)
    ins.then_inc(*sig.up("om_ps", lane))


def memory_omT_tensor(k, pe, sig, lane, shared, m, trip):
    pe.wait_ge(*sig.at("om", lane, trip, 1))
    transpose_z_tensor(k, pe, sig, lane, trip, m.om, bank(k, lane, 0)).then_inc(*sig.up("omT_ps", lane))
    for t in (0, 1):
        proj_token(k, bank(k, lane, 2)[:, t * D:(t + 1) * D], m.swaT, t * P, w_of(k, "L0_attn", "lin1", KC))


def memory_gate_tensor(k, pe, sig, lane, shared, m, trip):
    pe.wait_ge(*sig.at("omT", lane, trip, 1))
    for t in (0, 1):
        ins = proj_token(k, bank(k, lane, 3)[:, t * D:(t + 1) * D], m.omT, t * P, w_of(k, "L0_attn", "lin2", KC))
    ins.then_inc(*sig.up("gate_ps", lane))


def memory_tensor(k, pe, sig, shared, mems, trip):
    for phase in (memory_hidden_tensor, memory_out_tensor, memory_omT_tensor, memory_gate_tensor):
        for lane, m in enumerate(mems):
            phase(k, pe, sig, lane, shared, m, trip)


def memory_scalar(k, act, sig, shared, mems, trip):
    a = k.nc.scalar.activation
    flat = lambda ap: ap.rearrange("p c t -> p (c t)")
    lanes = list(enumerate(mems))
    for lane, m in lanes:
        for i in range(4):
            act.wait_ge(*sig.at("h_ps", lane, trip, i + 1))
            for c in (2 * i, 2 * i + 1):
                ins = a(m.aT[:, c, :], bank(k, lane, i)[:, c % 2 * SEQ:(c % 2 + 1) * SEQ], ACT.Sigmoid,
                        bias=shared.db1[:, c:c + 1])
            ins.then_inc(*sig.up("sg", lane))
    for lane, m in lanes:
        act.wait_ge(*sig.at("swaT_ps", lane, trip, 1))
        a(flat(m.swaT), bank(k, lane, 0), ACT.Copy)
        act.wait_ge(*sig.at("om_ps", lane, trip, 1))
        a(flat(m.om), bank(k, lane, 1), ACT.Copy).then_inc(*sig.up("om", lane))
    for lane, m in lanes:
        act.wait_ge(*sig.at("omT_ps", lane, trip, 1))
        a(flat(m.omT), bank(k, lane, 0), ACT.Copy).then_inc(*sig.up("omT", lane))
    for lane, m in lanes:
        act.wait_ge(*sig.at("gate_ps", lane, trip, 1))
        a(flat(m.g1), bank(k, lane, 2), ACT.Sigmoid)
        a(flat(m.g2), bank(k, lane, 3), ACT.Sigmoid).then_inc(*sig.up("gate", lane))


def memory_vector(k, dve, sig, shared, mems, trip):
    v = k.nc.vector
    chains = [Chain(dve, sig, lane, trip) for lane in (0, 1)]
    for lane in (0, 1):
        stats_vector(k, dve, sig, lane, trip)
    for lane, m in enumerate(mems):
        for i in range(4):
            dve.wait_ge(*sig.at("sg", lane, trip, i + 1))
            for c in (2 * i, 2 * i + 1):
                ins = v.scalar_tensor_tensor(m.aT[:, c, :], bank(k, lane, i)[:, c % 2 * SEQ:(c % 2 + 1) * SEQ],
                                             shared.db1[:, c:c + 1], m.aT[:, c, :], ALU.add, ALU.mult)
            ins.then_inc(*sig.up("aT", lane))
    for lane, m in enumerate(mems):
        ch = chains[lane]
        dve.wait_ge(*sig.at("gate", lane, trip, 1))
        v.tensor_tensor(m.g1, m.g1, m.swa, ALU.mult)
        ch.link(v.tensor_tensor(m.g2, m.g2, m.om, ALU.mult))
        ch.link(v.tensor_tensor(m.g1, m.g1, m.g2, ALU.add))
        x = x_of(k, trip, lane)
        v.tensor_tensor(x, x, m.g1, ALU.add).then_inc(*sig.up("done", lane))
        ch.close()


def memory_gpsimd(k, pool, sig, shared, mems, trip):
    copy = k.nc.gpsimd.tensor_copy
    for lane, m in enumerate(mems):
        pool.wait_ge(*sig.at("done", lane, trip, 0))
        hold(k, pool, "gpsimd")
        at = trip * 2 + lane
        copy(m.zT, shared.zT_all[:, :, bass.ts(at, SEQ)])
        copy(m.swa.rearrange("p t d -> p (t d)"), shared.swa_all[:, bass.ts(at, 2 * D)])\
            .then_inc(*sig.up("tok", lane))


def L0_attn_tensor(k, pe, s):
    b = s.buf
    enter(k, pe, s.window_mem)
    pe.wait_ge(k.mem_loaded, 32)
    window_tensor(k, pe, s.window_mem, b, b.windows[0:1], 0, mem=True)
    enter(k, pe, s.window)
    with pe.Fori(0, s.window.trips) as trip:
        window_tensor(k, pe, s.window, b, b.windows, trip)
    enter(k, pe, s.grad_mem)
    grad_tensor(k, pe, s.grad_mem, b.grads[0:1], 0, MEM)
    enter(k, pe, s.grad)
    with pe.Fori(0, s.grad.trips) as trip:
        grad_tensor(k, pe, s.grad, b.grads, trip, P)
    enter(k, pe, s.memory)
    with pe.Fori(0, s.memory.trips) as trip:
        memory_tensor(k, pe, s.memory, b, b.mems, trip)


def L0_attn_scalar(k, act, s):
    b = s.buf
    enter(k, act, s.window_mem)
    window_scalar(k, act, s.window_mem, b, b.windows[0:1], 0, mem=True)
    enter(k, act, s.window)
    with act.Fori(0, s.window.trips) as trip:
        window_scalar(k, act, s.window, b, b.windows, trip)
    enter(k, act, s.grad_mem)
    grad_scalar(k, act, s.grad_mem, b.grads[0:1], 0, MEM)
    enter(k, act, s.grad)
    with act.Fori(0, s.grad.trips) as trip:
        grad_scalar(k, act, s.grad, b.grads, trip, P)
    enter(k, act, s.memory)
    with act.Fori(0, s.memory.trips) as trip:
        memory_scalar(k, act, s.memory, b, b.mems, trip)


def L0_attn_vector(k, dve, s, x_loaded, const_loaded, n_const):
    b = s.buf
    v = k.nc.vector
    v.memset(k.xs[:, 0:SPARE, :], 0.0)
    v.memset(k.xs[:, SPARE + TILES:, :], 0.0)
    v.memset(k.norm[:, TILES:, :], 0.0).then_inc(s.first.sems["done"][0], 1)
    v.memset(k.rstd[:, TILES:], 0.0).then_inc(s.first.sems["done"][1], 1)
    dve.wait_ge(x_loaded, 16)
    norms_vector(k, dve, s.norms)
    dve.wait_ge(const_loaded, n_const)
    enter(k, dve, s.window_mem)
    window_vector(k, dve, s.window_mem, b, b.windows[0:1], 0, mem=True)
    enter(k, dve, s.window)
    with dve.Fori(0, s.window.trips) as trip:
        window_vector(k, dve, s.window, b, b.windows, trip)
    enter(k, dve, s.grad_mem)
    grad_vector(k, dve, s.grad_mem, b, b.grads[0:1], 0, MEM, mem=True)
    enter(k, dve, s.grad)
    with dve.Fori(0, s.grad.trips) as trip:
        grad_vector(k, dve, s.grad, b, b.grads, trip, P)
    update_vector(k, dve, s.update, b)
    enter(k, dve, s.memory)
    with dve.Fori(0, s.memory.trips) as trip:
        memory_vector(k, dve, s.memory, b, b.mems, trip)


def L0_attn_gpsimd(k, pool, s):
    b = s.buf
    enter(k, pool, s.window)
    with pool.Fori(0, s.window.trips) as trip:
        window_gpsimd(k, pool, s.window, b, b.windows, trip)
    enter(k, pool, s.grad_mem)
    grad_gpsimd(k, pool, s.grad_mem, b, b.grads[0:1], 0, MEM, mem=True)
    enter(k, pool, s.grad)
    with pool.Fori(0, s.grad.trips) as trip:
        grad_gpsimd(k, pool, s.grad, b, b.grads, trip, P)
    enter(k, pool, s.memory)
    with pool.Fori(0, s.memory.trips) as trip:
        memory_gpsimd(k, pool, s.memory, b, b.mems, trip)


def experts_plan(k):
    c, bufs = lane_buffers(k)
    for buf in bufs:
        buf.l, buf.gate, buf.m, buf.rank = c.take(2, 8), c.take(2, 8), c.take(4), c.take(2, 8)
        buf.gt, buf.eq = c.take(128), c.take(128)
        buf.th, buf.aT = c.take(2, SEQ), c.take(2, SEQ)
    norms = norms_plan(k, "L0_ffn")
    sig = Signals(k.signals, "L0_ffn", B // 2, 2, z=1, zT_ps=1, zT=1, router_ps=1, logit=1, gate=1, h_ps=E_ALL,
                  th=E_ALL, aT=E_ALL, out_ps=E_ROUTED + 1, added=E_ROUTED, done=1, dve_step=k.steps["L0_ffn"])
    return Bag(bufs=bufs, norms=norms, sig=sig)


def experts_up_tensor(k, pe, sig, lane, trip, buf, e):
    w1, w3 = (w_of(k, "L0_ffn", n, E_ALL * KC) for n in ("w1", "w3"))
    if e >= 2:
        pe.wait_ge(*sig.at("aT", lane, trip, e - 1))
    for i, w in enumerate((w1, w3)):
        ins = products(k, bank(k, lane, e % 2)[:, i * SEQ:(i + 1) * SEQ],
                       [(w[:, e * KC + c, :], buf.zT[:, c, :]) for c in range(KC)])
    ins.then_inc(*sig.up("h_ps", lane))


def experts_down_tensor(k, pe, sig, lane, trip, buf, e):
    w2 = w_of(k, "L0_ffn", "w2", E_ALL)
    shared = e >= E_ROUTED
    out = bank(k, lane, 2 + e % 2 if not shared else 2)
    pe.wait_ge(*sig.at("aT", lane, trip, e + 1))
    if e == 1:
        pe.wait_ge(*sig.at("logit", lane, trip, 1))
    if 2 <= e <= E_ROUTED:
        pe.wait_ge(*sig.at("added", lane, trip, e - 1))
    for t in (0, 1):
        ins = k.nc.tensor.matmul(out[:, t * D:(t + 1) * D], buf.aT[:, e % 2, t * P:(t + 1) * P], w2[:, e, :],
                                 start=not shared or (e == E_ROUTED and t == 0), stop=not shared or e == E_ALL - 1,
                                 skip_group_check=shared)
    if e != E_ROUTED:
        ins.then_inc(*sig.up("out_ps", lane))


def L0_ffn_tensor(k, pe, s):
    enter(k, pe, s.sig)
    with pe.Fori(0, s.sig.trips) as trip:
        zT_tensor(k, pe, s.sig, trip, s.bufs, 0)
        for lane, buf in enumerate(s.bufs):
            pe.wait_ge(*s.sig.at("zT", lane, trip, 1))
            for t in (0, 1):
                ins = proj_token(k, bank(k, lane, 3)[:, t * 8:(t + 1) * 8], buf.zT, t * P,
                                 w_of(k, "L0_ffn", "router", KC), row_of(k, "L0_ffn", "rb"))
            ins.then_inc(*s.sig.up("router_ps", lane))
        for e in range(E_ALL + 1):
            for lane, buf in enumerate(s.bufs):
                if e < E_ALL:
                    experts_up_tensor(k, pe, s.sig, lane, trip, buf, e)
            for lane, buf in enumerate(s.bufs):
                if e:
                    experts_down_tensor(k, pe, s.sig, lane, trip, buf, e - 1)


def L0_ffn_scalar(k, act, s):
    a = k.nc.scalar.activation
    enter(k, act, s.sig)
    with act.Fori(0, s.sig.trips) as trip:
        zT_scalar(k, act, s.sig, trip, s.bufs, 0)
        for lane, buf in enumerate(s.bufs):
            act.wait_ge(*s.sig.at("logit", lane, trip, 1))
            a(buf.gate, buf.gate, ACT.Exp).then_inc(*s.sig.up("gate", lane))
        for e in range(E_ALL):
            for lane, buf in enumerate(s.bufs):
                act.wait_ge(*s.sig.at("h_ps", lane, trip, e + 1))
                if e >= 2:
                    act.wait_ge(*s.sig.at("aT", lane, trip, e - 1))
                a(buf.th[:, e % 2, :], bank(k, lane, e % 2)[:, 0:SEQ], ACT.Tanh, scale=0.5)\
                    .then_inc(*s.sig.up("th", lane))


def logits_vector(k, dve, sig, lane, trip, ch, buf):
    v = k.nc.vector
    dve.wait_ge(*sig.at("router_ps", lane, trip, 1))
    ch.link(v.tensor_copy(buf.l, bank(k, lane, 3)[:, 0:16].rearrange("p (t e) -> p t e", t=2)))
    ch.link(v.tensor_reduce(buf.m[:, 0:2], buf.l, AX, ALU.max))
    v.tensor_tensor(buf.gate, buf.l, buf.m[:, 0:2].unsqueeze(2).broadcast_to([P, 2, 8]), ALU.subtract)\
        .then_inc(*sig.up("logit", lane))


def gates_vector(k, dve, sig, lane, trip, ch, buf):
    v = k.nc.vector
    gt, eq = (b.rearrange("p (t e f) -> p t e f", t=2, e=8) for b in (buf.gt, buf.eq))
    for t in (0, 1):
        mine = buf.l[:, t, :].unsqueeze(2).broadcast_to([P, 8, 8])
        other = buf.l[:, t, :].unsqueeze(1).broadcast_to([P, 8, 8])
        v.tensor_tensor(gt[:, t], other, mine, ALU.is_gt)
        ins = v.tensor_tensor(eq[:, t], other, mine, ALU.is_equal)
    ch.link(ins)
    for t in (0, 1):
        ins = v.tensor_tensor(eq[:, t], eq[:, t], k.earlier.rearrange("p (e f) -> p e f", e=8), ALU.mult)
    ch.link(ins)
    ch.link(v.tensor_tensor(buf.gt, buf.gt, buf.eq, ALU.add))
    ch.link(v.tensor_reduce(buf.rank.rearrange("p t e -> p (t e)"), buf.gt.rearrange("p (a f) -> p a f", f=8), AX, ALU.add))
    dve.wait_ge(*sig.at("gate", lane, trip, 1))
    ch.link(v.scalar_tensor_tensor(buf.gate, buf.rank, 2.0, buf.gate, ALU.is_lt, ALU.mult))
    ch.link(v.tensor_reduce(buf.m[:, 0:2], buf.gate, AX, ALU.add))
    ch.link(v.reciprocal(buf.m[:, 2:4], buf.m[:, 0:2]))
    ch.link(v.tensor_tensor(buf.gate, buf.gate, buf.m[:, 2:4].unsqueeze(2).broadcast_to([P, 2, 8]), ALU.mult))


def expert_act_vector(k, dve, sig, lane, trip, ch, buf, e):
    v = k.nc.vector
    h = bank(k, lane, e % 2)
    aT = buf.aT[:, e % 2, :]
    dve.wait_ge(*sig.at("th", lane, trip, e + 1))
    if e == 2:
        dve.wait_ge(*sig.at("out_ps", lane, trip, 1))
    elif 2 < e <= 9:
        dve.wait_ge(*sig.at("out_ps", lane, trip, e - 1))
    ch.link(v.scalar_tensor_tensor(aT, buf.th[:, e % 2, :], 1.0, h[:, 0:SEQ], ALU.add, ALU.mult))
    v.scalar_tensor_tensor(aT, aT, 0.5, h[:, SEQ:2 * SEQ], ALU.mult, ALU.mult).then_inc(*sig.up("aT", lane))


def expert_add_vector(k, dve, sig, lane, trip, buf, e):
    v = k.nc.vector
    x = x_of(k, trip, lane)
    out = bank(k, lane, 2 + e % 2).rearrange("p (t d) -> p t d", t=2)
    dve.wait_ge(*sig.at("out_ps", lane, trip, e + 1))
    if e:
        dve.wait_ge(*sig.at("added", lane, trip, e))
    hold(k, dve, "vector")
    for t in (0, 1):
        ins = v.scalar_tensor_tensor(x[:, t, :], out[:, t, :], buf.gate[:, t, e:e + 1], x[:, t, :], ALU.mult, ALU.add)
    ins.then_inc(*sig.up("added", lane))


def L0_ffn_vector(k, dve, s):
    enter(k, dve, s.sig)
    norms_vector(k, dve, s.norms)
    with dve.Fori(0, s.sig.trips) as trip:
        chains = [Chain(dve, s.sig, lane, trip) for lane in (0, 1)]
        for lane, buf in enumerate(s.bufs):
            ln_vector(k, dve, s.sig, lane, trip, buf)
        for lane in (0, 1):
            stats_vector(k, dve, s.sig, lane, trip)
        for lane, buf in enumerate(s.bufs):
            logits_vector(k, dve, s.sig, lane, trip, chains[lane], buf)
        for lane, buf in enumerate(s.bufs):
            gates_vector(k, dve, s.sig, lane, trip, chains[lane], buf)
        for e in range(E_ALL + 1):
            for lane, buf in enumerate(s.bufs):
                if e < E_ALL:
                    expert_act_vector(k, dve, s.sig, lane, trip, chains[lane], buf, e)
            for lane, buf in enumerate(s.bufs):
                if 1 <= e <= E_ROUTED:
                    expert_add_vector(k, dve, s.sig, lane, trip, buf, e - 1)
        for lane in (0, 1):
            x = x_of(k, trip, lane)
            dve.wait_ge(*s.sig.at("added", lane, trip, E_ROUTED))
            dve.wait_ge(*s.sig.at("out_ps", lane, trip, E_ROUTED + 1))
            k.nc.vector.tensor_tensor(x, x, bank(k, lane, 2).rearrange("p (t d) -> p t d", t=2), ALU.add)\
                .then_inc(*s.sig.up("done", lane))
            chains[lane].close()


def self_qk_tensor(k, pe, sig, lane, trip, a, buf, stage, left, n=""):
    pe.wait_ge(*sig.at("zT", lane, trip, 1))
    pe.wait_ge(*sig.at(left, lane, trip, 0))
    for i, w in enumerate((w_of(k, stage, "wq" + n, KC), w_of(k, stage, "wk" + n, KC))):
        for c in range(HC):
            ins = proj_feature(k, bank(k, lane, 2 * i + c // 2)[:, c % 2 * SEQ:(c % 2 + 1) * SEQ], w, buf.zT,
                               c * P, P)
    ins.then_inc(*sig.up(a.p + "qkv_ps", lane))


def self_v_tensor(k, pe, sig, lane, trip, a, buf, stage, n=""):
    pe.wait_ge(*sig.at(a.p + "q", lane, trip, 1))
    for t in (0, 1):
        ins = proj_token(k, bank(k, lane, t)[:, 0:H * VW], buf.zT, t * P, w_of(k, stage, "wv" + n, KC),
                         row_of(k, stage, "bv" + n))
    ins.then_inc(*sig.up(a.p + "v_ps", lane))


def self_kv_vector(k, dve, sig, lane, trip, a, buf, bk):
    v = k.nc.vector
    dve.wait_ge(*sig.at(a.p + "qkv_ps", lane, trip, 1))
    for c in range(HC):
        v.tensor_scalar(buf.kT[:, c, :], bank(k, lane, 2 + c // 2)[:, c % 2 * SEQ:(c % 2 + 1) * SEQ],
                        col_of(k, bk, c), None, ALU.add)
    dve.wait_ge(*sig.at(a.p + "v_ps", lane, trip, 1))
    v.tensor_copy(buf.v, banks(k, lane, 0, 2)[:, :, 0:H * VW]).then_inc(*sig.up(a.p + "kv", lane))


def block_plan(k):
    a = attention("self")
    c, bufs = lane_buffers(k)
    for buf in bufs:
        attention_buffers(c, a, buf)
        buf.x1, buf.x1T = c.take(2, D), c.take(KC, SEQ)
        buf.f = buf.s.rearrange("p c t -> p (c t)")[:, 0:FF // P * SEQ].rearrange("p (c t) -> p c t", t=SEQ)
    norms = norms_plan(k, "L1_attn")
    sig = Signals(k.signals, "L1_attn", B // 2, 2, AHEAD, z=1, zT_ps=1, zT=1, qkv_ps=1, q=1, v_ps=1, kv=1, x1=1, x1T_ps=1,
                  x1T=1, f_ps=1, f=1, out_ps=1, taken=1, done=1, dve_step=k.steps["L1_attn"], **attention_signals(a))
    return Bag(norms=norms, a=a, bufs=bufs, sig=sig)


def L1_attn_tensor(k, pe, s):
    sig, st = s.sig, "L1_attn"
    enter(k, pe, sig)
    zT_tensor(k, pe, sig, 0, s.bufs, 2)
    with pe.Fori(0, sig.trips) as trip:
        for lane, buf in enumerate(s.bufs):
            self_qk_tensor(k, pe, sig, lane, trip, s.a, buf, st, "taken")
        for lane, buf in enumerate(s.bufs):
            self_v_tensor(k, pe, sig, lane, trip, s.a, buf, st)
        for lane in (0, 1):
            qkv_wait_tensor(k, pe, sig, lane, trip, s.a)
        attention_tensor(k, pe, sig, trip, s.a, s.bufs)
        for lane, buf in enumerate(s.bufs):
            pe.wait_ge(*sig.at("x1", lane, trip, 1))
            transpose_z_tensor(k, pe, sig, lane, trip, buf.x1, bank(k, lane, 2)).then_inc(*sig.up("x1T_ps", lane))
        for lane, buf in enumerate(s.bufs):
            pe.wait_ge(*sig.at("x1T", lane, trip, 1))
            for c in range(FF // P):
                ins = proj_feature(k, bank(k, lane, c // 2)[:, c % 2 * SEQ:(c % 2 + 1) * SEQ],
                                   w_of(k, st, "ff1", KC), buf.x1T, c * P, P)
            ins.then_inc(*sig.up("f_ps", lane))
        zT_tensor(k, pe, sig, trip + 1, s.bufs, 2)
        for lane, buf in enumerate(s.bufs):
            pe.wait_ge(*sig.at("f", lane, trip, 1))
            for t in (0, 1):
                ins = proj_token(k, bank(k, lane, 3)[:, t * D:(t + 1) * D], buf.f, t * P,
                                 w_of(k, st, "ff2", FF // P), row_of(k, st, "ff2b"), FF // P)
            ins.then_inc(*sig.up("out_ps", lane))


def L1_attn_scalar(k, act, s):
    sig = s.sig
    enter(k, act, sig)
    zT_scalar(k, act, sig, 0, s.bufs, 2)
    with act.Fori(0, sig.trips) as trip:
        for lane, buf in enumerate(s.bufs):
            q_scalar(k, act, sig, lane, trip, s.a, buf, "L1_attn_bq")
        attention_scalar(k, act, sig, trip, s.a, s.bufs)
        for lane, buf in enumerate(s.bufs):
            act.wait_ge(*sig.at("x1T_ps", lane, trip, 1))
            k.nc.scalar.activation(buf.x1T.rearrange("p c t -> p (c t)"), bank(k, lane, 2), ACT.Copy)\
                .then_inc(*sig.up("x1T", lane))
        for lane, buf in enumerate(s.bufs):
            act.wait_ge(*sig.at("f_ps", lane, trip, 1))
            for c in range(FF // P):
                ins = k.nc.scalar.activation(buf.f[:, c, :],
                                             bank(k, lane, c // 2)[:, c % 2 * SEQ:(c % 2 + 1) * SEQ], ACT.Relu,
                                             bias=col_of(k, "L1_attn_ff1b", c))
            ins.then_inc(*sig.up("f", lane))
        zT_scalar(k, act, sig, trip + 1, s.bufs, 2)


def gained_ln_vector(k, ch, src, dst, st, gain, shift):
    v = k.nc.vector
    ch.link(layernorm(k, ch, src, dst, st))
    ch.link(v.tensor_tensor(dst, dst, gain.unsqueeze(1).broadcast_to([P, 2, D]), ALU.mult))
    return v.tensor_tensor(dst, dst, shift.unsqueeze(1).broadcast_to([P, 2, D]), ALU.add)


def L1_attn_vector(k, dve, s):
    v, sig = k.nc.vector, s.sig
    g1, b1, g2, b2 = (spread_of(k, "L1_attn", n) for n in SPREAD["L1_attn"])
    enter(k, dve, sig)
    norms_vector(k, dve, s.norms)
    first_z_vector(k, sig, s.bufs)
    with dve.Fori(0, sig.trips) as trip:
        chains = [Chain(dve, sig, lane, trip) for lane in (0, 1)]
        for lane in (0, 1):
            stats_vector(k, dve, sig, lane, trip)
        for lane, buf in enumerate(s.bufs):
            self_kv_vector(k, dve, sig, lane, trip, s.a, buf, "L1_attn_bk")
        attention_vector(k, dve, sig, trip, chains, s.a, s.bufs)
        for lane, buf in enumerate(s.bufs):
            ch = chains[lane]
            dve.wait_ge(*sig.at("o", lane, trip, len(s.a.rounds)))
            ch.link(v.tensor_tensor(buf.z, buf.z, buf.o, ALU.add))
            gained_ln_vector(k, ch, buf.z, buf.x1, buf.st, g1, b1).then_inc(*sig.up("x1", lane))
        later_z_vector(k, dve, sig, s.bufs, trip)
        for lane, buf in enumerate(s.bufs):
            ch = chains[lane]
            y = buf.o
            dve.wait_ge(*sig.at("out_ps", lane, trip, 1))
            ch.link(v.tensor_tensor(buf.x1, buf.x1, bank(k, lane, 3).rearrange("p (t d) -> p t d", t=2), ALU.add))
            dve.sem_inc(*sig.up("taken", lane))
            ch.link(gained_ln_vector(k, ch, buf.x1, y, buf.st, g2, b2))
            x = x_of(k, trip, lane)
            v.tensor_tensor(x, x, y, ALU.add).then_inc(*sig.up("done", lane))
            ch.close()


def two_attentions_plan(k):
    a, b = attention("self"), attention("cross", p="c_")
    c, bufs = lane_buffers(k)
    for buf in bufs:
        attention_buffers(c, a, buf)
        buf.second = Bag(zT=buf.zT, ctxT=c.take(KC, CTX), qT=buf.qT, kT=c.take(HC, 4 * CTX), v=buf.v, s=buf.s,
                                     probT=buf.probT, raw=buf.raw, o=buf.o, oT=buf.oT, m=buf.m,
                         rec=buf.rec, sums=buf.sums)
        buf.ctxT = buf.second.ctxT
    norms = norms_plan(k, "L1_xattn")
    sig = Signals(k.signals, "L1_xattn", B // 2, 2, AHEAD, z=1, zT_ps=1, zT=1, ctx=1, qkv_ps=1, q=1, v_ps=1, kv=1, oT_ps=1,
                  oT=1, hT_ps=1, zT2=1, c_qkv_ps=1, c_q=1, c_kv=1, c_oT_ps=1, c_oT=1, out_ps=1, done=1,
                  dve_step=k.steps["L1_xattn"], **attention_signals(a), **attention_signals(b))
    return Bag(norms=norms, a=a, b=b, bufs=bufs, seconds=[buf.second for buf in bufs], sig=sig)


def L1_xattn_tensor(k, pe, s):
    sig, st = s.sig, "L1_xattn"
    enter(k, pe, sig)
    zT_tensor(k, pe, sig, 0, s.bufs)
    with pe.Fori(0, sig.trips) as trip:
        for lane, buf in enumerate(s.bufs):
            self_qk_tensor(k, pe, sig, lane, trip, s.a, buf, st, "done", "1")
        for lane, buf in enumerate(s.bufs):
            self_v_tensor(k, pe, sig, lane, trip, s.a, buf, st, "1")
        for lane in (0, 1):
            qkv_wait_tensor(k, pe, sig, lane, trip, s.a)
        attention_tensor(k, pe, sig, trip, s.a, s.bufs)
        for lane, buf in enumerate(s.bufs):
            oT_tensor(k, pe, sig, lane, trip, s.a, buf)
        for lane, buf in enumerate(s.bufs):
            pe.wait_ge(*sig.at("oT", lane, trip, 1))
            for c in range(KC):
                ins = proj_feature(k, bank(k, lane, 0)[:, c * SEQ:(c + 1) * SEQ], w_of(k, st, "wo1", KC), buf.oT,
                                   c * P, P)
            ins.then_inc(*sig.up("hT_ps", lane))
        for lane, buf in enumerate(s.seconds):
            cross_qkv_tensor(k, pe, sig, lane, trip, s.b, buf, st, "2")
        for lane in (0, 1):
            qkv_wait_tensor(k, pe, sig, lane, trip, s.b)
        attention_tensor(k, pe, sig, trip, s.b, s.seconds)
        for lane, buf in enumerate(s.seconds):
            oT_tensor(k, pe, sig, lane, trip, s.b, buf)
        zT_tensor(k, pe, sig, trip + 1, s.bufs)
        for lane, buf in enumerate(s.seconds):
            out_tensor(k, pe, sig, lane, trip, s.b, buf, w_of(k, st, "wo2", KC), row_of(k, st, "bo2"))


def L1_xattn_scalar(k, act, s):
    sig = s.sig
    enter(k, act, sig)
    zT_scalar(k, act, sig, 0, s.bufs)
    with act.Fori(0, sig.trips) as trip:
        for lane, buf in enumerate(s.bufs):
            q_scalar(k, act, sig, lane, trip, s.a, buf, "L1_xattn_bq1")
        attention_scalar(k, act, sig, trip, s.a, s.bufs)
        for lane, buf in enumerate(s.bufs):
            oT_scalar(k, act, sig, lane, trip, s.a, buf)
        for lane, buf in enumerate(s.bufs):
            act.wait_ge(*sig.at("hT_ps", lane, trip, 1))
            for c in range(KC):
                ins = k.nc.scalar.activation(buf.zT[:, c, :], bank(k, lane, 0)[:, c * SEQ:(c + 1) * SEQ],
                                             ACT.Identity, bias=col_of(k, "L1_xattn_bo1", c))
            ins.then_inc(*sig.up("zT2", lane))
        for lane, buf in enumerate(s.seconds):
            q_scalar(k, act, sig, lane, trip, s.b, buf, "L1_xattn_bq2")
        attention_scalar(k, act, sig, trip, s.b, s.seconds)
        for lane, buf in enumerate(s.seconds):
            oT_scalar(k, act, sig, lane, trip, s.b, buf)
        zT_scalar(k, act, sig, trip + 1, s.bufs)


def L1_xattn_vector(k, dve, s):
    sig = s.sig
    enter(k, dve, sig)
    norms_vector(k, dve, s.norms)
    keys_vector(k, s.seconds)
    first_z_vector(k, sig, s.bufs)
    with dve.Fori(0, sig.trips) as trip:
        chains = [Chain(dve, sig, lane, trip) for lane in (0, 1)]
        for lane in (0, 1):
            stats_vector(k, dve, sig, lane, trip)
        for lane, buf in enumerate(s.bufs):
            self_kv_vector(k, dve, sig, lane, trip, s.a, buf, "L1_xattn_bk1")
        attention_vector(k, dve, sig, trip, chains, s.a, s.bufs)
        for lane, buf in enumerate(s.seconds):
            cross_kv_vector(k, dve, sig, lane, trip, s.b, buf, "L1_xattn_bk2")
        attention_vector(k, dve, sig, trip, chains, s.b, s.seconds)
        later_z_vector(k, dve, sig, s.bufs, trip)
        for lane, buf in enumerate(s.bufs):
            residual_vector(k, dve, sig, lane, trip)
            chains[lane].close()


def round_e4m3(k, link, u, power, near, out):
    v = k.nc.vector
    link(v.tensor_scalar(power.bitcast(U32), u.bitcast(U32), 0x7F800000, None, ALU.bitwise_and))
    link(v.tensor_scalar(power, power, 2.0 ** -6, 1.5 * 2.0 ** 20, ALU.max, ALU.mult))
    link(v.tensor_tensor(near, u, power, ALU.add))
    link(v.tensor_tensor(near, near, power, ALU.subtract))
    link(v.tensor_tensor(power, near, near, ALU.mult))
    link(v.tensor_scalar(power, power, 448.0 ** 2, BIG, ALU.is_gt, ALU.mult))
    link(v.tensor_scalar(power, power, BIG, 0.0, ALU.mult, ALU.mult))
    return v.tensor_tensor(out, power, near, ALU.add)


def inverses(k, link, s, w):
    v = k.nc.vector

    def top(out, src, bits):
        link(v.tensor_scalar(out.bitcast(U32), src.bitcast(U32), 0xFFFFFFFF - (1 << (24 - bits)) + 1, None,
                             ALU.bitwise_and))

    link(v.reciprocal(w.r, s))
    top(w.rh, w.r, 12)
    link(v.tensor_tensor(w.rl, w.r, w.rh, ALU.subtract))
    top(w.sh, s, 12)
    link(v.tensor_tensor(w.sl, s, w.sh, ALU.subtract))
    link(v.tensor_tensor(w.e, w.rh, w.sh, ALU.mult))
    link(v.tensor_scalar(w.e, w.e, -1.0, 1.0, ALU.mult, ALU.add))
    for i, j in ((w.rh, w.sl), (w.rl, w.sh), (w.rl, w.sl)):
        link(v.tensor_tensor(w.part, i, j, ALU.mult))
        link(v.tensor_tensor(w.e, w.e, w.part, ALU.subtract))
    top(w.r1, w.r, 16)
    link(v.tensor_tensor(w.r2, w.r, w.r1, ALU.subtract))
    link(v.tensor_tensor(w.e, w.e, w.r, ALU.mult))
    link(v.tensor_tensor(w.r2, w.r2, w.e, ALU.add))


def over(k, link, out, src, w, i):
    v = k.nc.vector
    link(v.tensor_scalar(out, src, w.r2[:, i:i + 1], None, ALU.mult))
    link(v.scalar_tensor_tensor(out, src, w.r1[:, i:i + 1], out, ALU.mult, ALU.add))


def fp8_plan(k):
    c, bufs = lane_buffers(k)
    for buf in bufs:
        buf.zb, buf.q = c.take(KC, SEQ, dt=BF16), c.take(KC, SEQ, dt=BF16)
        buf.u, buf.power, buf.near = c.take(KC * SEQ), c.take(KC * SEQ), c.take(KC * SEQ)
        buf.y = c.take(2, D, dt=BF16)
    w = Bag(q=c.take(KC, D, dt=BF16), u=c.take(KC * D), power=c.take(KC * D), near=c.take(KC * D),
                        scale=c.take(1), **{n: c.take(2) for n in ("r", "rh", "rl", "sh", "sl", "e", "part", "r1", "r2")})
    norms = norms_plan(k, "L1_ffn")
    prep = Signals(k.signals, "L1_ffn", 1, 1, dve_step=k.steps["fp8_prep"], done=1)
    sig = Signals(k.signals, "L1_ffn", B // 2, 2, z=1, zT_ps=1, zT=1, q=1, out_ps=1, done=1,
                  dve_step=k.steps["L1_ffn"])
    return Bag(norms=norms, bufs=bufs, w=w, prep=prep, sig=sig)


def L1_ffn_tensor(k, pe, s):
    sig = s.sig
    enter(k, pe, sig)
    with pe.Fori(0, sig.trips) as trip:
        zT_tensor(k, pe, sig, trip, s.bufs, 0)
        for lane, buf in enumerate(s.bufs):
            pe.wait_ge(*sig.at("q", lane, trip, 1))
            for t in (0, 1):
                ins = proj_token(k, bank(k, lane, 1)[:, t * D:(t + 1) * D], buf.q, t * P, s.w.q)
            ins.then_inc(*sig.up("out_ps", lane))


def L1_ffn_scalar(k, act, s):
    enter(k, act, s.sig)
    with act.Fori(0, s.sig.trips) as trip:
        for lane, buf in enumerate(s.bufs):
            act.wait_ge(*s.sig.at("zT_ps", lane, trip, 1))
            k.nc.scalar.activation(buf.zb.rearrange("p c t -> p (c t)"), bank(k, lane, 0), ACT.Copy)\
                .then_inc(*s.sig.up("zT", lane))


def L1_ffn_vector(k, dve, s):
    v, sig, w = k.nc.vector, s.sig, s.w
    enter(k, dve, s.prep)
    norms_vector(k, dve, s.norms)
    ch = Chain(dve, s.prep, 0, 0)
    i = SCALARS.index("s_in")
    inverses(k, ch.link, k.scalars[:, i:i + 2], w)
    over(k, ch.link, w.u, k.fp8_kernel, w, 1)
    round_e4m3(k, ch.link, w.u, w.power, w.near, w.q.rearrange("p c d -> p (c d)"))
    v.tensor_tensor(w.scale, scalar_of(k, "s_in"), scalar_of(k, "s_k"), ALU.mult).then_inc(*s.prep.up("done"))
    ch.close()
    enter(k, dve, sig)
    with dve.Fori(0, sig.trips) as trip:
        chains = [Chain(dve, sig, lane, trip) for lane in (0, 1)]
        for lane, buf in enumerate(s.bufs):
            ln_vector(k, dve, sig, lane, trip, buf)
        for lane in (0, 1):
            stats_vector(k, dve, sig, lane, trip)
        for lane, buf in enumerate(s.bufs):
            ch = chains[lane]
            dve.wait_ge(*sig.at("zT", lane, trip, 1))
            over(k, ch.link, buf.u, buf.zb.rearrange("p c t -> p (c t)"), w, 0)
            round_e4m3(k, ch.link, buf.u, buf.power, buf.near, buf.q.rearrange("p c t -> p (c t)"))\
                .then_inc(*sig.up("q", lane))
        for lane, buf in enumerate(s.bufs):
            ch = chains[lane]
            x = x_of(k, trip, lane)
            dve.wait_ge(*sig.at("out_ps", lane, trip, 1))
            ch.link(v.tensor_scalar(buf.y.rearrange("p t d -> p (t d)"), bank(k, lane, 1), w.scale, None, ALU.mult))
            ch.link(v.tensor_tensor(buf.y, buf.y, k.fp8_bias.unsqueeze(1).broadcast_to([P, 2, D]), ALU.add))
            v.tensor_tensor(x, x, buf.y, ALU.add).then_inc(*sig.up("done", lane))
            ch.close()


GROUPS = NH1 // 4
PARTS = 3
PAIRS = PARTS * PARTS
ROWS_DMAS = 2 * PAIRS + PARTS


def width_one_plan(k):
    c, bufs = lane_buffers(k)
    for buf in bufs:
        buf.parts = c.take(PARTS, 3, SEQ, dt=BF16)
        buf.v1 = c.take(2, NH1, 2)
        buf.oT = c.take(3, SEQ)
        buf.qrows, buf.krows = c.take(16, SEQ, dt=BF16), c.take(16, SEQ, dt=BF16)
        buf.raw = c.take(GROUPS, SEQ)
        buf.qkm, buf.rest = buf.raw[:, 0:3, :], buf.raw[:, 3:6, :]
        buf.kmax, buf.kmin = buf.raw[:, 6, :], buf.raw[:, 7, :]
    prob = c.take(2, 3, 512)
    norms = norms_plan(k, "L2_attn")
    prep = Signals(k.signals, "L2_attn", 1, 2, done=1)
    sig = Signals(k.signals, "L2_attn", B // 2, 2, z=1, zT_ps=1, zT=1, qkv_ps=1, kv=1, parts=1, s_ps=GROUPS,
                  prob=GROUPS, pv_ps=GROUPS, raw=GROUPS // 2, oT=1, out_ps=1, done=1, dve_step=k.steps["L2_attn"])
    moved = Signals(k.signals, "L2_attn", B // 2, 2, rows=ROWS_DMAS * 16, heads=2 * 4 * 16)
    return Bag(norms=norms, bufs=bufs, prob=prob, prep=prep, sig=sig, moved=moved)


def L2_attn_sync(k, sp, s):
    with sp.Fori(0, s.sig.trips) as trip:
        for lane, buf in enumerate(s.bufs):
            sp.wait_ge(*s.sig.at("parts", lane, trip, 1))
            rows = s.moved.sems["rows"][lane]
            part = lambda a, which: buf.parts[0:NH1, a, which, :]
            for row in range(PAIRS):
                i, a = divmod(row, PARTS)
                sp.dma_start(buf.qrows[row:P:PAD, :, :], part(a, 0)).then_inc(rows, 16)
                sp.dma_start(buf.krows[row:P:PAD, :, :], part(i, 1)).then_inc(rows, 16)
            for a in range(PARTS):
                sp.dma_start(buf.qrows[PAIRS + a:P:PAD, :, :], part(a, 2)).then_inc(rows, 16)
        for lane, buf in enumerate(s.bufs):
            sp.wait_ge(*s.sig.at("raw", lane, trip, GROUPS // 2))
            for u in range(4):
                for i in (0, 1):
                    sp.dma_start(buf.oT[u:NH1:4, i, :], buf.raw[PAD * u + i:PAD * u + i + 1, :, :])\
                        .then_inc(s.moved.sems["heads"][lane], 16)


def group_tensor(k, pe, s, lane, trip, buf, g):
    mm, r = k.nc.tensor.matmul, g // 4
    base = 3 * (g % 2)
    if g >= 2:
        pe.wait_ge(*s.sig.at("prob", lane, trip, g - 1))
    elif lane == 1:
        pe.wait_ge(*s.sig.at("prob", 0, trip, GROUPS - 1 + g))
    for i, mask in ((0, "keyA"), (1, "keyA"), (2, "keyC")):
        mm(k.ps[:, base + i, :], k.identb[:, :], mask_of(k, mask), start=True, stop=False, skip_group_check=True)
    for u in range(4):
        hh = g % 4 * 4 + u
        q, kk = (ap[PAD * r:PAD * r + PAIRS + PARTS, hh, :] for ap in (buf.qrows, buf.krows))
        mm(k.ps[:, base + u // 2, u % 2 * SEQ:(u % 2 + 1) * SEQ], kk[:, 0:P], q, start=False, stop=True,
           skip_group_check=True)
        ins = mm(k.ps[:, base + 2, u * P:(u + 1) * P], kk[:, P:SEQ], q[:, P:SEQ], start=False, stop=True,
                 skip_group_check=True)
    ins.then_inc(*s.sig.up("s_ps", lane))


def group_out_tensor(k, pe, s, lane, trip, buf, g):
    mm, prob = k.nc.tensor.matmul, s.prob[:, g % 2]
    pe.wait_ge(*s.sig.at("prob", lane, trip, g + 1))
    if g % 2 == 0 and g >= 4:
        pe.wait_ge(*s.sig.at("raw", lane, trip, g // 2 - 1))
    elif g % 2 == 0 and lane == 1:
        pe.wait_ge(*s.sig.at("raw", 0, trip, GROUPS // 2 - 1 + g // 2))
    for u in range(4):
        h = 4 * g + u
        out = k.ps[PAD * u:PAD * u + 2, 6 + g // 2 % 2, g % 2 * SEQ:(g % 2 + 1) * SEQ]
        at = u % 2 * SEQ
        mm(out, buf.v1[:, 0, h, :], prob[:, u // 2, at:at + SEQ], start=True, stop=False, skip_group_check=True)
        ins = mm(out[:, P:SEQ], buf.v1[:, 1, h, :], prob[:, 2, u * P:(u + 1) * P], start=False, stop=True,
                 skip_group_check=True)
    ins.then_inc(*s.sig.up("pv_ps", lane))


def L2_attn_tensor(k, pe, s):
    sig, st = s.sig, "L2_attn"
    enter(k, pe, sig)
    wqkv = w_of(k, st, "wqkv", KC)
    with pe.Fori(0, sig.trips) as trip:
        for lane, buf in enumerate(s.bufs):
            if lane == 0:
                pe.wait_ge(*sig.at("done", 1, trip, 0))
            pe.wait_ge(*sig.at("z", lane, trip, 1))
            transpose_z_tensor(k, pe, sig, lane, trip, buf.z, k.ps[:, 3 * lane, :]).then_inc(*sig.up("zT_ps", lane))
        for lane, buf in enumerate(s.bufs):
            pe.wait_ge(*sig.at("zT", lane, trip, 1))
            for i in (0, 1):
                proj_feature(k, k.ps[0:NH1, 3 * lane, i * SEQ:(i + 1) * SEQ], wqkv, buf.zT, i * NH1, NH1)
            for t in (0, 1):
                ins = proj_token(k, k.ps[:, 3 * lane + 1, t * NH1:(t + 1) * NH1], buf.zT, t * P,
                                 wqkv[:, :, 2 * NH1:3 * NH1])
            ins.then_inc(*sig.up("qkv_ps", lane))
        for lane in (0, 1):
            pe.wait_ge(*sig.at("kv", lane, trip, 1))
        for lane, buf in enumerate(s.bufs):
            pe.wait_ge(*s.moved.at("rows", lane, trip, ROWS_DMAS * 16))
            group_tensor(k, pe, s, lane, trip, buf, 0)
            for g in range(GROUPS):
                if g + 1 < GROUPS:
                    group_tensor(k, pe, s, lane, trip, buf, g + 1)
                group_out_tensor(k, pe, s, lane, trip, buf, g)
        for lane, buf in enumerate(s.bufs):
            pe.wait_ge(*sig.at("oT", lane, trip, 1))
            if lane == 0:
                pe.wait_ge(*sig.at("prob", 1, trip, GROUPS))
            for t in (0, 1):
                ins = products(k, k.ps[:, lane, t * D:(t + 1) * D],
                               [(buf.oT[0:NH1, 0, t * P:(t + 1) * P], w_of(k, st, "wout")[0:NH1, :])])
            ins.then_inc(*sig.up("out_ps", lane))


def L2_attn_scalar(k, act, s):
    sig, a = s.sig, k.nc.scalar.activation
    enter(k, act, sig)
    with act.Fori(0, sig.trips) as trip:
        for lane, buf in enumerate(s.bufs):
            act.wait_ge(*sig.at("zT_ps", lane, trip, 1))
            a(buf.zT.rearrange("p c t -> p (c t)"), k.ps[:, 3 * lane, :], ACT.Copy).then_inc(*sig.up("zT", lane))
        for lane, buf in enumerate(s.bufs):
            for g in range(GROUPS):
                act.wait_ge(*sig.at("s_ps", lane, trip, g + 1))
                if g >= 2:
                    act.wait_ge(*sig.at("pv_ps", lane, trip, g - 1))
                elif lane == 1:
                    act.wait_ge(*sig.at("pv_ps", 0, trip, GROUPS - 1 + g))
                a(s.prob[:, g % 2], k.ps[:, 3 * (g % 2):3 * (g % 2) + 3, :], ACT.Exp, scale=NH1 ** -0.5)\
                    .then_inc(*sig.up("prob", lane))


def split_vector(k, link, x, rest, parts):
    v = k.nc.vector
    link(v.tensor_copy(parts[:, 0], x))
    link(v.tensor_tensor(rest, x, parts[:, 0], ALU.subtract))
    link(v.tensor_copy(parts[:, 1], rest))
    link(v.tensor_tensor(rest, rest, parts[:, 1], ALU.subtract))
    return v.tensor_copy(parts[:, 2], rest)


def L2_attn_vector(k, dve, s):
    v, sig = k.nc.vector, s.sig
    enter(k, dve, s.prep)
    norms_vector(k, dve, s.norms)
    for lane, buf in enumerate(s.bufs):
        v.memset(buf.v1, 1.0)
        v.memset(buf.krows, 1.0).then_inc(*s.prep.up("done", lane))
    enter(k, dve, sig)
    with dve.Fori(0, sig.trips) as trip:
        chains = [Chain(dve, sig, lane, trip) for lane in (0, 1)]
        for lane, buf in enumerate(s.bufs):
            ln_vector(k, dve, sig, lane, trip, buf)
        for lane in (0, 1):
            stats_vector(k, dve, sig, lane, trip)
        for lane, buf in enumerate(s.bufs):
            ch = chains[lane]
            dve.wait_ge(*sig.at("qkv_ps", lane, trip, 1))
            qkm, kmax, kmin = buf.qkm[0:NH1], buf.kmax[0:NH1], buf.kmin[0:NH1]
            ch.link(v.tensor_copy(qkm[:, 0:2, :], k.ps[0:NH1, 3 * lane, :].rearrange("p (c t) -> p c t", c=2)))
            v.tensor_copy(buf.v1[:, :, :, 0:1],
                          k.ps[:, 3 * lane + 1, 0:2 * NH1].rearrange("p (t h o) -> p t h o", t=2, o=1))\
                .then_inc(*sig.up("kv", lane))
            v.tensor_tensor_scan(kmax, qkm[:, 1, :], qkm[:, 1, :], -BIG, ALU.max, ALU.max)
            ch.link(v.tensor_tensor_scan(kmin, qkm[:, 1, :], qkm[:, 1, :], BIG, ALU.min, ALU.min))
            v.scalar_tensor_tensor(kmax, qkm[:, 0, :], -1.0, kmax, ALU.mult, ALU.mult)
            ch.link(v.scalar_tensor_tensor(kmin, qkm[:, 0, :], -1.0, kmin, ALU.mult, ALU.mult))
            ch.link(v.tensor_tensor(qkm[:, 2, :], kmax, kmin, ALU.min))
            split_vector(k, ch.link, qkm, buf.rest[0:NH1], buf.parts[0:NH1]).then_inc(*sig.up("parts", lane))
        for lane, buf in enumerate(s.bufs):
            for pair in range(GROUPS // 2):
                dve.wait_ge(*sig.at("pv_ps", lane, trip, 2 * pair + 2))
                if pair == 0:
                    dve.wait_ge(*s.moved.at("rows", lane, trip, ROWS_DMAS * 16))
                v.tensor_copy(buf.raw[:, 2 * pair:2 * pair + 2, :].rearrange("p g t -> p (g t)"),
                              k.ps[:, 6 + pair % 2, :]).then_inc(*sig.up("raw", lane))
        for lane, buf in enumerate(s.bufs):
            ch = chains[lane]
            out, sums, rec = (buf.oT[0:NH1, i, :] for i in range(3))
            dve.wait_ge(*s.moved.at("heads", lane, trip, 2 * 4 * 16))
            ch.link(v.reciprocal(rec, sums))
            v.tensor_tensor(out, out, rec, ALU.mult).then_inc(*sig.up("oT", lane))
        for lane, buf in enumerate(s.bufs):
            ch = chains[lane]
            x = x_of(k, trip, lane)
            dve.wait_ge(*sig.at("out_ps", lane, trip, 1))
            v.tensor_tensor(x, x, k.ps[:, lane, :].rearrange("p (t d) -> p t d", t=2), ALU.add)\
                .then_inc(*sig.up("done", lane))
            ch.close()


SC = SLOTS // P
SH_HALF = SLOTS // 2


def slots_plan(k):
    c, bufs = lane_buffers(k, 1)
    buf = bufs[0]
    buf.seT, buf.norm, buf.slots = c.take(KC, SLOTS), c.take(3 * SC), w_of(k, "L2_ffn", "slots", SC)
    buf.ex = c.take(SC, SEQ)
    buf.disp = c.take(2, SLOTS)
    buf.l = c.take(2 * SLOTS)
    buf.combT = c.take(SC, SEQ)
    buf.slotsT, buf.hT, buf.out = c.take(KC, SLOTS), c.take(E_SLOT_HID // P, SH_HALF), c.take(SC, D)
    buf.m, buf.rec = c.take(2 * SC + 4), c.take(2)
    buf.zn, buf.sq = c.take(2, D), c.take(2, D)
    norms = norms_plan(k, "L2_ffn")
    prep = Signals(k.signals, "L2_ffn", 1, 1, se=1, seT_ps=1, seT=1, done=1, dve_step=k.steps["slots_prep"])
    sig = Signals(k.signals, "L2_ffn", B, 1, z=1, zT_ps=1, zT=1, lT_ps=1, ex=1, l=1, l_ps=1, cmax=1, comb=1,
                  disp=1, dispT_ps=1, dispT_a=1, dispT_v=1, slots_ps=1, slots=1, combT_ps=1, combT_a=1, combT_v=1,
                  hid_ps=16, hid=16, proc_ps=2, proc=2, out_ps=1, done=1, dve_step=k.steps["L2_ffn"])
    return Bag(norms=norms, buf=buf, prep=prep, sig=sig)


def rms_vector(k, ch, src, dst, squares, st, n):
    v = k.nc.vector
    ch.link(v.tensor_tensor(squares, src, src, ALU.mult))
    ch.link(v.tensor_reduce(st[:, 0:n], squares, AX, ALU.add))
    rsqrt(k, ch.link, st[:, n:2 * n], st[:, 0:n], st[:, 2 * n:3 * n])
    ch.link(v.tensor_scalar(st[:, n:2 * n], st[:, n:2 * n], 1e12, None, ALU.min))
    for i in range(n):
        ins = v.tensor_scalar(dst[:, i, :], src[:, i, :], st[:, n + i:n + i + 1], float(D) ** 0.5, ALU.mult, ALU.mult)
    return ins



def hidden_tensor(k, pe, s, e, half, first, last):
    w1 = w_of(k, "L2_ffn", "w1", KC)
    for j in range(first, last):
        n = 8 * half + j
        if n >= 2:
            pe.wait_ge(*s.sig.at("hid", 0, e, n - 1))
        elif n == 0:
            pe.wait_ge(*s.sig.at("slots", 0, e, 1))
        proj_feature(k, k.ps[:, 4 + j % 2, :], w1, s.buf.slotsT[:, :, half * 512:(half + 1) * 512], j * P, P)\
            .then_inc(*s.sig.up("hid_ps"))


def processed_tensor(k, pe, s, e, half, first, last):
    w2 = w_of(k, "L2_ffn", "w2", E_SLOT_HID // P)
    if first == 0:
        pe.wait_ge(*s.sig.at("hid", 0, e, 8 * half + 8))
        if half:
            pe.wait_ge(*s.sig.at("proc", 0, e, 1))
        else:
            pe.wait_ge(*s.sig.at("done", 0, e, 0))
    for n in range(first, last):
        ins = products(k, k.ps[:, 6 + n // 2, n % 2 * D:(n % 2 + 1) * D],
                       [(s.buf.hT[:, j, n * P:(n + 1) * P], w2[:, j, :]) for j in range(E_SLOT_HID // P)])
    if last == 4:
        ins.then_inc(*s.sig.up("proc_ps"))


def combined_tensor(k, pe, s, e):
    for name, n in (("proc", 2), ("combT_a", 1), ("combT_v", 1)):
        pe.wait_ge(*s.sig.at(name, 0, e, n))
    for t in (0, 1):
        ins = products(k, k.ps[:, 6, t * D:(t + 1) * D],
                       [(s.buf.combT[:, n, t * P:(t + 1) * P], s.buf.out[:, n, :]) for n in range(SC)])
    ins.then_inc(*s.sig.up("out_ps"))


def slot_zT_tensor(k, pe, s, f, first):
    pe.wait_ge(*s.sig.at("z", 0, f, 1))
    if not first:
        pe.wait_ge(*s.sig.at("combT_a", 0, f, 0))
        pe.wait_ge(*s.sig.at("combT_v", 0, f, 0))
    transpose_z_tensor(k, pe, s.sig, 0, f, s.buf.zn, k.ps[:, 0, :]).then_inc(*s.sig.up("zT_ps"))


def logits_tensor(k, pe, s, f):
    pe.wait_ge(*s.sig.at("zT", 0, f, 1))
    for n in range(SC):
        ins = proj_feature(k, k.ps[:, n // 2, n % 2 * SEQ:(n % 2 + 1) * SEQ], s.buf.seT, s.buf.zT, n * P, P)
    ins.then_inc(*s.sig.up("lT_ps"))


def to_token_tensor(k, src, t):
    for n in range(SC):
        ins = k.nc.tensor.transpose(k.ps[:, 2 * t + n // 4, n % 4 * P:(n % 4 + 1) * P], src[:, n, t * P:(t + 1) * P],
                                    k.ident[:, :])
    return ins


def logits_turn_tensor(k, pe, s, f):
    pe.wait_ge(*s.sig.at("l", 0, f, 1))
    for t in (0, 1):
        ins = to_token_tensor(k, s.buf.l.rearrange("p (n t) -> p n t", n=SC), t)
    ins.then_inc(*s.sig.up("l_ps"))


def dispatch_turn_tensor(k, pe, s, f):
    pe.wait_ge(*s.sig.at("disp", 0, f, 1))
    pe.wait_ge(*s.sig.at("comb", 0, f, 1))
    for t in (0, 1):
        ins = to_token_tensor(k, s.buf.ex, t)
    ins.then_inc(*s.sig.up("dispT_ps"))


def slots_tensor(k, pe, s, f):
    pe.wait_ge(*s.sig.at("dispT_a", 0, f, 1))
    pe.wait_ge(*s.sig.at("dispT_v", 0, f, 1))
    for c in range(KC):
        for half in (0, 1):
            ins = products(k, k.ps[:, 2 * c + half, :],
                           [(s.buf.zn[:, t, c * P:(c + 1) * P], s.buf.disp[:, t, half * 512:(half + 1) * 512])
                            for t in (0, 1)])
    ins.then_inc(*s.sig.up("slots_ps"))


def combine_turn_tensor(k, pe, s, f):
    pe.wait_ge(*s.sig.at("slots", 0, f, 1))
    comb = s.buf.l.rearrange("p (t n) -> p t n", t=2)
    for n in range(SC):
        for t in (0, 1):
            ins = k.nc.tensor.transpose(k.ps[:, n // 2, (n % 2 * 2 + t) * P:(n % 2 * 2 + t + 1) * P],
                                        comb[:, t, n * P:(n + 1) * P], k.ident[:, :])
    ins.then_inc(*s.sig.up("combT_ps"))


def slots_step_tensor(k, pe, s, e, f, first=False):
    if e is not None:
        hidden_tensor(k, pe, s, e, 0, 0, 4)
    if f is not None:
        slot_zT_tensor(k, pe, s, f, first)
    if e is not None:
        hidden_tensor(k, pe, s, e, 0, 4, 8)
    if f is not None:
        logits_tensor(k, pe, s, f)
    if e is not None:
        processed_tensor(k, pe, s, e, 0, 0, 3)
    if f is not None:
        logits_turn_tensor(k, pe, s, f)
    if e is not None:
        processed_tensor(k, pe, s, e, 0, 3, 4)
        hidden_tensor(k, pe, s, e, 1, 0, 4)
    if f is not None:
        dispatch_turn_tensor(k, pe, s, f)
    if e is not None:
        hidden_tensor(k, pe, s, e, 1, 4, 8)
    if f is not None:
        slots_tensor(k, pe, s, f)
    if e is not None:
        processed_tensor(k, pe, s, e, 1, 0, 4)
    if f is not None:
        combine_turn_tensor(k, pe, s, f)
    if e is not None:
        combined_tensor(k, pe, s, e)


def L2_ffn_tensor(k, pe, s):
    buf, tr = s.buf, k.nc.tensor.transpose
    enter(k, pe, s.prep)
    pe.wait_ge(*s.prep.at("se", 0, 0, 1))
    for n in range(SC):
        for c in range(KC):
            ins = tr(k.ps[:, 2 * c + n // 4, n % 4 * P:(n % 4 + 1) * P], buf.slots[:, n, c * P:(c + 1) * P],
                     k.ident[:, :])
    ins.then_inc(*s.prep.up("seT_ps"))
    enter(k, pe, s.sig)
    slots_step_tensor(k, pe, s, None, 0, first=True)
    with pe.Fori(0, B - 1) as trip:
        slots_step_tensor(k, pe, s, trip, trip + 1)
    slots_step_tensor(k, pe, s, B - 1, None)


def gelu_scalar(k, act, s, e, half, first, last):
    for j in range(first, last):
        act.wait_ge(*s.sig.at("hid_ps", 0, e, 8 * half + j + 1))
        if half and j == 0:
            act.wait_ge(*s.sig.at("proc_ps", 0, e, 1))
        k.nc.scalar.activation(s.buf.hT[:, j, :], k.ps[:, 4 + j % 2, :], ACT.Gelu).then_inc(*s.sig.up("hid"))


def slots_step_scalar(k, act, s, e, f):
    sig, buf, a = s.sig, s.buf, k.nc.scalar.activation
    flat = lambda ap: ap.rearrange("p b f -> p (b f)")
    if e is not None:
        gelu_scalar(k, act, s, e, 0, 0, 4)
    if f is not None:
        act.wait_ge(*sig.at("zT_ps", 0, f, 1))
        for c in range(KC):
            ins = a(buf.zT[:, c, :], k.ps[:, 0, c * SEQ:(c + 1) * SEQ], ACT.Copy, scale=col_of(k, "L2_ffn_gx", c))
        ins.then_inc(*sig.up("zT"))
    if e is not None:
        gelu_scalar(k, act, s, e, 0, 4, 8)
    if f is not None:
        act.wait_ge(*sig.at("l", 0, f, 1))
        for n in range(SC):
            ins = a(buf.ex[:, n, :], buf.l[:, n * SEQ:(n + 1) * SEQ], ACT.Exp,
                    bias=buf.m[:, n:n + 1], accum_out=buf.m[:, SC + n:SC + n + 1])
        ins.then_inc(*sig.up("ex"))
        act.wait_ge(*sig.at("cmax", 0, f, 1))
        comb = buf.l.rearrange("p (t n) -> p t n", t=2)
        for t in (0, 1):
            ins = a(comb[:, t, :], flat(k.ps[:, 2 * t:2 * t + 2, :]), ACT.Exp,
                    bias=buf.m[:, 2 * SC + t:2 * SC + t + 1], accum_out=buf.m[:, 2 * SC + 2 + t:2 * SC + 3 + t])
        ins.then_inc(*sig.up("comb"))
    if e is not None:
        gelu_scalar(k, act, s, e, 1, 0, 4)
    if f is not None:
        act.wait_ge(*sig.at("dispT_ps", 0, f, 1))
        a(buf.disp[:, 0, :], flat(k.ps[:, 0:2, :]), ACT.Copy).then_inc(*sig.up("dispT_a"))
    if e is not None:
        gelu_scalar(k, act, s, e, 1, 4, 8)
    if f is not None:
        act.wait_ge(*sig.at("slots_ps", 0, f, 1))
        for c in range(KC):
            ins = a(buf.slotsT[:, c, :], flat(k.ps[:, 2 * c:2 * c + 2, :]), ACT.Copy, scale=col_of(k, "L2_ffn_gx", c))
        ins.then_inc(*sig.up("slots"))
        act.wait_ge(*sig.at("combT_ps", 0, f, 1))
        if e is not None:
            act.wait_ge(*sig.at("out_ps", 0, e, 1))
        a(flat(buf.combT[:, 0:SC // 2, :]), flat(k.ps[:, 0:2, :]), ACT.Copy).then_inc(*sig.up("combT_a"))


def L2_ffn_scalar(k, act, s):
    a = k.nc.scalar.activation
    enter(k, act, s.prep)
    act.wait_ge(*s.prep.at("seT_ps", 0, 0, 1))
    for c in range(KC):
        ins = a(s.buf.seT[:, c, :], k.ps[:, 2 * c:2 * c + 2, :].rearrange("p b f -> p (b f)"), ACT.Copy,
                scale=col_of(k, "L2_ffn_gs", c))
    ins.then_inc(*s.prep.up("seT"))
    enter(k, act, s.sig)
    slots_step_scalar(k, act, s, None, 0)
    with act.Fori(0, B - 1) as trip:
        slots_step_scalar(k, act, s, trip, trip + 1)
    slots_step_scalar(k, act, s, B - 1, None)


def processed_vector(k, dve, s, e, half):
    dve.wait_ge(*s.sig.at("proc_ps", 0, e, half + 1))
    k.nc.vector.tensor_copy(s.buf.out[:, 4 * half:4 * half + 4, :].rearrange("p n d -> p (n d)"),
                            k.ps[:, 6:8, :].rearrange("p b f -> p (b f)")).then_inc(*s.sig.up("proc"))


def slots_step_vector(k, dve, s, e, f, first=False):
    sig, buf, v = s.sig, s.buf, k.nc.vector
    flat = lambda ap: ap.rearrange("p b f -> p (b f)")
    if f is not None:
        ch = Chain(dve, sig, 0, f)
        if not first:
            dve.wait_ge(*sig.at("slots_ps", 0, f, 0))
        hold(k, dve, "vector")
        ch.link(ln_apply(k, f, 0, 1, buf.z))
        rms_vector(k, ch, buf.z, buf.zn, buf.sq, buf.norm, 2).then_inc(*sig.up("z"))
    if e is not None:
        stats_vector(k, dve, sig, 0, e, 1)
    if f is not None:
        dve.wait_ge(*sig.at("lT_ps", 0, f, 1))
        v.tensor_reduce(buf.m[:, 0:SC], k.ps[:, 0:4, :].rearrange("p b (c t) -> p (b c) t", c=2), AX, ALU.max,
                        negate=True)
        v.tensor_copy(buf.l, flat(k.ps[:, 0:4, :])).then_inc(*sig.up("l"))
        dve.wait_ge(*sig.at("ex", 0, f, 1))
        ch.link(v.reciprocal(buf.m[:, SC:2 * SC], buf.m[:, SC:2 * SC]))
        v.tensor_tensor(buf.ex, buf.ex, buf.m[:, SC:2 * SC].unsqueeze(2).broadcast_to([P, SC, SEQ]), ALU.mult)\
            .then_inc(*sig.up("disp"))
        dve.wait_ge(*sig.at("l_ps", 0, f, 1))
        v.tensor_reduce(buf.m[:, 2 * SC:2 * SC + 2], k.ps[:, 0:4, :].rearrange("p (t h) f -> p t (h f)", t=2), AX,
                        ALU.max, negate=True).then_inc(*sig.up("cmax"))
    if e is not None:
        processed_vector(k, dve, s, e, 0)
    if f is not None:
        dve.wait_ge(*sig.at("dispT_ps", 0, f, 1))
        v.tensor_copy(buf.disp[:, 1, :], flat(k.ps[:, 2:4, :])).then_inc(*sig.up("dispT_v"))
    if e is not None:
        processed_vector(k, dve, s, e, 1)
        dve.wait_ge(*sig.at("out_ps", 0, e, 1))
        hold(k, dve, "vector")
        x = x_of(k, e, 0, 1)
        for t in (0, 1):
            ins = v.scalar_tensor_tensor(x[:, t, :], k.ps[:, 6, t * D:(t + 1) * D], buf.rec[:, t:t + 1], x[:, t, :],
                                         ALU.mult, ALU.add)
        ins.then_inc(*sig.up("done"))
    if f is not None:
        dve.wait_ge(*sig.at("combT_ps", 0, f, 1))
        if e is not None:
            dve.wait_ge(*sig.at("done", 0, e, 1))
        v.tensor_copy(flat(buf.combT[:, SC // 2:SC, :]), flat(k.ps[:, 2:4, :])).then_inc(*sig.up("combT_v"))
        ch.link(v.reciprocal(buf.rec, buf.m[:, 2 * SC + 2:2 * SC + 4]))
        ch.close()


def L2_ffn_vector(k, dve, s):
    sig, buf, v = s.sig, s.buf, k.nc.vector
    ch = Chain(dve, s.prep, 0, 0)
    enter(k, dve, s.prep)
    norms_vector(k, dve, s.norms)
    rms_vector(k, ch, buf.slots, buf.slots, buf.out, buf.norm, SC).then_inc(*s.prep.up("se"))
    dve.wait_ge(*s.prep.at("seT", 0, 0, 1))
    v.memset(buf.m, 0.0).then_inc(*s.prep.up("done"))
    ch.close()
    enter(k, dve, sig)
    slots_step_vector(k, dve, s, None, 0, first=True)
    with dve.Fori(0, B - 1) as trip:
        slots_step_vector(k, dve, s, trip, trip + 1)
    slots_step_vector(k, dve, s, B - 1, None)


def scan_plan(k):
    c, bufs = lane_buffers(k)
    for buf in bufs:
        buf.zn = c.take(2, D)
        buf.a, buf.b, buf.c = c.take(KC, SEQ), c.take(KC, SEQ), c.take(KC, SEQ)
        buf.prod, buf.sum = c.take(KC, SEQ), c.take(KC, SEQ)
    ones = c.take(SEQ)
    norms = norms_plan(k, "L3_attn")
    prep = Signals(k.signals, "L3_attn", 1, 1, done=1)
    sig = Signals(k.signals, "L3_attn", B // 2, 2, z=1, zT_ps=1, zT=1, abc_ps=1, abc=1, o=1, out_ps=1, done=1,
                  dve_step=k.steps["L3_attn"])
    return Bag(norms=norms, bufs=bufs, ones=ones, prep=prep, sig=sig)


def L3_attn_tensor(k, pe, s):
    sig = s.sig
    enter(k, pe, sig)
    with pe.Fori(0, sig.trips) as trip:
        for lane, buf in enumerate(s.bufs):
            pe.wait_ge(*sig.at("z", lane, trip, 1))
            transpose_z_tensor(k, pe, sig, lane, trip, buf.zn, bank(k, lane, 3)).then_inc(*sig.up("zT_ps", lane))
        for lane, buf in enumerate(s.bufs):
            pe.wait_ge(*sig.at("zT", lane, trip, 1))
            for i, w in enumerate(("wa", "wb", "wc")):
                for c in range(KC):
                    ins = proj_feature(k, bank(k, lane, i)[:, c * SEQ:(c + 1) * SEQ], w_of(k, "L3_attn", w, KC),
                                       buf.zT, c * P, P)
            ins.then_inc(*sig.up("abc_ps", lane))
        for lane, buf in enumerate(s.bufs):
            pe.wait_ge(*sig.at("o", lane, trip, 1))
            for t in (0, 1):
                for c in range(KC):
                    ins = k.nc.tensor.transpose(bank(k, lane, 3)[:, (2 * t + c) * P:(2 * t + c + 1) * P],
                                                buf.b[:, c, t * P:(t + 1) * P], k.ident[:, :])
            ins.then_inc(*sig.up("out_ps", lane))


def L3_attn_scalar(k, act, s):
    sig, a = s.sig, k.nc.scalar.activation
    enter(k, act, sig)
    with act.Fori(0, sig.trips) as trip:
        for lane, buf in enumerate(s.bufs):
            act.wait_ge(*sig.at("zT_ps", lane, trip, 1))
            for c in range(KC):
                ins = a(buf.zT[:, c, :], bank(k, lane, 3)[:, c * SEQ:(c + 1) * SEQ], ACT.Identity,
                        bias=col_of(k, "L3_attn_be", c), scale=col_of(k, "L3_attn_g", c))
            ins.then_inc(*sig.up("zT", lane))
        for lane, buf in enumerate(s.bufs):
            act.wait_ge(*sig.at("abc_ps", lane, trip, 1))
            for i, (dst, fn, b) in enumerate(((buf.a, ACT.Sigmoid, "ba"), (buf.b, ACT.Identity, "bb"),
                                              (buf.c, ACT.Identity, "bc"))):
                for c in range(KC):
                    ins = a(dst[:, c, :], bank(k, lane, i)[:, c * SEQ:(c + 1) * SEQ], fn,
                            bias=col_of(k, "L3_attn_" + b, c))
            ins.then_inc(*sig.up("abc", lane))


def L3_attn_vector(k, dve, s):
    v, sig = k.nc.vector, s.sig
    enter(k, dve, s.prep)
    norms_vector(k, dve, s.norms)
    v.memset(s.ones, 1.0).then_inc(*s.prep.up("done"))
    enter(k, dve, sig)
    with dve.Fori(0, sig.trips) as trip:
        chains = [Chain(dve, sig, lane, trip) for lane in (0, 1)]
        for lane, buf in enumerate(s.bufs):
            ch = chains[lane]
            dve.wait_ge(*sig.at("done", lane, trip, 0))
            hold(k, dve, "vector")
            ch.link(ln_apply(k, trip, lane, 2, buf.z))
            layernorm(k, ch, buf.z, buf.zn, buf.st).then_inc(*sig.up("z", lane))
        for lane in (0, 1):
            stats_vector(k, dve, sig, lane, trip)
        for lane, buf in enumerate(s.bufs):
            ch = chains[lane]
            flat = lambda ap: ap.rearrange("p c t -> p (c t)")
            dve.wait_ge(*sig.at("abc", lane, trip, 1))
            for c in range(KC):
                ins = v.tensor_tensor_scan(buf.prod[:, c, :], buf.a[:, c, :], s.ones, 1.0, ALU.mult, ALU.mult)
            ch.link(ins)
            ch.link(v.tensor_scalar(flat(buf.a), flat(buf.prod), 1e-8, None, ALU.add))
            ch.link(v.reciprocal(flat(buf.a), flat(buf.a)))
            ch.link(v.tensor_tensor(flat(buf.a), flat(buf.b), flat(buf.a), ALU.mult))
            for c in range(KC):
                ins = v.tensor_tensor_scan(buf.sum[:, c, :], buf.a[:, c, :], s.ones, 0.0, ALU.add, ALU.mult)
            ch.link(ins)
            for c in range(KC):
                ins = v.scalar_tensor_tensor(buf.b[:, c, :], buf.sum[:, c, :], col_of(k, "L3_attn_h0", c),
                                             buf.prod[:, c, :], ALU.add, ALU.mult)
            ch.link(ins)
            v.tensor_tensor(flat(buf.b), flat(buf.b), flat(buf.c), ALU.mult).then_inc(*sig.up("o", lane))
        for lane, buf in enumerate(s.bufs):
            ch = chains[lane]
            x = x_of(k, trip, lane)
            dve.wait_ge(*sig.at("out_ps", lane, trip, 1))
            ch.link(v.tensor_tensor(buf.z, buf.z, bank(k, lane, 3).rearrange("p (t d) -> p t d", t=2), ALU.add))
            v.tensor_tensor(x, x, buf.z, ALU.add).then_inc(*sig.up("done", lane))
            ch.close()


FW = 2 * HD


def features_plan(k):
    a = attention("cross", width=FW, scale=1.0 / 16.0)
    c, bufs = lane_buffers(k)
    for buf in bufs:
        buf.ctxT = c.take(KC, CTX)
        attention_buffers(c, a, buf)
    norms = norms_plan(k, "L3_xattn")
    sig = Signals(k.signals, "L3_xattn", B // 2, 2, AHEAD, z=1, zT_ps=1, zT=1, ctx=1, qkv_ps=1, q=1, kv=1, oT_ps=1, oT=1,
                  out_ps=1, done=1, dve_step=k.steps["L3_xattn"], **attention_signals(a))
    return Bag(norms=norms, a=a, bufs=bufs, sig=sig)


def L3_xattn_tensor(k, pe, s):
    sig, st = s.sig, "L3_xattn"
    enter(k, pe, sig)
    wf, wv, bf = w_of(k, st, "wf", KC), w_of(k, st, "wv", KC), row_of(k, st, "bf")
    zT_tensor(k, pe, sig, 0, s.bufs)
    with pe.Fori(0, sig.trips) as trip:
        for lane, buf in enumerate(s.bufs):
            pe.wait_ge(*sig.at("zT", lane, trip, 1))
            pe.wait_ge(*sig.at("ctx", lane, trip, 1))
            pe.wait_ge(*sig.at("done", lane, trip, 0))
            for src, n, at in ((buf.zT, SEQ, 0), (buf.ctxT, CTX, 2)):
                for c in range(HC):
                    out = bank(k, lane, c // 2)[:, c % 2 * SEQ:(c % 2 + 1) * SEQ] if at == 0 else \
                        bank(k, lane, 2)[:, c * P:c * P + CTX]
                    for d in range(KC):
                        k.nc.tensor.matmul(out, wf[:, d, c * P:(c + 1) * P], src[:, d, :], start=d == 0, stop=False)
                    k.nc.tensor.matmul(out, bf[:, c * P:(c + 1) * P], k.ones[0:1, 0:n], start=False, stop=True)
            products(k, bank(k, lane, 3)[0:CTX, 0:D], [(buf.ctxT[:, c, :], wv[:, c, :]) for c in range(KC)],
                     row_of(k, st, "bv")).then_inc(*sig.up("qkv_ps", lane))
        for lane in (0, 1):
            pe.wait_ge(*sig.at("q", lane, trip, 1))
        attention_tensor(k, pe, sig, trip, s.a, s.bufs)
        for lane, buf in enumerate(s.bufs):
            oT_tensor(k, pe, sig, lane, trip, s.a, buf)
        zT_tensor(k, pe, sig, trip + 1, s.bufs)
        for lane, buf in enumerate(s.bufs):
            out_tensor(k, pe, sig, lane, trip, s.a, buf, w_of(k, st, "fc", 4), row_of(k, st, "fcb"), 4)


def L3_xattn_scalar(k, act, s):
    sig, a = s.sig, k.nc.scalar.activation
    enter(k, act, sig)
    zT_scalar(k, act, sig, 0, s.bufs)
    with act.Fori(0, sig.trips) as trip:
        for lane, buf in enumerate(s.bufs):
            act.wait_ge(*sig.at("qkv_ps", lane, trip, 1))
            a(buf.qT.rearrange("p c t -> p (c t)"), banks(k, lane, 0, 2).rearrange("p b f -> p (b f)"), ACT.Exp,
              scale=col_of(k, "sign"))
            for i in range(4):
                rows = slice(PAD * i, PAD * (i + 1))
                a(buf.kT[rows, :, i * CTX:(i + 1) * CTX], cut(bank(k, lane, 2)[rows], chunk=HC)[:, :, 0:CTX],
                  ACT.Exp, scale=col_of(k, "sign")[rows])
            v = buf.v[0:CTX, 0, :].rearrange("p (h e) -> p h e", h=H)
            v_ps = bank(k, lane, 3)[0:CTX, 0:D].rearrange("p (h e) -> p h e", h=H)
            a(v[:, :, 0:HD], v_ps, ACT.Exp)
            a(v[:, :, HD:2 * HD], v_ps, ACT.Exp, scale=-1.0).then_inc(*sig.up("q", lane))
        attention_scalar(k, act, sig, trip, s.a, s.bufs)
        for lane, buf in enumerate(s.bufs):
            oT_scalar(k, act, sig, lane, trip, s.a, buf)
        zT_scalar(k, act, sig, trip + 1, s.bufs)


def L3_xattn_vector(k, dve, s):
    sig = s.sig
    enter(k, dve, sig)
    norms_vector(k, dve, s.norms)
    keys_vector(k, s.bufs)
    first_z_vector(k, sig, s.bufs)
    with dve.Fori(0, sig.trips) as trip:
        chains = [Chain(dve, sig, lane, trip) for lane in (0, 1)]
        for lane in (0, 1):
            stats_vector(k, dve, sig, lane, trip)
        attention_vector(k, dve, sig, trip, chains, s.a, s.bufs)
        later_z_vector(k, dve, sig, s.bufs, trip)
        for lane, buf in enumerate(s.bufs):
            residual_vector(k, dve, sig, lane, trip)
            chains[lane].close()


CYCLES = 3
GN = 4


def coupling_plan(k):
    c, bufs = lane_buffers(k)
    for buf in bufs:
        buf.o = [buf.z, c.take(2, D)]
        buf.gT, buf.g1, buf.g2, buf.g2b, buf.gf = c.take(KC), c.take(1), c.take(1), c.take(P), c.take(1)
        buf.h1, buf.h2, buf.h3, buf.tf = c.take(KC, SEQ), c.take(SEQ), c.take(SEQ), c.take(2)
        buf.c0, buf.cp, buf.cn = c.take(2), c.take(2), c.take(2)
    w = Bag(half_b=c.take(2), ar=c.take(3), zeros=c.take(P))
    norms = norms_plan(k, "L3_ffn")
    prep = Signals(k.signals, "L3_ffn", 1, 1, done=1)
    sig = Signals(k.signals, "L3_ffn", B // 2, 2, z=1, g_ps=GN, gT=GN, oT_ps=CYCLES, oT=CYCLES,
                  hid_ps=3 * CYCLES, hid=3 * CYCLES, tf_ps=CYCLES, tf=CYCLES, turn=CYCLES, done=1, stored=16,
                  dve_step=k.steps["L3_ffn"])
    return Bag(norms=norms, bufs=bufs, w=w, prep=prep, sig=sig)


def L3_ffn_tensor(k, pe, s):
    sig, mm, st = s.sig, k.nc.tensor.matmul, "L3_ffn"
    enter(k, pe, sig)
    gc1, gc2, gc3 = w_of(k, st, "gc1", KC), w_of(k, st, "gc2"), w_of(k, st, "gc3")
    cn1, cn2, cn3, cn4 = w_of(k, st, "cn1", KC), w_of(k, st, "cn2", KC), w_of(k, st, "cn3"), w_of(k, st, "cn4")
    with pe.Fori(0, sig.trips) as trip:
        for lane, buf in enumerate(s.bufs):
            g = bank(k, lane, 3)
            pe.wait_ge(*sig.at("z", lane, trip, 1))
            for c in range(KC):
                ins = products(k, g[:, c:c + 1], [(buf.z[:, t, c * P:(c + 1) * P], col_of(k, "mean"))
                                                  for t in (0, 1)])
            ins.then_inc(*sig.up("g_ps", lane))
        for lane, buf in enumerate(s.bufs):
            pe.wait_ge(*sig.at("gT", lane, trip, 1))
            products(k, bank(k, lane, 3)[:, 4:5], [(gc1[:, c, :], buf.gT[:, c:c + 1]) for c in range(KC)])\
                .then_inc(*sig.up("g_ps", lane))
        for lane, buf in enumerate(s.bufs):
            pe.wait_ge(*sig.at("gT", lane, trip, 2))
            products(k, bank(k, lane, 3)[0:64, 8:9], [(gc2, buf.g1)]).then_inc(*sig.up("g_ps", lane))
        for lane, buf in enumerate(s.bufs):
            pe.wait_ge(*sig.at("gT", lane, trip, 3))
            products(k, bank(k, lane, 3)[:, 12:13], [(buf.g2b[0:64, :], gc3[0:64, :])])\
                .then_inc(*sig.up("g_ps", lane))
        for i in range(CYCLES):
            for lane, buf in enumerate(s.bufs):
                if i:
                    pe.wait_ge(*sig.at("turn", lane, trip, i))
                transpose_z_tensor(k, pe, sig, lane, trip, buf.o[i % 2], bank(k, lane, 0))\
                    .then_inc(*sig.up("oT_ps", lane))
            for lane, buf in enumerate(s.bufs):
                pe.wait_ge(*sig.at("oT", lane, trip, i + 1))
                for c in range(KC):
                    ins = proj_feature(k, bank(k, lane, 1)[:, c * SEQ:(c + 1) * SEQ], cn1, buf.zT, c * P, P)
                ins.then_inc(*sig.up("hid_ps", lane))
            for lane, buf in enumerate(s.bufs):
                pe.wait_ge(*sig.at("hid", lane, trip, 3 * i + 1))
                proj_feature(k, bank(k, lane, 2)[:, 0:SEQ], cn2, buf.h1, 0, P).then_inc(*sig.up("hid_ps", lane))
            for lane, buf in enumerate(s.bufs):
                pe.wait_ge(*sig.at("hid", lane, trip, 3 * i + 2))
                products(k, bank(k, lane, 0)[0:64, 0:SEQ], [(cn3, buf.h2)]).then_inc(*sig.up("hid_ps", lane))
            for lane, buf in enumerate(s.bufs):
                pe.wait_ge(*sig.at("hid", lane, trip, 3 * i + 3))
                if i == 0:
                    pe.wait_ge(*sig.at("gT", lane, trip, GN))
                for t in (0, 1):
                    ins = products(k, bank(k, lane, 3)[:, t:t + 1], [(buf.h3[0:64, t * P:(t + 1) * P], cn4[0:64, :])])
                ins.then_inc(*sig.up("tf_ps", lane))


def L3_ffn_scalar(k, act, s):
    sig, a = s.sig, k.nc.scalar.activation
    enter(k, act, sig)
    with act.Fori(0, sig.trips) as trip:
        for lane, buf in enumerate(s.bufs):
            act.wait_ge(*sig.at("g_ps", lane, trip, 1))
            a(buf.gT, bank(k, lane, 3)[:, 0:KC], ACT.Copy).then_inc(*sig.up("gT", lane))
        for lane, buf in enumerate(s.bufs):
            act.wait_ge(*sig.at("g_ps", lane, trip, 2))
            a(buf.g1, bank(k, lane, 3)[:, 4:5], ACT.Gelu, bias=col_of(k, "L3_ffn_gb1")).then_inc(*sig.up("gT", lane))
        for lane, buf in enumerate(s.bufs):
            act.wait_ge(*sig.at("g_ps", lane, trip, 3))
            a(buf.g2b[0:64, :], bank(k, lane, 3)[0:64, 8:9].broadcast_to([64, P]), ACT.Gelu,
              bias=col_of(k, "L3_ffn_gb2", 0, 64)).then_inc(*sig.up("gT", lane))
        for lane, buf in enumerate(s.bufs):
            act.wait_ge(*sig.at("g_ps", lane, trip, 4))
            a(buf.gf, bank(k, lane, 3)[:, 12:13], ACT.Tanh, bias=s.w.half_b[:, 1:2], scale=0.5)\
                .then_inc(*sig.up("gT", lane))
        for i in range(CYCLES):
            for lane, buf in enumerate(s.bufs):
                act.wait_ge(*sig.at("oT_ps", lane, trip, i + 1))
                a(buf.zT.rearrange("p c t -> p (c t)"), bank(k, lane, 0), ACT.Copy).then_inc(*sig.up("oT", lane))
            for lane, buf in enumerate(s.bufs):
                act.wait_ge(*sig.at("hid_ps", lane, trip, 3 * i + 1))
                for c in range(KC):
                    ins = a(buf.h1[:, c, :], bank(k, lane, 1)[:, c * SEQ:(c + 1) * SEQ], ACT.Gelu,
                            bias=col_of(k, "L3_ffn_cb1", c))
                ins.then_inc(*sig.up("hid", lane))
            for lane, buf in enumerate(s.bufs):
                act.wait_ge(*sig.at("hid_ps", lane, trip, 3 * i + 2))
                a(buf.h2, bank(k, lane, 2)[:, 0:SEQ], ACT.Gelu, bias=col_of(k, "L3_ffn_cb2"))\
                    .then_inc(*sig.up("hid", lane))
            for lane, buf in enumerate(s.bufs):
                act.wait_ge(*sig.at("hid_ps", lane, trip, 3 * i + 3))
                a(buf.h3[0:64, :], bank(k, lane, 0)[0:64, 0:SEQ], ACT.Gelu, bias=col_of(k, "L3_ffn_cb3", 0, 64))\
                    .then_inc(*sig.up("hid", lane))
            for lane, buf in enumerate(s.bufs):
                act.wait_ge(*sig.at("tf_ps", lane, trip, i + 1))
                a(buf.tf, bank(k, lane, 3)[:, 0:2], ACT.Tanh, bias=s.w.half_b[:, 0:1], scale=0.5)\
                    .then_inc(*sig.up("tf", lane))


def L3_ffn_vector(k, dve, s):
    v, sig, w = k.nc.vector, s.sig, s.w
    enter(k, dve, s.prep)
    norms_vector(k, dve, s.norms)
    b4, b3 = scalar_of(k, "cn_b4"), scalar_of(k, "gc_b3")
    v.tensor_scalar(w.half_b[:, 0:1], b4, 0.5, None, ALU.mult)
    v.tensor_scalar(w.half_b[:, 1:2], b3, 0.5, None, ALU.mult)
    v.tensor_scalar(w.ar[:, 0:1], scalar_of(k, "ar"), 0.7, None, ALU.mult)
    v.tensor_scalar(w.ar[:, 1:2], scalar_of(k, "ar"), 0.3, None, ALU.mult).then_inc(*s.prep.up("done"))
    enter(k, dve, sig)
    with dve.Fori(0, sig.trips) as trip:
        chains = [Chain(dve, sig, lane, trip) for lane in (0, 1)]
        for lane, buf in enumerate(s.bufs):
            ln_vector(k, dve, sig, lane, trip, buf)
        for lane, buf in enumerate(s.bufs):
            ch = chains[lane]
            dve.wait_ge(*sig.at("gT", lane, trip, GN))
            ch.link(v.tensor_scalar(buf.c0[:, 0:1], buf.gf, w.ar[:, 0:1], 0.1, ALU.mult, ALU.add))
        for i in range(CYCLES):
            for lane, buf in enumerate(s.bufs):
                ch = chains[lane]
                o, n = buf.o[i % 2], buf.o[(i + 1) % 2]
                dve.wait_ge(*sig.at("tf", lane, trip, i + 1))
                ch.link(v.tensor_scalar(buf.cp, buf.tf, w.ar[:, 1:2], buf.c0[:, 0:1], ALU.mult, ALU.add))
                ch.link(v.tensor_scalar(buf.cn, buf.cp, -1.0, None, ALU.mult))
                q = D // 4
                for t in (0, 1):
                    for j, (src, c) in enumerate(((2, buf.cp), (3, buf.cn), (0, buf.cn), (1, buf.cp))):
                        ins = v.scalar_tensor_tensor(n[:, t, j * q:(j + 1) * q], o[:, t, src * q:(src + 1) * q],
                                                     c[:, t:t + 1], o[:, t, j * q:(j + 1) * q], ALU.mult, ALU.add)
                ins.then_inc(*sig.up("turn", lane))
        for lane, buf in enumerate(s.bufs):
            x = x_of(k, trip, lane)
            dve.wait_ge(*sig.at("turn", lane, trip, CYCLES))
            v.tensor_tensor(x, x, buf.o[CYCLES % 2], ALU.add).then_inc(*sig.up("done", lane))
            chains[lane].close()


def store_sync(k, sp, s, out):
    with sp.Fori(0, s.sig.trips) as trip:
        for lane in (0, 1):
            sp.wait_ge(*s.sig.at("done", lane, trip, 1))
            sp.dma_start(out[bass.ts(trip * 2 + lane, 2), :, :].rearrange("t p d -> p t d"), x_of(k, trip, lane))\
                .then_inc(s.sig.sems["stored"][lane], 16)
    for lane in (0, 1):
        sp.wait_ge(*s.sig.at("stored", lane, s.sig.trips - 1, 16))


STEPS = dict(window_mem=2, window=4, grad_mem=4, grad=3, update=2, memory=2, L0_xattn=34, L0_ffn=20, L1_attn=42,
             L1_xattn=15, fp8_prep=26, L1_ffn=11, L2_attn=9, L2_xattn=6, slots_prep=13, L2_ffn=16, L3_attn=21, L3_xattn=6,
             L3_ffn=7)


def build(nc, a):
    ctx = ExitStack()
    with ctx:
        sb = lambda name, shape, dt=F32: ctx.enter_context(nc.sbuf_tensor(name, shape, dt))
        k = Bag(nc=nc, pack={}, rows={}, spread={}, slot={}, rowslot={}, loaded={}, steps=STEPS)
        sizes = {}
        for st in STAGES:
            k.pack[st], n = places(PACKS[st])
            _, m = places(ROWS[st])
            spread, d = places([(name, D) for name in SPREAD.get(st, [])])
            k.spread[st] = {name: (at + n + m, w) for name, (at, w) in spread.items()}
            sizes[st] = (n, m, d)
        in_slot = lambda st: sizes[st][0] + sizes[st][2] + (sizes[st][1] if st != STAGES[0] else 0)
        slot_size = [max(in_slot(st) for st in STAGES[i::2]) for i in (0, 1)]
        row_start = {st: sizes[st][0] for st in STAGES}
        row_start[STAGES[0]] = slot_size[1] - sizes[STAGES[0]][1]
        assert in_slot(STAGES[1]) <= row_start[STAGES[0]]
        for st in STAGES:
            k.rows[st] = {name: (at + row_start[st], w) for name, (at, w) in places(ROWS[st])[0].items()}
        slots = [sb(f"weights_{i}", [P, slot_size[i]]) for i in (0, 1)]
        for i, st in enumerate(STAGES):
            k.slot[st] = slots[i % 2]
            k.rowslot[st] = slots[i % 2 if i else 1]
        k.xs = sb("x", [P, SPARE + TILES + SPARE, D])
        k.norm, k.stats = sb("norm", [P, TILES + SPARE, 2]), sb("stats", [P, (SPARE + TILES) * 6])
        k.rstd = sb("rstd", [P, TILES + SPARE])[:, :]
        k.var, k.newton = (sb(n, [P, TILES])[:, :] for n in ("var", "newton"))
        k.ctxT = sb("ctxT", [P, KC, B * CTX])
        k.ident, k.identb = sb("ident", [P, P]), sb("identb", [P, P], BF16)
        k.maskpos, n = places(MASKS)
        k.masks = sb("masks", [P, n], BF16)
        k.colpos, n = places(COLS)
        k.cols = sb("cols", [P, n])
        k.scalars = sb("scalars", [P, len(SCALARS)])
        k.earlier = sb("earlier", [P, 64])
        k.ones = sb("ones", [1, SEQ])
        k.fp8_kernel_t, k.fp8_bias_t = sb("fp8_kernel", [P, KC * D], BF16), sb("fp8_bias", [P, D], BF16)
        k.fp8_kernel, k.fp8_bias = k.fp8_kernel_t[:, :], k.fp8_bias_t[:, :]
        k.earlier = k.earlier[:, :]
        k.arena_size = ARENA
        k.arena = sb("arena", [P, ARENA])
        k.ps = ctx.enter_context(nc.psum_tensor("ps", [P, 8, 512], F32))
        k.signals = SignalPool(nc, ctx)
        k.signals.lanes("done", 2)
        sem = lambda name: ctx.enter_context(nc.semaphore(name))
        k.held = {e: sem("held_" + e) for e in ("vector", "gpsimd", "tensor")}
        x_loaded, const_loaded, k.mem_loaded = sem("x_loaded"), sem("const_loaded"), sem("mem_loaded")
        slot_loaded = [sem(f"weights_{i}_loaded") for i in (0, 1)]
        total = [0, 0]
        loads = {}
        for i, st in enumerate(STAGES):
            n, m, d = sizes[st]
            loads[st] = (n > 0) + (m > 0) + len(SPREAD.get(st, []))
            total[i % 2] += 16 * loads[st]
            k.loaded[st] = (slot_loaded[i % 2], total[i % 2])

        s = {}
        s["L0_attn"] = memory_plan(k)
        s["L0_xattn"] = xattn_plan(k, "L0_xattn", True)
        s["L0_ffn"] = experts_plan(k)
        s["L1_attn"] = block_plan(k)
        s["L1_xattn"] = two_attentions_plan(k)
        s["L1_ffn"] = fp8_plan(k)
        s["L2_attn"] = width_one_plan(k)
        s["L2_xattn"] = xattn_plan(k, "L2_xattn", False)
        s["L2_ffn"] = slots_plan(k)
        s["L3_attn"] = scan_plan(k)
        s["L3_xattn"] = features_plan(k)
        s["L3_ffn"] = coupling_plan(k)
        last = {st: (s[st].memory if st == "L0_attn" else s[st].sig) for st in STAGES}
        constants = [(k.ctxT, "ctxT"), (k.ident, "ident"), (k.identb, "identb"), (k.masks, "masks"), (k.cols, "cols"),
                     (k.ones, "ones"), (k.fp8_kernel_t, "fp8_kernel")]
        n_const = 16 * (len(constants) + 3)
        buf0 = s["L0_attn"].buf
        block = ctx.enter_context(nc.Block())

        @block.sync
        def _(sp):
            def load(st):
                i = STAGES.index(st)
                if i >= 2:
                    sig = last[STAGES[i - 2]]
                    for lane in range(2):
                        sp.wait_ge(sig.sems["done"][lane], sig.ends[lane])
                n, m, _ = sizes[st]
                sem, _ = k.loaded[st]
                if n:
                    sp.dma_start(k.slot[st][:, 0:n], a["w_" + st][:, :]).then_inc(sem, 16)
                if m:
                    sp.dma_start(k.rowslot[st][0:1, row_start[st]:row_start[st] + m], a["r_" + st][:, :]).then_inc(sem, 16)
                for name in SPREAD.get(st, []):
                    sp.dma_start(spread_of(k, st, name), a["L1_attn_" + name].unsqueeze(0).broadcast_to([P, D]))\
                        .then_inc(sem, 16)

            sp.dma_start(k.xs[:, SPARE:SPARE + TILES, :], a["x"].rearrange("t p d -> p t d")).then_inc(x_loaded, 16)
            load("L0_attn")
            sp.dma_start(buf0.zT_all[:, :, B * SEQ:B * SEQ + MEM], a["memT"].rearrange("(c p) t -> p c t", p=P))\
                .then_inc(k.mem_loaded, 16)
            sp.dma_start(buf0.z_all[0:MEM, TILES * D:(TILES + 1) * D], a["mem"][:, :]).then_inc(k.mem_loaded, 16)
            for tile, name in constants:
                dst = tile[:, :, :] if name == "ctxT" else tile[:, :]
                src = a[name].rearrange("(c p) t -> p c t", p=P) if name == "ctxT" else a[name][:, :]
                sp.dma_start(dst, src).then_inc(const_loaded, 16)
            sp.dma_start(k.earlier, a["earlier"].broadcast_to([P, 64])).then_inc(const_loaded, 16)
            sp.dma_start(k.scalars[:, :], a["scalars"].broadcast_to([P, len(SCALARS)])).then_inc(const_loaded, 16)
            sp.dma_start(k.fp8_bias, a["fp8_bias"].unsqueeze(0).broadcast_to([P, D])).then_inc(const_loaded, 16)
            for i, st in enumerate(STAGES):
                if i + 1 < len(STAGES):
                    load(STAGES[i + 1])
                if st == "L2_attn":
                    L2_attn_sync(k, sp, s[st])
            store_sync(k, sp, s["L3_ffn"], a["out"])

        @block.gpsimd
        def _(pool):
            pool.wait_ge(const_loaded, n_const)
            L0_attn_gpsimd(k, pool, s["L0_attn"])
            xattn_gpsimd(k, pool, s["L0_xattn"])
            xattn_gpsimd(k, pool, s["L1_xattn"])
            xattn_gpsimd(k, pool, s["L2_xattn"])
            xattn_gpsimd(k, pool, s["L3_xattn"])

        @block.tensor
        def _(pe):
            pe.wait_ge(const_loaded, n_const)
            L0_attn_tensor(k, pe, s["L0_attn"])
            xattn_tensor(k, pe, s["L0_xattn"])
            L0_ffn_tensor(k, pe, s["L0_ffn"])
            L1_attn_tensor(k, pe, s["L1_attn"])
            L1_xattn_tensor(k, pe, s["L1_xattn"])
            L1_ffn_tensor(k, pe, s["L1_ffn"])
            L2_attn_tensor(k, pe, s["L2_attn"])
            xattn_tensor(k, pe, s["L2_xattn"])
            L2_ffn_tensor(k, pe, s["L2_ffn"])
            L3_attn_tensor(k, pe, s["L3_attn"])
            L3_xattn_tensor(k, pe, s["L3_xattn"])
            L3_ffn_tensor(k, pe, s["L3_ffn"])

        @block.scalar
        def _(act):
            act.wait_ge(const_loaded, n_const)
            L0_attn_scalar(k, act, s["L0_attn"])
            xattn_scalar(k, act, s["L0_xattn"])
            L0_ffn_scalar(k, act, s["L0_ffn"])
            L1_attn_scalar(k, act, s["L1_attn"])
            L1_xattn_scalar(k, act, s["L1_xattn"])
            L1_ffn_scalar(k, act, s["L1_ffn"])
            L2_attn_scalar(k, act, s["L2_attn"])
            xattn_scalar(k, act, s["L2_xattn"])
            L2_ffn_scalar(k, act, s["L2_ffn"])
            L3_attn_scalar(k, act, s["L3_attn"])
            L3_xattn_scalar(k, act, s["L3_xattn"])
            L3_ffn_scalar(k, act, s["L3_ffn"])

        @block.vector
        def _(dve):
            L0_attn_vector(k, dve, s["L0_attn"], x_loaded, const_loaded, n_const)
            xattn_vector(k, dve, s["L0_xattn"])
            L0_ffn_vector(k, dve, s["L0_ffn"])
            L1_attn_vector(k, dve, s["L1_attn"])
            L1_xattn_vector(k, dve, s["L1_xattn"])
            L1_ffn_vector(k, dve, s["L1_ffn"])
            L2_attn_vector(k, dve, s["L2_attn"])
            xattn_vector(k, dve, s["L2_xattn"])
            L2_ffn_vector(k, dve, s["L2_ffn"])
            L3_attn_vector(k, dve, s["L3_attn"])
            L3_xattn_vector(k, dve, s["L3_xattn"])
            L3_ffn_vector(k, dve, s["L3_ffn"])


ARENA = 27300


def layouts(i):
    import numpy as np

    i = {n: np.asarray(v) for n, v in i.items()}
    f32, bf16 = np.float32, i["L1_ffn_kernel"].dtype

    def chunks(w):
        n = w.shape[0] // P
        return w.reshape(n, P, -1).transpose(1, 0, 2).reshape(P, -1)

    def padded(w):
        out = np.zeros((w.shape[0], H, PAD), f32)
        out[:, :, 0:HD] = w.reshape(w.shape[0], H, HD)
        return out.reshape(w.shape[0], H * PAD)

    def widened(w, heads, e):
        out = np.zeros((w.shape[0], heads, e + 1), f32)
        out[:, :, 0:e] = w.reshape(w.shape[0], heads, e)
        return out.reshape(w.shape[0], heads * (e + 1))

    def with_ones(b, heads, e):
        out = np.ones((heads, e + 1), f32)
        out[:, 0:e] = b.reshape(heads, e)
        return out.reshape(-1)

    def low(w):
        out = np.zeros((P, w.shape[1]), f32)
        out[0:w.shape[0]] = w
        return out

    heads = lambda w: w.transpose(1, 0, 2).reshape(D, H * HD)
    g = lambda st, n: i[f"{st}_{n}"]
    a = {}

    def put(st, **w):
        parts = [w[n] for n, _ in PACKS[st]]
        for (n, c), p in zip(PACKS[st], parts):
            assert p.shape == (P, c), (st, n, p.shape, c)
        if parts:
            a["w_" + st] = np.ascontiguousarray(np.concatenate(parts, 1), f32)

    def put_rows(st, **r):
        parts = [r[n].reshape(-1) for n, _ in ROWS[st]]
        for (n, c), p in zip(ROWS[st], parts):
            assert p.shape == (c,), (st, n, p.shape, c)
        a["r_" + st] = np.ascontiguousarray(np.concatenate(parts)[None], f32)

    st = "L0_attn"
    put(st, wq=chunks(g(st, "wq").T), wk=chunks(g(st, "wk").T), wv=chunks(widened(g(st, "wv").T, SH, SD_)),
        wo=chunks(g(st, "wo").T), lin1=chunks(g(st, "lin1").T), lin2=chunks(g(st, "lin2").T),
        w1T=chunks(g(st, "w1").T), w2T=chunks(g(st, "w2").T), w2=chunks(g(st, "w2")))
    put_rows(st, v1=with_ones(np.zeros(D, f32), SH, SD_), b1=g(st, "b1"), b2=g(st, "b2"))
    for st in ("L0_xattn", "L2_xattn"):
        put(st, wq=chunks(padded(g(st, "Wq").T)), wk=chunks(padded(g(st, "Wk").T)),
            wv=chunks(widened(g(st, "Wv").T, H, HD)), wo=chunks(g(st, "Wo").T))
        put_rows(st, bv=with_ones(g(st, "bv"), H, HD), bo=g(st, "bo"))
    st = "L0_ffn"
    up = lambda n: np.concatenate([chunks(w) for w in list(g(st, "routed_" + n)) + list(g(st, "shared_" + n))], 1)
    put(st, router=chunks(g(st, "router_w")), w1=up("w1"), w3=up("w3"), w2=up("w2"))
    put_rows(st, rb=g(st, "router_b"))
    st = "L1_attn"
    put(st, wq=chunks(padded(heads(g(st, "q_proj")))), wk=chunks(padded(heads(g(st, "k_proj")))),
        wv=chunks(widened(heads(g(st, "v_proj")), H, HD)), ff1=chunks(g(st, "ff1_w")), ff2=chunks(g(st, "ff2_w")))
    put_rows(st, bv=with_ones(g(st, "v_bias"), H, HD), ff2b=g(st, "ff2_b"))
    for n in SPREAD[st]:
        a[f"{st}_{n}"] = g(st, n)
    st = "L1_xattn"
    w = {}
    for n in "12":
        w["wq" + n], w["wk" + n] = (chunks(padded(heads(g(st, W + n)))) for W in ("Wq", "Wk"))
        w["wv" + n], w["wo" + n] = chunks(widened(heads(g(st, "Wv" + n)), H, HD)), chunks(g(st, "Wo" + n))
    put(st, **w)
    put_rows(st, bv1=with_ones(g(st, "bv1"), H, HD), bv2=with_ones(g(st, "bv2"), H, HD), bo2=g(st, "bo2"))
    st = "L2_attn"
    put(st, wqkv=chunks(g(st, "w_qkv").T), wout=low(g(st, "w_out").T))
    st = "L2_ffn"
    put(st, slots=chunks(g(st, "slot_embeds").reshape(SLOTS, D)), w1=chunks(g(st, "w1")), w2=chunks(g(st, "w2")))
    st = "L3_attn"
    put(st, wa=chunks(g(st, "Wa").T), wb=chunks(g(st, "Wb").T), wc=chunks(g(st, "Wc").T))
    st = "L3_xattn"
    fm, fb = g(st, "fm_w"), g(st, "fm_b")
    wf, wv = np.zeros((H, HD, H, 2, HD), f32), np.zeros((H, HD, H, HD), f32)
    for h in range(H):
        wf[h, :, h, 0], wf[h, :, h, 1], wv[h, :, h] = fm.T, fm.T, fm.T
    put(st, wf=chunks(wf.reshape(D, H * PAD)), wv=chunks(wv.reshape(D, D)), fc=chunks(g(st, "fc_w").T))
    put_rows(st, bf=np.tile(fb, 2 * H), bv=np.tile(fb, H), fcb=g(st, "fc_b"))
    st = "L3_ffn"
    put(st, cn1=chunks(g(st, "cn_w1")), cn2=chunks(g(st, "cn_w2")), cn3=low(g(st, "cn_w3")), cn4=low(g(st, "cn_w4")),
        gc1=chunks(g(st, "gc_w1")), gc2=low(g(st, "gc_w2")), gc3=low(g(st, "gc_w3")))

    col = lambda b: b.reshape(-1, P).T
    pad_col = lambda b: col(padded(b.reshape(1, D)).reshape(-1))
    c = {"L0_attn_b1": col(i["L0_attn_b1"]), "L1_attn_bq": pad_col(i["L1_attn_q_bias"]),
         "L1_attn_bk": pad_col(i["L1_attn_k_bias"]), "L1_attn_ff1b": col(i["L1_attn_ff1_b"]),
         "L1_xattn_bo1": col(i["L1_xattn_bo1"]), "L2_ffn_gx": col(i["L2_ffn_gamma_x"]),
         "L2_ffn_gs": col(i["L2_ffn_gamma_slot"]), "L3_attn_g": col(i["L3_attn_gamma"]),
         "L3_attn_be": col(i["L3_attn_beta"]), "L3_attn_h0": col(i["L3_attn_h0"]),
         "sign": np.where(np.arange(P) % PAD < HD, 1.0, -1.0)[:, None], "mean": np.full((P, 1), 1.0 / SEQ),
         "one": np.ones((P, 1))}
    for n in ("L0_xattn_bq", "L0_xattn_bk", "L1_xattn_bq1", "L1_xattn_bk1", "L1_xattn_bq2", "L1_xattn_bk2",
              "L2_xattn_bq", "L2_xattn_bk"):
        c[n] = pad_col(i[n])
    for n in ("ba", "bb", "bc"):
        c["L3_attn_" + n] = col(i["L3_attn_" + n])
    for n, src in (("cb1", "cn_b1"), ("cb2", "cn_b2"), ("cb3", "cn_b3"), ("gb1", "gc_b1"), ("gb2", "gc_b2")):
        b = i["L3_ffn_" + src]
        c["L3_ffn_" + n] = low(b[:, None]) if b.shape[0] < P else col(b)
    a["cols"] = np.ascontiguousarray(np.concatenate([c[n] for n, _ in COLS], 1), f32)
    assert a["cols"].shape[1] == sum(n for _, n in COLS)
    sc = {"alpha": "L0_attn_alpha", "theta": "L0_attn_theta", "s_in": "L1_ffn_input_scale",
          "s_k": "L1_ffn_kernel_scale", "cn_b4": "L3_ffn_cn_b4", "gc_b3": "L3_ffn_gc_b3",
          "ar": "L3_ffn_adaptive_range"}
    a["scalars"] = np.ascontiguousarray(np.concatenate([i[sc[n]].reshape(1, 1) for n in SCALARS], 1), f32)
    a["fp8_kernel"] = np.ascontiguousarray(chunks(i["L1_ffn_kernel"]))
    a["fp8_bias"] = i["L1_ffn_bias"]
    a["x"] = i["x"].reshape(TILES, P, D)
    a["ctxT"] = np.ascontiguousarray(i["ctx_1024"].reshape(B * CTX, D).T)
    a["mem"], a["memT"] = i["L0_attn_mem"], np.ascontiguousarray(i["L0_attn_mem"].T)

    a["ident"] = np.eye(P, dtype=f32)
    a["identb"] = np.eye(P).astype(bf16)
    a["ones"] = np.ones((1, SEQ), f32)
    a["earlier"] = np.tril(np.ones((8, 8), f32), -1).reshape(1, 64)
    r, q = np.arange(P)[:, None], np.arange(P)[None, :]
    seen, all_, m = q <= r, np.ones((P, P), bool), np.arange(MEM)[None, :]
    ahead = {"selfA": [seen] * 4, "selfB": [all_, seen] * 2, "keyA": [seen.T, all_] * 2, "keyC": [seen.T] * 4,
             "swa0": [m > r - MEM, seen] * 2, "swa1": [q > r, seen] * 2, "swam": [m <= r] * 2}
    mask = np.concatenate([np.concatenate(ahead[n], 1) for n, _ in MASKS], 1)
    a["masks"] = np.where(mask, 0.0, -1e30).astype(bf16)
    return a


def kernel(**inputs):
    import concourse.bacc as bacc
    from concourse.bass_utils import run_bass_kernel_spmd

    nc = bacc.Bacc("TRN2", target_bir_lowering=False, num_devices=1)
    arrays, args = {}, {}
    for name, v in layouts(inputs).items():
        arrays["in_" + name] = v
        args[name] = nc.dram_tensor("in_" + name, v.shape, mybir.dt.from_np(v.dtype), kind="ExternalInput").ap()
    args["out"] = nc.dram_tensor("out", (TILES, P, D), F32, kind="ExternalOutput").ap()
    build(nc, args)
    result = run_bass_kernel_spmd(nc, [arrays], core_ids=[0])
    return result.results[0]["out"].reshape(B, SEQ, D)
```
